# Optimizing a Trainium2 kernel written in Bass

```python
import numpy as np
import jax
import jax.numpy as jnp

def _softmax(x, axis=-1):
    return jax.nn.softmax(x, axis=axis)

def _gelu(x):
    return jax.nn.gelu(x, approximate=True)

def _silu(x):
    return jax.nn.silu(x)

def _sigmoid(x):
    return jax.nn.sigmoid(x)

def _layernorm(x, axis=-1, eps=1e-05):
    m = jnp.mean(x, axis=axis, keepdims=True)
    v = jnp.var(x, axis=axis, keepdims=True)
    return (x - m) / jnp.sqrt(v + eps)

def _scatter_add(tgt, idx, src, axis=0):
    return tgt.at[idx].add(src)

def _segment_sum(src, seg, n):
    return jax.ops.segment_sum(src, seg, n)
kernel_name = 'mk_hybrid_d1_jaxref_r8_06bdb6'

def setup_inputs(seed: int=0):
    np.random.seed(seed)
    _w = jnp.asarray

    def _L0_attn_a_setup():
        import jax, jax.numpy as jnp
        import numpy as np
        D_K, HEADS, K_BITS, L_TABLES = (128, 16, 4, 8)
        HEAD_DIM = D_K // HEADS
        R = 1 << K_BITS
        S = L_TABLES * R
        B, T = (4, 512)

        def _protos_T():
            r = np.arange(R)
            bits = r[:, None] >> K_BITS - 1 - np.arange(K_BITS) & 1
            corners = (2.0 * bits - 1.0).astype(np.float32)
            return jnp.asarray(corners.T)
        key = jax.random.key(seed)
        ks = jax.random.split(key, 7)
        x = jax.random.normal(ks[0], (B, T, D_K), dtype=jnp.float32)
        sc = 0.02
        Wq = jax.random.normal(ks[1], (D_K, D_K), dtype=jnp.float32) * sc
        Wk = jax.random.normal(ks[2], (D_K, D_K), dtype=jnp.float32) * sc
        Wv = jax.random.normal(ks[3], (D_K, D_K), dtype=jnp.float32) * sc
        Wo = jax.random.normal(ks[4], (D_K, D_K), dtype=jnp.float32) * sc
        bo = jnp.zeros((D_K,), dtype=jnp.float32)
        planes = jax.random.normal(ks[5], (L_TABLES * K_BITS, HEAD_DIM), dtype=jnp.float32)
        planes_T = planes.T
        logit_temp = jnp.zeros((), dtype=jnp.float32)
        protos_T = _protos_T()
        return {'x': x, 'Wq': Wq, 'Wk': Wk, 'Wv': Wv, 'Wo': Wo, 'bo': bo, 'planes_T': planes_T, 'protos_T': protos_T, 'logit_temp': logit_temp}
    _L0_attn_a_in = _L0_attn_a_setup()

    def _L0_attn_b_setup():
        import jax, jax.numpy as jnp
        import numpy as np
        T, N, D, H = (128, 32, 128, 128)
        LR = 0.001

        def _recon(params, z):
            W1, b1, W2, b2 = params
            h = jax.nn.gelu(z @ W1.T + b1, approximate=False)
            return z + h @ W2.T + b2
        key = jax.random.key(seed)
        ks = jax.random.split(key, 6)
        sd = 1.0 / np.sqrt(D)
        sh = 1.0 / np.sqrt(H)
        s4 = 1.0 / np.sqrt(H // 4)
        return {'in_seq': jax.random.normal(ks[0], (T, N, D), jnp.float32), 't_k': jax.random.normal(ks[1], (H, D), jnp.float32) * sd, 't_v': jax.random.normal(ks[2], (H, D), jnp.float32) * sd, 't_q': jax.random.normal(ks[3], (H, D), jnp.float32) * sd, 'W1': jax.random.normal(ks[4], (H // 4, H), jnp.float32) * sh, 'b1': jnp.zeros((H // 4,), jnp.float32), 'W2': jax.random.normal(ks[5], (H, H // 4), jnp.float32) * s4, 'b2': jnp.zeros((H,), jnp.float32)}
    _L0_attn_b_in = _L0_attn_b_setup()

    def _L0_ffn_setup():
        import jax, jax.numpy as jnp
        import numpy as np
        from jax import lax
        B, S, H = (2, 128, 128)
        I = 64
        E = 32
        TOP_K = 4
        N_GROUP = 4
        TOPK_GROUP = 2
        SCALE = 2.5
        N_SHARED = 2
        SH_I = I * N_SHARED

        def _route(tokens, router_weight, router_bias):
            logits = tokens.astype(jnp.float32) @ router_weight.astype(jnp.float32).T
            scores = jax.nn.sigmoid(logits)
            sfc = scores + router_bias[None, :]
            T = tokens.shape[0]
            grp = sfc.reshape(T, N_GROUP, E // N_GROUP)
            group_scores = lax.top_k(grp, 2)[0].sum(-1)
            _, gidx = lax.top_k(group_scores, TOPK_GROUP)
            gmask = jax.nn.one_hot(gidx, N_GROUP, dtype=sfc.dtype).sum(1)
            smask = jnp.broadcast_to(gmask[:, :, None], (T, N_GROUP, E // N_GROUP)).reshape(T, E)
            tmp = jnp.where(smask > 0, sfc, 0.0)
            _, topk_idx = lax.top_k(tmp, TOP_K)
            topk_w = jnp.take_along_axis(scores, topk_idx, axis=1)
            topk_w = topk_w / (topk_w.sum(-1, keepdims=True) + 1e-20)
            topk_w = topk_w * SCALE
            return (topk_idx, topk_w)
        key = jax.random.key(seed)
        ks = jax.random.split(key, 10)
        std = 0.02
        return {'hidden_states': jax.random.normal(ks[0], (B, S, H), jnp.float32), 'router_weight': jax.random.normal(ks[1], (E, H), jnp.float32) * std, 'router_bias': jnp.zeros((E,), jnp.float32), 'gate_w': jax.random.normal(ks[2], (E, I, H), jnp.float32) * std, 'up_w': jax.random.normal(ks[3], (E, I, H), jnp.float32) * std, 'down_w': jax.random.normal(ks[4], (E, H, I), jnp.float32) * std, 'shared_gate_w': jax.random.normal(ks[5], (SH_I, H), jnp.float32) * std, 'shared_up_w': jax.random.normal(ks[6], (SH_I, H), jnp.float32) * std, 'shared_down_w': jax.random.normal(ks[7], (H, SH_I), jnp.float32) * std}
    _L0_ffn_in = _L0_ffn_setup()
    _d = {'L0_attn_a_x': _L0_attn_a_in['x'], 'L0_attn_a_Wq': _L0_attn_a_in['Wq'], 'L0_attn_a_Wk': _L0_attn_a_in['Wk'], 'L0_attn_a_Wv': _L0_attn_a_in['Wv'], 'L0_attn_a_Wo': _L0_attn_a_in['Wo'], 'L0_attn_a_bo': _L0_attn_a_in['bo'], 'L0_attn_a_planes_T': _L0_attn_a_in['planes_T'], 'L0_attn_a_protos_T': _L0_attn_a_in['protos_T'], 'L0_attn_a_logit_temp': _L0_attn_a_in['logit_temp'], 'L0_attn_b_t_k': _L0_attn_b_in['t_k'], 'L0_attn_b_t_v': _L0_attn_b_in['t_v'], 'L0_attn_b_t_q': _L0_attn_b_in['t_q'], 'L0_attn_b_W1': _L0_attn_b_in['W1'], 'L0_attn_b_b1': _L0_attn_b_in['b1'], 'L0_attn_b_W2': _L0_attn_b_in['W2'], 'L0_attn_b_b2': _L0_attn_b_in['b2'], 'L0_ffn_router_weight': _L0_ffn_in['router_weight'], 'L0_ffn_router_bias': _L0_ffn_in['router_bias'], 'L0_ffn_gate_w': _L0_ffn_in['gate_w'], 'L0_ffn_up_w': _L0_ffn_in['up_w'], 'L0_ffn_down_w': _L0_ffn_in['down_w'], 'L0_ffn_shared_gate_w': _L0_ffn_in['shared_gate_w'], 'L0_ffn_shared_up_w': _L0_ffn_in['shared_up_w'], 'L0_ffn_shared_down_w': _L0_ffn_in['shared_down_w']}
    _x0 = _d['L0_attn_a_x']
    _d['L0_attn_a_x'] = jax.random.normal(jax.random.fold_in(jax.random.key(seed), 1), (4, 1024, 128), dtype=_x0.dtype)
    del _x0
    return _d

def reference(L0_attn_a_x, L0_attn_a_Wq, L0_attn_a_Wk, L0_attn_a_Wv, L0_attn_a_Wo, L0_attn_a_bo, L0_attn_a_planes_T, L0_attn_a_protos_T, L0_attn_a_logit_temp, L0_attn_b_t_k, L0_attn_b_t_v, L0_attn_b_t_q, L0_attn_b_W1, L0_attn_b_b1, L0_attn_b_W2, L0_attn_b_b2, L0_ffn_router_weight, L0_ffn_router_bias, L0_ffn_gate_w, L0_ffn_up_w, L0_ffn_down_w, L0_ffn_shared_gate_w, L0_ffn_shared_up_w, L0_ffn_shared_down_w):

    def _L0_attn_a_ref(x, Wq, Wk, Wv, Wo, bo, planes_T, protos_T, logit_temp):
        import jax, jax.numpy as jnp
        import numpy as np
        D_K, HEADS, K_BITS, L_TABLES = (128, 16, 4, 8)
        HEAD_DIM = D_K // HEADS
        R = 1 << K_BITS
        S = L_TABLES * R
        B, T = (4, 512)

        def _protos_T():
            r = np.arange(R)
            bits = r[:, None] >> K_BITS - 1 - np.arange(K_BITS) & 1
            corners = (2.0 * bits - 1.0).astype(np.float32)
            return jnp.asarray(corners.T)
        Bx, Tx, D = x.shape
        dim = planes_T.shape[0]
        H = D // dim
        k_bits, r = protos_T.shape
        l_tables = planes_T.shape[1] // k_bits
        s = l_tables * r

        def heads(W):
            return (x @ W.T).reshape(Bx, Tx, H, dim).transpose(0, 2, 1, 3)
        Q, K, V = (heads(Wq), heads(Wk), heads(Wv))
        scale = jnp.clip(jnp.exp(logit_temp), 0.01, 20.0)
        projK = jnp.einsum('bhtd,dp->bhtp', K, planes_T).reshape(Bx, H, Tx, l_tables, k_bits)
        logitsK = jnp.einsum('bhtlk,kr->bhtlr', jnp.tanh(projK) / scale, protos_T)
        probsK = jax.nn.softmax(logitsK, axis=-1).reshape(Bx, H, Tx, s)
        bucket_K = jnp.einsum('bhts,bhtd->bhsd', probsK, K)
        bucket_V = jnp.einsum('bhts,bhtd->bhsd', probsK, V)
        scores = jnp.einsum('bhtd,bhsd->bhts', Q, bucket_K) / jnp.sqrt(jnp.float32(dim))
        attn = jax.nn.softmax(scores, axis=-1)
        out = jnp.einsum('bhts,bhsd->bhtd', attn, bucket_V)
        out = out.transpose(0, 2, 1, 3).reshape(Bx, Tx, D)
        return out @ Wo.T + bo

    def _L0_attn_b_ref(in_seq, t_k, t_v, t_q, W1, b1, W2, b2):
        import jax, jax.numpy as jnp
        import numpy as np
        T, N, D, H = (128, 32, 128, 128)
        LR = 0.001

        def _recon(params, z):
            W1, b1, W2, b2 = params
            h = jax.nn.gelu(z @ W1.T + b1, approximate=False)
            return z + h @ W2.T + b2

        def loss_fn(params, z, y):
            return jnp.mean((_recon(params, z) - y) ** 2)

        def step(params, x):
            z = x @ t_k.T
            y = x @ t_v.T
            grads = jax.grad(loss_fn)(params, z, y)
            new_params = jax.tree_util.tree_map(lambda p, g: jax.lax.stop_gradient(p - LR * g), params, grads)
            out = _recon(new_params, x @ t_q.T)
            return (new_params, out)
        _, outs = jax.lax.scan(step, (W1, b1, W2, b2), in_seq)
        return outs

    def _L0_ffn_ref(hidden_states, router_weight, router_bias, gate_w, up_w, down_w, shared_gate_w, shared_up_w, shared_down_w):
        import jax, jax.numpy as jnp
        import numpy as np
        from jax import lax
        B, S, H = (2, 128, 128)
        I = 64
        E = 32
        TOP_K = 4
        N_GROUP = 4
        TOPK_GROUP = 2
        SCALE = 2.5
        N_SHARED = 2
        SH_I = I * N_SHARED

        def _route(tokens, router_weight, router_bias):
            logits = tokens.astype(jnp.float32) @ router_weight.astype(jnp.float32).T
            scores = jax.nn.sigmoid(logits)
            sfc = scores + router_bias[None, :]
            T = tokens.shape[0]
            grp = sfc.reshape(T, N_GROUP, E // N_GROUP)
            group_scores = lax.top_k(grp, 2)[0].sum(-1)
            _, gidx = lax.top_k(group_scores, TOPK_GROUP)
            gmask = jax.nn.one_hot(gidx, N_GROUP, dtype=sfc.dtype).sum(1)
            smask = jnp.broadcast_to(gmask[:, :, None], (T, N_GROUP, E // N_GROUP)).reshape(T, E)
            tmp = jnp.where(smask > 0, sfc, 0.0)
            _, topk_idx = lax.top_k(tmp, TOP_K)
            topk_w = jnp.take_along_axis(scores, topk_idx, axis=1)
            topk_w = topk_w / (topk_w.sum(-1, keepdims=True) + 1e-20)
            topk_w = topk_w * SCALE
            return (topk_idx, topk_w)
        tokens = hidden_states.reshape(-1, H)
        topk_idx, topk_w = _route(tokens, router_weight, router_bias)
        gate_vals = jax.nn.silu(jnp.einsum('th,eih->tei', tokens, gate_w))
        up_vals = jnp.einsum('th,eih->tei', tokens, up_w)
        hidden_vals = gate_vals * up_vals
        expert_out = jnp.einsum('tei,ehi->teh', hidden_vals, down_w)
        sel = jnp.take_along_axis(expert_out, topk_idx[:, :, None], axis=1)
        mixed = (sel * topk_w[:, :, None].astype(sel.dtype)).sum(1)
        mixed = mixed.reshape(hidden_states.shape)
        sg = jax.nn.silu(jnp.einsum('bsh,ih->bsi', hidden_states, shared_gate_w))
        su = jnp.einsum('bsh,ih->bsi', hidden_states, shared_up_w)
        shared = jnp.einsum('bsi,hi->bsh', sg * su, shared_down_w)
        return mixed + shared
    x = L0_attn_a_x
    x = x + _L0_attn_a_ref(_layernorm(x, axis=-1), L0_attn_a_Wq, L0_attn_a_Wk, L0_attn_a_Wv, L0_attn_a_Wo, L0_attn_a_bo, L0_attn_a_planes_T, L0_attn_a_protos_T, L0_attn_a_logit_temp)
    x = x + _L0_ffn_ref(_layernorm(x, axis=-1), L0_ffn_router_weight, L0_ffn_router_bias, L0_ffn_gate_w, L0_ffn_up_w, L0_ffn_down_w, L0_ffn_shared_gate_w, L0_ffn_shared_up_w, L0_ffn_shared_down_w)
    x = x + _L0_attn_b_ref(_layernorm(x, axis=-1), L0_attn_b_t_k, L0_attn_b_t_v, L0_attn_b_t_q, L0_attn_b_W1, L0_attn_b_b1, L0_attn_b_W2, L0_attn_b_b2)
    x = x + _L0_ffn_ref(_layernorm(x, axis=-1), L0_ffn_router_weight, L0_ffn_router_bias, L0_ffn_gate_w, L0_ffn_up_w, L0_ffn_down_w, L0_ffn_shared_gate_w, L0_ffn_shared_up_w, L0_ffn_shared_down_w)
    return x

_drawn_inputs = setup_inputs


def setup_inputs(seed=0):
    import zlib

    import numpy as np

    out = dict(_drawn_inputs(seed))
    spreads = {'L0_attn_a_bo': (0.0, 0.1),
     'L0_attn_b_b1': (0.0, 0.1),
     'L0_attn_b_b2': (0.0, 0.1),
     'L0_ffn_router_bias': (0.0, 0.8)}
    factors = {'L0_attn_b_t_k': 25.0,
     'L0_attn_b_t_v': 64.0,
     'L0_ffn_router_weight': 8.0,
     'L0_ffn_gate_w': 8.0,
     'L0_ffn_up_w': 8.0,
     'L0_ffn_down_w': 8.0,
     'L0_ffn_shared_gate_w': 7.458,
     'L0_ffn_shared_up_w': 7.41,
     'L0_ffn_shared_down_w': 7.382}
    for name, (base, spread) in spreads.items():
        noise = np.random.default_rng([zlib.crc32(name.encode()), seed]).standard_normal(out[name].shape)
        drawn = base * np.exp(spread * noise) if base else spread * noise
        out[name] = jnp.asarray(drawn.astype(out[name].dtype))
    for name, factor in factors.items():
        out[name] = (out[name] * factor).astype(out[name].dtype)
    return out
```

```python
from contextlib import ExitStack

import numpy as np
import concourse.bass as bass
from concourse import mybir

F32 = mybir.dt.float32
F32R = mybir.dt.float32r
BF16 = mybir.dt.bfloat16
ALU = mybir.AluOpType
ACT = mybir.ActivationFunctionType
AX = mybir.AxisListType
ds = bass.ds

P = 128
NB = 4
NI = 8
GT = 4
GN = GT * P
NG = NB * NI // GT
HEADS, HD = 16, 8
TABLES, BITS, CORNERS = 8, 4, 16
NP = TABLES * BITS
S = TABLES * CORNERS
HC = 4
NC = HEADS // HC
EXPERTS, INNER, TOPK, NGROUP = 32, 64, 4, 4
GE = EXPERTS // NGROUP
UNITS = EXPERTS * INNER // P
ROUTE_SCALE = 2.5
LN_EPS = 1e-5
LR = 1e-3
RH = 32
LOWEST = -3.0e38


class Chain:

    def __init__(self, eng, sem, per_turn=0, turn=0):
        self.eng, self.sem, self.base, self.n, self.per_turn = eng, sem, turn * per_turn, 0, per_turn

    def step(self, ins):
        self.n += 1
        ins.then_inc(self.sem, 1)
        self.eng.wait_ge(self.sem, self.base + self.n)

    def close(self):
        assert self.n == self.per_turn, (self.n, self.per_turn)


def apart(eng, tick):
    eng.sem_inc(tick, 1)


def split_rows(v, c, hi, lo, src, tmp=None):
    c.step(v.tensor_copy(hi, src))
    c.step(v.tensor_tensor(lo, src, hi.bitcast(F32), ALU.subtract))


def three_pass(t, out, lhs, rhs, start=True, stop=True):
    t.matmul(out, lhs[0], rhs[0], start=start, stop=False, skip_group_check=True)
    t.matmul(out, lhs[1], rhs[0], start=False, stop=False, skip_group_check=True)
    return t.matmul(out, lhs[0], rhs[1], start=False, stop=stop, skip_group_check=True)


def build(nc, A, out, stages=4):
    top = ExitStack()
    with top:
        def mk(ctx):
            return (lambda n, s, d: ctx.enter_context(nc.sbuf_tensor(n, s, d)),
                    lambda n: ctx.enter_context(nc.semaphore(n)))
        sb, sem = mk(top)
        PS = top.enter_context(nc.psum_tensor("PS", [P, 8, 512], F32))
        x = sb("x", [P, NB * NI, P], F32)
        ident = sb("ident", [P, P], F32)
        W = {n: sb(n, [P, UNITS + 1, P], F32R) for n in ("gH", "gL", "uH", "uL", "dH", "dL")}
        rwH, rwL = sb("rwH", [P, EXPERTS], F32R), sb("rwL", [P, EXPERTS], F32R)
        rbias = sb("rbias", [P, EXPERTS], F32)
        sel = sb("sel", [96, UNITS, P], BF16)
        s_done = sem("s_done")

        prepare(nc, A, mk, x, ident, W, rwH, rwL, rbias, sel, PS)
        if stages >= 1:
            attention(nc, A, mk, x, ident, PS)
        if stages >= 2:
            ffn(nc, A, mk, "f1", x, ident, W, rwH, rwL, rbias, sel, PS)
        if stages >= 3:
            recon(nc, A, mk, x, ident, PS)
        if stages >= 4:
            ffn(nc, A, mk, "f2", x, ident, W, rwH, rwL, rbias, sel, PS)
        block = top.enter_context(nc.Block())

        @block.sync
        def _(sp):
            o = out.rearrange("b (p i) d -> p b i d", i=NI)
            for b in range(NB):
                sp.dma_start(o[:, b], x[:, b * NI:(b + 1) * NI, :]).then_inc(s_done, 16)
            sp.wait_ge(s_done, 16 * NB)


def prepare(nc, A, mk, x, ident, W, rwH, rwL, rbias, sel, PS):
    ctx = ExitStack()
    with ctx:
        sb, sem = mk(ctx)
        raw = {n: sb("raw_" + n, [P, UNITS + 1, P], F32) for n in "gud"}
        rw = sb("raw_rw", [P, EXPERTS], F32)
        selF = sb("selF", [96, UNITS, P], F32)
        s_x, s_w, s_c = sem("p_x"), sem("p_w"), sem("p_c")
        block = ctx.enter_context(nc.Block())

        @block.sync
        def _(sp):
            xi = A["x"].rearrange("b (p i) d -> p b i d", i=NI)
            for b in range(NB):
                sp.dma_start(x[:, b * NI:(b + 1) * NI, :], xi[:, b]).then_inc(s_x, 16)
            sp.dma_start(ident[:], A["ident"]).then_inc(s_x, 16)
            for n in "gud":
                sp.dma_start(raw[n][:], A["w_" + n]).then_inc(s_w, 16)
            sp.dma_start(rw[:], A["rwT"]).then_inc(s_w, 16)
            sp.dma_start(selF[:], A["sel"]).then_inc(s_w, 16)
            sp.dma_start(rbias[:], A["rbias"].partition_broadcast(P)).then_inc(s_w, 16)
            sp.wait_ge(s_x, 16 * (NB + 1))

        @block.vector
        def _(v):
            c = Chain(v, s_c)
            v.wait_ge(s_w, 96)
            for n in "gud":
                split_rows(v, c, W[n + "H"][:], W[n + "L"][:], raw[n][:])
            split_rows(v, c, rwH[:], rwL[:], rw[:])
            c.step(v.tensor_copy(sel[:], selF[:]))



def attention(nc, A, mk, x, ident, PS):
    ctx = ExitStack()
    with ctx:
        sb, sem = mk(ctx)
        wq = sb("a_wq", [P, NC, HC, 32], F32)
        wqH, wqL = sb("a_wqH", [P, NC, P], F32R), sb("a_wqL", [P, NC, P], F32R)
        wkv = sb("a_wkv", [P, 2, HEADS, HD], F32)
        wkvH, wkvL = sb("a_wkvH", [P, 2 * P], F32R), sb("a_wkvL", [P, 2 * P], F32R)
        wk = sb("a_wk", [P, P], F32)
        plane = sb("a_plane", [P, HEADS * NP], F32)
        m1H, m1L = sb("a_m1H", [P, 512], F32R), sb("a_m1L", [P, 512], F32R)
        proto = sb("a_proto", [P, HC * S], F32)
        prH, prL = sb("a_prH", [P, 512], F32R), sb("a_prL", [P, 512], F32R)
        wo = sb("a_wo", [P, NC, P], F32)
        bo = sb("a_bo", [1, P], F32)
        msk = sb("a_msk", [P, 2], F32)
        temp = sb("a_temp", [P, 4], F32)
        ones = sb("a_ones", [P, 32], F32)
        ones1 = sb("a_ones1", [1, P], F32)
        st = sb("a_st", [P, GT, 6], F32)
        mv = sb("a_mv", [P, GT, 2], F32)
        half_neg = sb("a_hn", [P, GT], F32)
        rstd = sb("a_rstd", [P, GT], F32)
        var_e = sb("a_vare", [P, GT], F32)
        xn = sb("a_xn", [P, GT, P], F32)
        xH, xL = sb("a_xH", [P, GN], F32R), sb("a_xL", [P, GN], F32R)
        af = sb("a_af", [P, 2, GN], F32)
        aH, aL = sb("a_aH", [P, NC, GN], F32R), sb("a_aL", [P, NC, GN], F32R)
        qH = sb("a_qH", [P, GN], F32R)
        kv = sb("a_kv", [P, 2, HEADS, 32], F32)
        qs = sb("a_qs", [P, NC, NI * P], F32R)
        dd = sb("a_dd", [P, 2, 1024], F32)
        ee = sb("a_ee", [P, 2, 1024], F32)
        pn = sb("a_pn", [P, 2, 1024], F32)
        mx = sb("a_mx", [P, 2, 64], F32)
        sm = sb("a_sm", [P, 2, 64], F32)
        ri = sb("a_ri", [P, 2, 64], F32)
        bT = sb("a_bT", [P, 512], F32)
        bH = sb("a_bH", [P, 512], F32R)
        kst = sb("a_kst", [P, NC, HC, S], F32R)
        bv = sb("a_bv", [P, HEADS, 32], F32)
        nm = sb("a_nm", [P, NI, HEADS], F32)
        nmH = sb("a_nmH", [P, NI, HEADS], F32R)
        nmp = sb("a_nmp", [P, NI, HEADS, 32], F32)
        e2 = ee
        rden = sb("a_rden", [P, GN], F32)
        oT = dd[:].rearrange("p h (c t) -> p (h c) t", c=2)

        s_w, s_wc, s_m1, s_rst = sem("a_w"), sem("a_wc"), sem("a_m1"), sem("a_rst")
        names = ("stat rstd xn xt xh xl ap af ah al kv kvc qp qh qs lg d e ri pn bk bt stk bvt bv sc mx nmp "
                 "nmt qf ss e2 pv o y x vc pc ac tick tickp").split()
        s = {n: sem("a_s_" + n) for n in names}

        block = ctx.enter_context(nc.Block())
        TPB, PJ, BK, MS = PS[:, 0, :], PS[:, 1, :], PS[:, 6, :], PS[:, 7, :]

        def LG(h):
            return PS[:, 2 + 2 * h:4 + 2 * h, :]

        NGB = NI // GT
        NH = 2 * NI

        @block.sync
        def _(sp):
            sp.wait_ge(s_m1, 1)
            wqv = A["wqT"].rearrange("f (c j d) -> f c j d", c=NC, j=HC)
            for r in range(3):
                for c in range(NC):
                    sp.dma_start(wq[:, c, :, 8 * r:8 * r + 8], wqv[:, c]).then_inc(s_w, 16)
            sp.dma_start(wkv[:, 0], A["wkT"].rearrange("f (h d) -> f h d", d=HD)).then_inc(s_w, 16)
            sp.dma_start(wkv[:, 1], A["wvT"].rearrange("f (h d) -> f h d", d=HD)).then_inc(s_w, 16)
            sp.dma_start(wk[:], A["wk"]).then_inc(s_w, 16)
            for h in range(HEADS):
                sp.dma_start(plane[HD * h:HD * h + HD, NP * h:NP * h + NP], A["planes"]).then_inc(s_w, 16)
            for n in range(HC * TABLES):
                sp.dma_start(proto[BITS * n:BITS * n + BITS, CORNERS * n:CORNERS * n + CORNERS],
                             A["protos"]).then_inc(s_w, 16)
            for j in range(HC):
                sp.dma_start(wo[32 * j:32 * j + HD, :, :],
                             A["woT"].rearrange("(c j d) o -> j d c o", c=NC, j=HC)[j]).then_inc(s_w, 16)
            sp.dma_start(bo[:], A["bo"].unsqueeze(0)).then_inc(s_w, 16)
            sp.dma_start(msk[:], A["msk"]).then_inc(s_w, 16)
            sp.dma_start(temp[:, 0:1], A["temp"].partition_broadcast(P)).then_inc(s_w, 16)
        WC = 1 + HC + 3 + 2 * 4
        NW = 12 + 3 + HEADS + HC * TABLES + HC + 3

        def batch_pool(g, b):
            c = Chain(g, s["pc"], 2, b)
            for k in range(NGB):
                g.wait_ge(s["stat"], b * NGB + (k + 1))
                apart(g, s["tickp"])
                c.step(g.tensor_scalar(var_e[:], mv[:, :, 1], LN_EPS, None, ALU.add))
                g.tensor_tensor(rstd[:], var_e[:], half_neg[:], ALU.pow).then_inc(s["rstd"], 1)
                for n in range(NC):
                    g.wait_ge(s["ah"], b * 8 + (4 * k + n + 1))
                    g.tensor_tensor(aL[:, n, :], af[:, n % 2, :], aH[:, n, :].bitcast(F32),
                                    ALU.subtract).then_inc(s["al"], 1)
                for i in range(GT):
                    for h in range(2):
                        n = 2 * (GT * k + i) + h
                        g.wait_ge(s["ri"], b * NH + (n + 1))
                        if n >= 2:
                            g.wait_ge(s["bk"], b * NH + (n - 1))
                        g.tensor_tensor(pn[:, h, :].rearrange("p (q r) -> p q r", r=CORNERS),
                                        ee[:, h, :].rearrange("p (q r) -> p q r", r=CORNERS),
                                        ri[:, h, :].unsqueeze(2).to_broadcast([P, 64, CORNERS]),
                                        ALU.mult).then_inc(s["pn"], 1)
            c.close()

        @block.gpsimd
        def _(g):
            g.memset(wq[:], 0.0)
            g.memset(plane[:], 0.0)
            g.memset(proto[:], 0.0)
            g.memset(wo[:], 0.0).then_inc(s_m1, 1)
            g.memset(half_neg[:], -0.5)
            g.memset(ones[:], 1.0)
            g.memset(bv[:], 0.0)
            g.memset(nmp[:], 0.0)
            g.memset(ones1[:], 1.0).then_inc(s_m1, 1)
            with g.Fori(0, NB) as b:
                batch_pool(g, b)

        def batch_scalar(a, b):
            for k in range(NGB):
                a.wait_ge(s["xt"], b * NGB + (k + 1))
                a.activation(xH[:], TPB, ACT.Copy).then_inc(s["xh"], 1)
                for n in range(NC):
                    m = 4 * k + n
                    a.wait_ge(s["ap"], b * 8 + (m + 1))
                    if m >= 2:
                        a.wait_ge(s["al"], b * 8 + (m - 1))
                    a.activation(af[:, n % 2, :], PJ, ACT.Tanh).then_inc(s["af"], 1)
                    a.wait_ge(s["af"], b * 8 + (m + 1))
                    a.activation(aH[:, n, :], af[:, n % 2, :], ACT.Copy).then_inc(s["ah"], 1)
                for n in range(NC):
                    a.wait_ge(s["qp"], b * 8 + (4 * k + n + 1))
                    if 4 * k + n >= 1:
                        a.wait_ge(s["qs"], b * 8 + (4 * k + n))
                    a.activation(qH[:], PJ, ACT.Copy).then_inc(s["qh"], 1)
                for i in range(GT):
                    T = GT * k + i
                    a.wait_ge(s["kv"], b * NI + (T + 1))
                    if T >= 2:
                        a.wait_ge(s["bk"], b * NH + 2 * (T - 1))
                    kvp = MS[:, 0:256].rearrange("p (w h d) -> p w h d", w=2, d=HD)
                    a.activation(kv[:, T % 2, :, 24:32], kvp[:, 1], ACT.Copy)
                    a.activation(kv[:, T % 2, :, 0:24].rearrange("p h (r d) -> p h r d", d=HD),
                                 kvp[:, 0].unsqueeze(2).to_broadcast([P, HEADS, 3, HD]),
                                 ACT.Copy).then_inc(s["kvc"], 1)
                    for h in range(2):
                        n = 2 * T + h
                        a.wait_ge(s["d"], b * NH + (n + 1))
                        if n >= 2:
                            a.wait_ge(s["pn"], b * NH + (n - 1))
                        a.activation(ee[:, h, :], dd[:, h, :], ACT.Exp).then_inc(s["e"], 1)
            a.wait_ge(s["bk"], b * NH + NH)
            a.activation(bT[:], BK, ACT.Copy).then_inc(s["bt"], 1)
            for k in range(NGB):
                for n in range(NC):
                    for h in range(2):
                        m = 2 * (NC * k + n) + h
                        a.wait_ge(s["ss"], b * NH + (m + 1))
                        if m >= 2:
                            a.wait_ge(s["pv"], b * NH + (m - 1))
                        a.activation(e2[:, h, :].rearrange("p (j t) -> p j t", j=2), LG(h), ACT.Exp,
                                     scale=float(HD) ** -0.5).then_inc(s["e2"], 1)

        @block.scalar
        def _(a):
            a.wait_ge(s_w, 16 * NW)
            a.activation(temp[:, 1:2], temp[:, 0:1], ACT.Exp).then_inc(s["ac"], 1)
            with a.Fori(0, NB) as b:
                batch_scalar(a, b)

        def batch_vector(v, b):
            c = Chain(v, s["vc"], NI + 2 * NH + 2 + 8, b)
            for k in range(NGB):
                for i in range(GT):
                    v.bn_stats(st[:, i, :], x[:, ds(b * NI + (GT * k + i), 1), :]
                               .rearrange("p o f -> p (o f)")).then_inc(s["vc"], 1)
                    c.n += 1
                v.wait_ge(s["vc"], c.base + c.n)
                apart(v, s["tick"])
                for i in range(GT):
                    last = v.bn_aggr(mv[:, i, :], st[:, i, :])
                last.then_inc(s["stat"], 1)
                v.wait_ge(s["rstd"], b * NGB + (k + 1))
                for i in range(GT):
                    last = v.tensor_scalar(xn[:, i, :], x[:, ds(b * NI + (GT * k + i), 1), :]
                                           .rearrange("p o f -> p (o f)"), mv[:, i, 0:1],
                                           rstd[:, i:i + 1], ALU.subtract, ALU.mult)
                last.then_inc(s["xn"], 1)
                v.wait_ge(s["xh"], b * NGB + (k + 1))
                v.tensor_tensor(xL[:], TPB, xH[:].bitcast(F32), ALU.subtract).then_inc(s["xl"], 1)
                for n in range(NC):
                    v.wait_ge(s["qh"], b * 8 + (4 * k + n + 1))
                    v.scalar_tensor_tensor(qs[:, n, GN * k:GN * k + GN], qH[:].bitcast(F32), msk[:, 0:1],
                                           PJ, ALU.mult, ALU.add).then_inc(s["qs"], 1)
                for i in range(GT):
                    T = GT * k + i
                    for h in range(2):
                        n = 2 * T + h
                        lg = LG(h).rearrange("p c (q r) -> p (c q) r", r=CORNERS)
                        v.wait_ge(s["lg"], b * NH + (n + 1))
                        c.step(v.tensor_reduce(mx[:, h, :], lg, AX.X, ALU.max))
                        if n >= 2:
                            v.wait_ge(s["e"], b * NH + (n - 1))
                        v.tensor_tensor(dd[:, h, :].rearrange("p (q r) -> p q r", r=CORNERS), lg,
                                        mx[:, h, :].unsqueeze(2).to_broadcast([P, 64, CORNERS]),
                                        ALU.subtract).then_inc(s["d"], 1)
                    for h in range(2):
                        n = 2 * T + h
                        v.wait_ge(s["e"], b * NH + (n + 1))
                        v.tensor_reduce(sm[:, h, :], ee[:, h, :].rearrange("p (q r) -> p q r", r=CORNERS),
                                        AX.X, ALU.add).then_inc(s["vc"], 1)
                        c.n += 1
                        v.wait_ge(s["vc"], c.base + c.n)
                        if n >= 2:
                            v.wait_ge(s["pn"], b * NH + (n - 1))
                        v.reciprocal(ri[:, h, :], sm[:, h, :]).then_inc(s["ri"], 1)
            v.wait_ge(s["bt"], b + 1)
            c.step(v.tensor_copy(bH[:], bT[:]))
            for j in range(HC):
                r = slice(32 * j, 32 * j + 24)
                last = v.scalar_tensor_tensor(kst[r, :, j, :],
                                              bH[r, :].bitcast(F32).rearrange("p (c s) -> p c s", c=NC),
                                              msk[r, 1:2], bT[r, :].rearrange("p (c s) -> p c s", c=NC),
                                              ALU.mult, ALU.add)
            last.then_inc(s["stk"], 1)
            v.wait_ge(s["bvt"], b + 1)
            v.tensor_copy(bv[:, :, 0:HD],
                          TPB.rearrange("p (h k) -> p h k", k=32)[:, :, 24:32]).then_inc(s["bv"], 1)
            for T in range(NI):
                for h in range(2):
                    n = 2 * T + h
                    v.wait_ge(s["sc"], b * NH + (n + 1))
                    v.tensor_reduce(nm[:, T, 8 * h:8 * h + 8],
                                    LG(h).rearrange("p c (j s) -> p (c j) s", s=S), AX.X, ALU.max,
                                    negate=True).then_inc(s["mx"], 1)
            v.wait_ge(s["mx"], b * NH + NH)
            c.step(v.tensor_copy(nmH[:], nm[:]))
            v.tensor_copy(nmp[:, :, :, 24], nmH[:].bitcast(F32))
            v.tensor_tensor(nmp[:, :, :, 25], nm[:], nmH[:].bitcast(F32), ALU.subtract).then_inc(s["nmp"], 1)
            for k in range(NGB):
                for n in range(NC):
                    q = qs[:, n, GN * k:GN * k + GN]
                    v.wait_ge(s["nmt"], b * 8 + (4 * k + n + 1))
                    v.tensor_tensor(q, q.bitcast(F32), TPB, ALU.add).then_inc(s["qf"], 1)
            for k in range(NGB):
                if k:
                    v.wait_ge(s["y"], b * NGB + k)
                for n in range(NC):
                    v.wait_ge(s["pv"], b * NH + 2 * (NC * k + n + 1))
                    c.step(v.reciprocal(rden[:], MS))
                    v.tensor_tensor(oT[:, n, :], PJ, rden[:], ALU.mult).then_inc(s["o"], 1)
                    v.wait_ge(s["o"], b * 8 + (4 * k + n + 1))
                v.wait_ge(s["y"], b * NGB + (k + 1))
                xg = x[:, ds(b * NI + GT * k, GT), :].rearrange("p i f -> p (i f)")
                v.tensor_tensor(xg, TPB, xg, ALU.add).then_inc(s["x"], 1)
            v.wait_ge(s["x"], b * NGB + NGB)
            c.close()

        @block.vector
        def _(v):
            c = Chain(v, s_wc)
            c.step(v.memset(kst[:].bitcast(F32), 0.0))
            for j in range(HC):
                c.step(v.memset(kst[32 * j:32 * j + 32, :, j, :].bitcast(F32), 1.0))
            v.wait_ge(s_w, 16 * NW)
            v.wait_ge(s["ac"], 1)
            c.step(v.tensor_scalar(temp[:, 2:3], temp[:, 1:2], 0.01, 20.0, ALU.max, ALU.min))
            c.step(v.reciprocal(temp[:, 3:4], temp[:, 2:3]))
            c.step(v.tensor_scalar(proto[:], proto[:], temp[:, 3:4], None, ALU.mult))
            split_rows(v, c, prH[:], prL[:], proto[:])
            split_rows(v, c, wqH[:], wqL[:], wq[:].rearrange("p c j k -> p c (j k)"))
            split_rows(v, c, wkvH[:], wkvL[:], wkv[:].rearrange("p w h d -> p (w h d)"))
            v.wait_ge(s_m1, 3)
            split_rows(v, c, m1H[:], m1L[:], TPB)
            with v.Fori(0, NB) as b:
                batch_vector(v, b)

        def batch_tensor(t, b):
            xs = (xH, xL)

            def buckets(T):
                for h in range(2):
                    t.wait_ge(s["pn"], b * NH + (2 * T + h + 1))
                    if h == 0:
                        t.wait_ge(s["kvc"], b * NI + (T + 1))
                    for n in (2 * h, 2 * h + 1):
                        for j in range(HC):
                            last = t.matmul(BK[32 * j:32 * j + 32, S * n:S * n + S],
                                            kv[:, T % 2, HC * n + j, :],
                                            pn[:, h, S * (HC * (n % 2) + j):S * (HC * (n % 2) + j) + S],
                                            start=(T == 0 and n == 0), stop=(T == NI - 1),
                                            skip_group_check=True)
                    last.then_inc(s["bk"], 1)

            for k in range(NGB):
                t.wait_ge(s["xn"], b * NGB + (k + 1))
                for i in range(GT):
                    last = t.transpose(TPB[:, P * i:P * i + P], xn[:, i, :], ident[:])
                last.then_inc(s["xt"], 1)
                t.wait_ge(s["xh"], b * NGB + (k + 1))
                t.wait_ge(s["xl"], b * NGB + (k + 1))
                for n in range(NC):
                    if n:
                        t.wait_ge(s["af"], b * 8 + (4 * k + n))
                    three_pass(t, PJ, (m1H[:, P * n:P * n + P], m1L[:, P * n:P * n + P]),
                               (xH[:], xL[:])).then_inc(s["ap"], 1)
                for n in range(NC):
                    if n:
                        t.wait_ge(s["qs"], b * 8 + (4 * k + n))
                    else:
                        t.wait_ge(s["af"], b * 8 + (4 * k + NC))
                    three_pass(t, PJ, (wqH[:, n, :], wqL[:, n, :]), (xH[:], xL[:])).then_inc(s["qp"], 1)
                t.wait_ge(s["ah"], b * 8 + (4 * k + NC))
                t.wait_ge(s["al"], b * 8 + (4 * k + NC))
                for i in range(GT):
                    T = GT * k + i
                    tok = slice(P * i, P * i + P)
                    if T:
                        t.wait_ge(s["kvc"], b * NI + T)
                    three_pass(t, MS[:, 0:256], (xH[:, tok], xL[:, tok]), (wkvH[:], wkvL[:])).then_inc(s["kv"], 1)
                    for h in range(2):
                        n = 2 * T + h
                        if n >= 2:
                            t.wait_ge(s["d"], b * NH + (n - 1))
                        for m in range(2):
                            last = three_pass(t, LG(h)[:, m, :], (aH[:, 2 * h + m, tok], aL[:, 2 * h + m, tok]),
                                              (prH[:], prL[:]))
                        last.then_inc(s["lg"], 1)
                    if T:
                        buckets(T - 1)
                if k == NGB - 1:
                    buckets(NI - 1)
            t.wait_ge(s["bt"], b + 1)
            for n in range(NC):
                last = t.transpose(TPB[:, P * n:P * n + P], bT[:, P * n:P * n + P], ident[:])
            last.then_inc(s["bvt"], 1)
            t.wait_ge(s["stk"], b + 1)
            t.wait_ge(s["qs"], b * 8 + 8)
            for T in range(NI):
                for h in range(2):
                    n = 2 * T + h
                    if n >= 2:
                        t.wait_ge(s["mx"], b * NH + (n - 1))
                    else:
                        t.wait_ge(s["d"], b * NH + NH)
                    for m in range(2):
                        last = t.matmul(LG(h)[:, m, :], qs[:, 2 * h + m, P * T:P * T + P],
                                        kst[:, 2 * h + m, :, :].rearrange("p j s -> p (j s)"),
                                        start=True, stop=True)
                    last.then_inc(s["sc"], 1)
            t.wait_ge(s["nmp"], b + 1)
            t.wait_ge(s["bv"], b + 1)
            for k in range(NGB):
                for n in range(NC):
                    if 4 * k + n:
                        t.wait_ge(s["qf"], b * 8 + (4 * k + n))
                    for i in range(GT):
                        last = t.transpose(TPB[:, P * i:P * i + P],
                                           nmp[:, GT * k + i, HC * n:HC * n + HC, :].rearrange("p j k -> p (j k)"),
                                           ident[:])
                    last.then_inc(s["nmt"], 1)
            t.wait_ge(s["qf"], b * 8 + 8)

            def values(m):
                k, n, h = m // 8, m // 2 % NC, m % 2
                t.wait_ge(s["e2"], b * NH + (m + 1))
                if h == 0 and m >= 2:
                    t.wait_ge(s["o"], b * 8 + m // 2)
                for g in range(2):
                    j = 2 * h + g
                    rows = slice(32 * j, 32 * j + 32)
                    t.matmul(PJ[rows, :], bv[:, HC * n + j, :], e2[:, h, GN * g:GN * g + GN],
                             start=True, stop=True)
                for g in range(2):
                    j = 2 * h + g
                    rows = slice(32 * j, 32 * j + 32)
                    last = t.matmul(MS[rows, :], ones[:], e2[:, h, GN * g:GN * g + GN],
                                    start=True, stop=True)
                last.then_inc(s["pv"], 1)

            def project(k):
                t.wait_ge(s["o"], b * 8 + 4 * k + 4)
                if k:
                    t.wait_ge(s["x"], b * NGB + k)
                for i in range(GT):
                    o = TPB[:, P * i:P * i + P]
                    for n in range(NC):
                        t.matmul(o, oT[:, n, P * i:P * i + P], wo[:, n, :], start=(n == 0), stop=False,
                                 skip_group_check=True)
                    last = t.matmul(o, ones1[:], bo[:], start=False, stop=True, skip_group_check=True)
                last.then_inc(s["y"], 1)

            for m in range(NH):
                k, n, h = m // 8, m // 2 % NC, m % 2
                if m >= 2:
                    t.wait_ge(s["e2"], b * NH + (m - 1))
                for g in range(2):
                    last = t.matmul(LG(h)[:, g, :], kst[:, n, 2 * h + g, :], qs[:, n, GN * k:GN * k + GN],
                                    start=True, stop=True)
                last.then_inc(s["ss"], 1)
                if m:
                    values(m - 1)
                if m == 8:
                    project(0)
            values(NH - 1)
            project(1)
            t.wait_ge(s["x"], b * NGB + NGB)

        @block.tensor
        def _(t):
            t.wait_ge(s_w, 16 * NW)
            t.wait_ge(s_m1, 2)
            t.matmul(TPB, wk[:], plane[:], start=True, stop=True).then_inc(s_m1, 1)
            t.wait_ge(s_wc, WC)
            with t.Fori(0, NB) as b:
                batch_tensor(t, b)



def ffn(nc, A, mk, tag, x, ident, W, rwH, rwL, rbias, sel, PS):
    ctx = ExitStack()
    with ctx:
        sb0, sem = mk(ctx)

        def sb(n, shape, d):
            return sb0(tag + n, shape, d)

        identb = sb("identb", [P, P], BF16)
        st, mv = sb("st", [P, GT, 6], F32), sb("mv", [P, GT, 2], F32)
        half_neg, rstd, var_e = (sb(n, [P, GT], F32) for n in ("hn", "rstd", "vare"))
        xn = sb("xn", [P, GT, P], F32)
        xH, xL = sb("xH", [P, 2, GN], F32R), sb("xL", [P, 2, GN], F32R)
        wT = sb("wT", [96, 2, GN], BF16)
        lg, near0, lgs, sil, rec, sc, wgt, w, r1, r2 = (
            sb(n, [P, GT, EXPERTS], F32) for n in "lg near0 lgs sil rec sc wgt w r1 r2".split())
        top8 = sb("top8", [P, GT, NGROUP, 8], F32)
        gsum = sb("gsum", [P, GT, 10], F32)
        g8, e8 = sb("g8", [P, GT, 8], F32), sb("e8", [P, GT, 8], F32)
        gsel = sb("gsel", [P, GT, 10], F32)
        gmask = sb("gmask", [P, GT, NGROUP], F32)
        sfc = sb("sfc", [P, GT, EXPERTS], F32)
        cand = sb("cand", [P, GT, EXPERTS + 4], F32)
        esel = sb("esel", [P, GT, EXPERTS + 4], F32)
        den, rden = sb("den", [P, GT], F32), sb("rden", [P, GT], F32)
        w3 = sb("w3", [P, GT, 96], BF16)
        sg, at, bt = (sb(n, [P, 2, GN], F32) for n in ("sg", "at", "bt"))
        bH, bL = sb("bH", [P, 2, GN], F32R), sb("bL", [P, 2, GN], F32R)
        yT = sb("yT", [P, GN], F32)
        names = ("stat rstd xn xt xh xl rt lgs sil w3 wt wtc G U WB sg a b bh bl dn yt yo vc init iv tick tickt tickp").split()
        s = {n: sem(tag + "_" + n) for n in names}
        NU = UNITS + 1
        TPB, RT, WB, Y = PS[:, 0, :], PS[:, 1, :], PS[:, 6, :], PS[:, 7, :]
        block = ctx.enter_context(nc.Block())

        def tokens(g):
            return x[:, ds(g * GT, GT), :]

        def run_groups(eng, main):
            with eng.Fori(0, NG // 2 - 1) as i:
                main(2 * i, True, 0)
                main(2 * i + 1, True, 1)
            main(NG - 2, True, 0)
            main(NG - 1, False, 1)

        @block.gpsimd
        def _(p):
            p.memset(half_neg[:], -0.5).then_inc(s["init"], 1)
            p.wait_ge(s["init"], 1)

            def prologue(g):
                p.wait_ge(s["stat"], g + 1)
                apart(p, s["tickp"])
                p.tensor_scalar(var_e[:], mv[:, :, 1], LN_EPS, None, ALU.add).then_inc(s["init"], 1)
                p.wait_ge(s["init"], g + 2)
                p.tensor_tensor(rstd[:], var_e[:], half_neg[:], ALU.pow).then_inc(s["rstd"], 1)

            def main(g, more, z):
                for u in range(NU):
                    k = g * NU + u
                    p.wait_ge(s["bh"], k + 1)
                    if u >= 2:
                        p.wait_ge(s["dn"], k - 1)
                    p.tensor_tensor(bL[:, u % 2, :], bt[:, u % 2, :], bH[:, u % 2, :].bitcast(F32),
                                    ALU.subtract).then_inc(s["bl"], 1)
                    if more and u == 1:
                        prologue(g + 1)

            prologue(0)
            run_groups(p, main)

        @block.scalar
        def _(a):
            def copy_x(g, z):
                a.wait_ge(s["xt"], g + 1)
                a.activation(xH[:, z, :], TPB, ACT.Copy).then_inc(s["xh"], 1)

            def silu_route(g):
                a.wait_ge(s["lgs"], g + 1)
                a.activation(sil[:], lgs[:], ACT.Silu).then_inc(s["sil"], 1)

            def copy_w(g, z):
                a.wait_ge(s["wt"], g + 1)
                a.activation(wT[:, z, :], RT[0:96, :].bitcast(BF16)[:, 0:GN], ACT.Copy).then_inc(s["wtc"], 1)

            def main(g, more, z):
                def high(u):
                    k = g * NU + u
                    a.wait_ge(s["b"], k + 1)
                    if u >= 2:
                        a.wait_ge(s["dn"], k - 1)
                    a.activation(bH[:, u % 2, :], bt[:, u % 2, :], ACT.Copy).then_inc(s["bh"], 1)

                for u in range(NU):
                    k = g * NU + u
                    a.wait_ge(s["G"], k + 1)
                    if u >= 2:
                        a.wait_ge(s["a"], k - 1)
                    a.activation(sg[:, u % 2, :], PS[:, 2 + u % 2, :], ACT.Silu).then_inc(s["sg"], 1)
                    if u:
                        high(u - 1)
                    if more and u == X_AT + 1:
                        copy_x(g + 1, 1 - z)
                    if more and u == ROUTE_AT + 1:
                        silu_route(g + 1)
                    if more and u == W_AT:
                        copy_w(g + 1, 1 - z)
                high(NU - 1)
                a.wait_ge(s["dn"], g * NU + NU)
                a.activation(yT[:], Y, ACT.Copy).then_inc(s["yt"], 1)

            copy_x(0, 0)
            silu_route(0)
            copy_w(0, 0)
            run_groups(a, main)

        @block.vector
        def _(v):
            c = Chain(v, s["iv"])
            c.step(v.tensor_copy(identb[:], ident[:]))
            c.step(v.memset(gsum[:], LOWEST))
            c.step(v.memset(cand[:], LOWEST))
            PER = 28

            def parts(g, z):
                c = Chain(v, s["vc"], PER, g)
                xg = tokens(g)

                def stats():
                    for i in range(GT):
                        last = v.bn_stats(st[:, i, :], x[:, ds(g * GT + i, 1), :].rearrange("p o f -> p (o f)"))
                    c.step(last)
                    apart(v, s["tick"])
                    for i in range(GT):
                        last = v.bn_aggr(mv[:, i, :], st[:, i, :])
                    last.then_inc(s["stat"], 1)

                def norm():
                    v.wait_ge(s["rstd"], g + 1)
                    for i in range(GT):
                        last = v.tensor_scalar(xn[:, i, :], x[:, ds(g * GT + i, 1), :].rearrange("p o f -> p (o f)"),
                                               mv[:, i, 0:1], rstd[:, i:i + 1], ALU.subtract, ALU.mult)
                    last.then_inc(s["xn"], 1)

                def low_x():
                    v.wait_ge(s["xh"], g + 1)
                    v.tensor_tensor(xL[:, z, :], TPB, xH[:, z, :].bitcast(F32), ALU.subtract).then_inc(s["xl"], 1)

                def logits():
                    v.wait_ge(s["rt"], g + 1)
                    c.step(v.tensor_copy(lg[:], RT[:, 0:GT * EXPERTS].rearrange("p (i e) -> p i e", i=GT)))
                    c.step(v.tensor_tensor(near0[:], lg[:], lg[:], ALU.mult))
                    c.step(v.tensor_scalar(near0[:], near0[:], 1e-24, 4e-12, ALU.is_lt, ALU.mult))
                    v.tensor_tensor(lgs[:], near0[:], lg[:], ALU.add).then_inc(s["lgs"], 1)
                    v.wait_ge(s["lgs"], g + 1)
                    c.step(v.reciprocal(rec[:], lgs[:]))

                def scores():
                    v.wait_ge(s["sil"], g + 1)
                    c.step(v.tensor_tensor(sc[:], sil[:], rec[:], ALU.mult))
                    c.step(v.tensor_tensor(sfc[:], sc[:], rbias[:].unsqueeze(1).to_broadcast([P, GT, EXPERTS]),
                                           ALU.add))
                    apart(v, s["tick"])
                    for i in range(GT):
                        for q in range(NGROUP):
                            last = v.max(top8[:, i, q, :], sfc[:, i, GE * q:GE * q + GE])
                    c.step(last)

                def groups():
                    c.step(v.tensor_tensor(gsum[:, :, 0:NGROUP], top8[:, :, :, 0], top8[:, :, :, 1], ALU.add))
                    apart(v, s["tick"])
                    for i in range(GT):
                        last = v.max(g8[:, i, :], gsum[:, i, :])
                    c.step(last)
                    c.step(v.memset(g8[:, :, 2:8], LOWEST))
                    apart(v, s["tick"])
                    for i in range(GT):
                        last = v.match_replace(gsel[:, i, :], g8[:, i, :], gsum[:, i, :], -LOWEST)
                    c.step(last)
                    c.step(v.tensor_scalar(gmask[:], gsel[:, :, 0:NGROUP], -LOWEST, None, ALU.is_equal))

                def experts():
                    cv = cand[:, :, 0:EXPERTS].rearrange("p i (q e) -> p i q e", q=NGROUP)
                    for i in range(GT):
                        last = v.tensor_tensor(cv[:, i], sfc[:, i, :].rearrange("p (q e) -> p q e", q=NGROUP),
                                               gmask[:, i, :].unsqueeze(2).to_broadcast([P, NGROUP, GE]), ALU.mult)
                    c.step(last)
                    c.step(v.tensor_scalar(cand[:, :, 0:EXPERTS], cand[:, :, 0:EXPERTS], 0.0, None, ALU.add))
                    apart(v, s["tick"])
                    for i in range(GT):
                        last = v.max(e8[:, i, :], cand[:, i, :])
                    c.step(last)
                    c.step(v.memset(e8[:, :, TOPK:8], LOWEST))
                    apart(v, s["tick"])
                    for i in range(GT):
                        last = v.match_replace(esel[:, i, :], e8[:, i, :], cand[:, i, :], -LOWEST)
                    c.step(last)

                def weights():
                    c.step(v.scalar_tensor_tensor(wgt[:], esel[:, :, 0:EXPERTS], -LOWEST, sc[:], ALU.is_equal,
                                                  ALU.mult))
                    c.step(v.tensor_reduce(den[:], wgt[:], AX.X, ALU.add))
                    c.step(v.tensor_scalar(den[:], den[:], 1e-20, None, ALU.add))
                    c.step(v.reciprocal(rden[:], den[:]))
                    c.step(v.tensor_tensor(w[:], wgt[:], rden[:].unsqueeze(2).to_broadcast([P, GT, EXPERTS]),
                                           ALU.mult))
                    c.step(v.tensor_scalar(w[:], w[:], ROUTE_SCALE, None, ALU.mult))

                def thirds():
                    c.step(v.tensor_copy(w3[:, :, 0:32], w[:]))
                    c.step(v.tensor_tensor(r1[:], w[:], w3[:, :, 0:32], ALU.subtract))
                    c.step(v.tensor_copy(w3[:, :, 32:64], r1[:]))
                    c.step(v.tensor_tensor(r2[:], r1[:], w3[:, :, 32:64], ALU.subtract))
                    v.tensor_copy(w3[:, :, 64:96], r2[:]).then_inc(s["w3"], 1)
                    assert c.n == PER, c.n

                return [stats, norm, low_x, logits, scores, groups, experts, weights, thirds]

            def main(g, more, z):
                after = {}
                if more:
                    for u, part in zip((0, 1, X_AT + 1, ROUTE_AT + 1, ROUTE_AT + 2, ROUTE_AT + 3, ROUTE_AT + 4,
                                        ROUTE_AT + 5, ROUTE_AT + 6), parts(g + 1, 1 - z)):
                        after[u] = part
                for u in range(NU):
                    k = g * NU + u
                    v.wait_ge(s["U"], k + 1)
                    v.wait_ge(s["sg"], k + 1)
                    if u >= 2:
                        v.wait_ge(s["bl"], k - 1)
                    shared = u == UNITS
                    v.tensor_tensor((bt if shared else at)[:, u % 2, :], sg[:, u % 2, :], PS[:, 4 + u % 2, :],
                                    ALU.mult).then_inc(s["a"], 1)
                    v.wait_ge(s["a"], k + 1)
                    if shared:
                        v.sem_inc(s["b"], 1)
                    else:
                        v.wait_ge(s["WB"], g * UNITS + (u + 1))
                        v.tensor_tensor(bt[:, u % 2, :], at[:, u % 2, :], WB, ALU.mult).then_inc(s["b"], 1)
                    if u in after:
                        after[u]()
                v.wait_ge(s["yo"], g + 1)
                xg = tokens(g).rearrange("p i f -> p (i f)")
                v.tensor_tensor(xg, TPB, xg, ALU.add).then_inc(s["iv"], 1)
                v.wait_ge(s["iv"], g + 4)

            for part in parts(0, 0):
                part()
            run_groups(v, main)

        @block.tensor
        def _(t):
            def transpose_x(g):
                t.wait_ge(s["xn"], g + 1)
                for i in range(GT):
                    last = t.transpose(TPB[:, P * i:P * i + P], xn[:, i, :], ident[:])
                last.then_inc(s["xt"], 1)

            def route(g, z):
                t.wait_ge(s["xl"], g + 1)
                for i in range(GT):
                    tok = slice(P * i, P * i + P)
                    last = three_pass(t, RT[:, EXPERTS * i:EXPERTS * i + EXPERTS], (xH[:, z, tok], xL[:, z, tok]),
                                      (rwH[:], rwL[:]))
                last.then_inc(s["rt"], 1)

            def transpose_w(g):
                t.wait_ge(s["w3"], g + 1)
                apart(t, s["tickt"])
                for i in range(GT):
                    last = t.transpose(RT[0:96, :].bitcast(BF16)[:, P * i:P * i + P], w3[:, i, :], identb[:])
                last.then_inc(s["wt"], 1)

            def main(g, more, z):
                xs = (xH[:, z, :], xL[:, z, :])

                def down(u):
                    k = g * NU + u
                    t.wait_ge(s["bl"], k + 1)
                    last = three_pass(t, Y, (W["dH"][:, u, :], W["dL"][:, u, :]), (bH[:, u % 2, :], bL[:, u % 2, :]),
                                      start=(u == 0), stop=(u == UNITS))
                    last.then_inc(s["dn"], 1)

                for u in range(NU):
                    k = g * NU + u
                    if u >= 2:
                        t.wait_ge(s["sg"], k - 1)
                    three_pass(t, PS[:, 2 + u % 2, :], (W["gH"][:, u, :], W["gL"][:, u, :]), xs).then_inc(s["G"], 1)
                    if u >= 2:
                        t.wait_ge(s["a"], k - 1)
                    three_pass(t, PS[:, 4 + u % 2, :], (W["uH"][:, u, :], W["uL"][:, u, :]), xs).then_inc(s["U"], 1)
                    if u < UNITS:
                        if u:
                            t.wait_ge(s["b"], k)
                        t.matmul(WB, sel[:, u, :], wT[:, z, :], start=True, stop=True).then_inc(s["WB"], 1)
                    if u >= 2:
                        down(u - 2)
                    if more and u == X_AT:
                        transpose_x(g + 1)
                    if more and u == ROUTE_AT:
                        route(g + 1, 1 - z)
                    if more and u == W_AT:
                        transpose_w(g + 1)
                down(NU - 2)
                down(NU - 1)
                t.wait_ge(s["yt"], g + 1)
                for i in range(GT):
                    last = t.transpose(TPB[:, P * i:P * i + P], yT[:, P * i:P * i + P], ident[:])
                last.then_inc(s["yo"], 1)

            transpose_x(0)
            route(0, 0)
            t.wait_ge(s["iv"], 3)
            transpose_w(0)
            t.wait_ge(s["wtc"], 1)
            run_groups(t, main)


X_AT, ROUTE_AT, W_AT = 3, 5, 14



def recon(nc, A, mk, x, ident, PS):
    ctx = ExitStack()
    with ctx:
        sb0, sem = mk(ctx)

        def sb(n, shape, d=F32):
            return sb0("r_" + n, shape, d)

        tk, tv, tq, tkT, tvT, tqT, dn, dT = (sb(n, [P, P]) for n in "tk tv tq tkT tvT tqT dn dT".split())
        w1T = sb("w1T", [P, RH])
        w2e = sb("w2e", [P, RH + 1])
        w2eT = sb("w2eT", [RH + 1, P])
        b1 = sb("b1", [RH, 1])
        st, mv = sb("st", [P, NI, 6]), sb("mv", [P, NI, 2])
        half_neg, rstd, var_e = (sb(n, [P, NI]) for n in ("hn", "rstd", "vare"))
        xn = sb("xn", [P, NI, P])
        xT = sb("xT", [P, NI * P])
        par = sb("par", [P, 2 * RH])
        hh = sb("hh", [RH + 1, RH])
        qpar = sb("qpar", [P, RH])
        N2 = NI * P
        v0, v1, vs, rv, cdf, ex, gp = (sb(n, [RH, N2]) for n in "v0 v1 vs rv cdf ex gp".split())
        hd = sb("hd", [96, N2])
        h2 = sb("h2", [RH + 1, N2])
        hdt = sb("hdt", [P, NI, 96])
        M = sb("M", [P, 96])
        gram = sb("gram", [RH + 1, RH + 1])
        names = "w wc stat rstd xn xt xT par parc pre vs ge v1 ex dh dp hdt hdc m mc upd updc w2t w2c q qc pq h2 o x vc ac mem g1 tick tickt tickp".split()
        s = {n: sem("r_" + n) for n in names}
        TPB, PRE, DH, HDT, MM, SM, OUT = (PS[:, n, :] for n in (0, 1, 2, 3, 4, 5, 7))
        C = 2.0 / (NI * P * P)
        SQ = 0.3989422804014327
        block = ctx.enter_context(nc.Block())
        NGB = NI // GT

        @block.sync
        def _(sp):
            for dst, n in ((tk, "tk"), (tv, "tv"), (tq, "tq"), (tkT, "tkT"), (tvT, "tvT"), (tqT, "tqT"), (w1T, "w1T")):
                sp.dma_start(dst[:], A[n]).then_inc(s["w"], 16)
            sp.dma_start(w2e[:, 0:RH], A["w2"]).then_inc(s["w"], 16)
            sp.dma_start(w2e[:, RH:RH + 1], A["b2"].unsqueeze(1)).then_inc(s["w"], 16)
            sp.dma_start(b1[:], A["b1"].unsqueeze(1)).then_inc(s["w"], 16)

        @block.gpsimd
        def _(p):
            p.memset(half_neg[:], -0.5)
            p.memset(hd[0:64, :], 0.0).then_inc(s["mem"], 1)
            p.wait_ge(s["mem"], 1)
            p.memset(hd[32:33, :], 1.0)
            p.memset(h2[32:33, :], 1.0).then_inc(s["mem"], 1)
            p.wait_ge(s["mem"], 2)
            with p.Fori(0, NB) as b:
                p.wait_ge(s["stat"], b + 1)
                apart(p, s["tickp"])
                p.tensor_scalar(var_e[:], mv[:, :, 1], LN_EPS, None, ALU.add).then_inc(s["g1"], 1)
                p.wait_ge(s["g1"], b + 1)
                p.tensor_tensor(rstd[:], var_e[:], half_neg[:], ALU.pow).then_inc(s["rstd"], 1)

        @block.scalar
        def _(a):
            def step(b):
                for k in range(NGB):
                    a.wait_ge(s["xt"], b * NGB + (k + 1))
                    a.activation(xT[:, GN * k:GN * k + GN], TPB, ACT.Copy).then_inc(s["xT"], 1)
                a.wait_ge(s["par"], b + 1)
                a.activation(par[:], SM[:, 0:2 * RH], ACT.Copy).then_inc(s["ac"], 1)
                a.activation(hh[:], SM[0:RH + 1, 2 * RH:3 * RH], ACT.Copy).then_inc(s["parc"], 1)
                a.wait_ge(s["vs"], b + 1)
                a.activation(hd[0:RH, :], vs[:], ACT.Gelu).then_inc(s["ge"], 1)
                a.activation(ex[:], v1[:], ACT.Exp, scale=-0.5).then_inc(s["ex"], 1)
                for k in range(NGB):
                    a.wait_ge(s["hdt"], b * NGB + (k + 1))
                    a.activation(hdt[:, GT * k:GT * k + GT, :], HDT[:, 0:GT * 96].rearrange("p (i c) -> p i c", i=GT),
                                 ACT.Copy).then_inc(s["hdc"], 1)
                a.wait_ge(s["m"], b + 1)
                a.activation(M[:], MM[:, 0:96], ACT.Copy).then_inc(s["ac"], 1)
                a.activation(gram[:], SM[0:RH + 1, 96:96 + RH + 1], ACT.Copy).then_inc(s["mc"], 1)
                a.wait_ge(s["w2t"], b + 2)
                a.activation(w2eT[:], DH[0:RH + 1, 0:P], ACT.Copy).then_inc(s["w2c"], 1)
                a.wait_ge(s["q"], b + 1)
                a.activation(qpar[:], SM[:, 160:160 + RH], ACT.Copy).then_inc(s["qc"], 1)
                for k in range(NGB):
                    a.wait_ge(s["pq"], b * NGB + (k + 1))
                    a.activation(h2[0:RH, GN * k:GN * k + GN], (PRE if k == 0 else DH)[0:RH, :], ACT.Gelu,
                                 bias=b1[:, 0:1]).then_inc(s["h2"], 1)

            a.wait_ge(s["w2t"], 1)
            a.activation(w2eT[:], DH[0:RH + 1, 0:P], ACT.Copy).then_inc(s["w2c"], 1)
            a.wait_ge(s["w2c"], 1)
            with a.Fori(0, NB) as b:
                step(b)

        @block.vector
        def _(v):
            PER = 1 + 2 + 1 + 2 + 2 + 3
            def step(b):
                c = Chain(v, s["vc"], PER, b)
                for i in range(NI):
                    last = v.bn_stats(st[:, i, :], x[:, ds(b * NI + i, 1), :].rearrange("p o f -> p (o f)"))
                c.step(last)
                apart(v, s["tick"])
                for i in range(NI):
                    last = v.bn_aggr(mv[:, i, :], st[:, i, :])
                last.then_inc(s["stat"], 1)
                v.wait_ge(s["rstd"], b + 1)
                for i in range(NI):
                    last = v.tensor_scalar(xn[:, i, :], x[:, ds(b * NI + i, 1), :].rearrange("p o f -> p (o f)"),
                                           mv[:, i, 0:1], rstd[:, i:i + 1], ALU.subtract, ALU.mult)
                last.then_inc(s["xn"], 1)
                v.wait_ge(s["pre"], b + 1)
                for k, bank in enumerate((PRE, DH)):
                    c.step(v.tensor_scalar(v0[:, GN * k:GN * k + GN], bank[0:RH, :], b1[:, 0:1], None, ALU.add))
                v.tensor_tensor(v1[:], v0[:], v0[:], ALU.mult).then_inc(s["v1"], 1)
                v.wait_ge(s["v1"], b + 1)
                c.step(v.tensor_scalar(rv[:], v1[:], 1e-24, 4e-12, ALU.is_lt, ALU.mult))
                v.tensor_tensor(vs[:], v0[:], rv[:], ALU.add).then_inc(s["vs"], 1)
                v.wait_ge(s["vs"], b + 1)
                c.step(v.reciprocal(rv[:], vs[:]))
                v.wait_ge(s["ge"], b + 1)
                c.step(v.tensor_tensor(cdf[:], hd[0:RH, :], rv[:], ALU.mult))
                v.wait_ge(s["ex"], b + 1)
                c.step(v.scalar_tensor_tensor(gp[:], v0[:], SQ, ex[:], ALU.mult, ALU.mult))
                c.step(v.tensor_tensor(gp[:], gp[:], cdf[:], ALU.add))
                v.wait_ge(s["dh"], b + 1)
                for k, bank in enumerate((PRE, DH)):
                    last = v.scalar_tensor_tensor(hd[64:96, GN * k:GN * k + GN], bank[0:RH, :], C,
                                                  gp[:, GN * k:GN * k + GN], ALU.mult, ALU.mult)
                last.then_inc(s["dp"], 1)
                v.wait_ge(s["upd"], b + 1)
                c.step(v.scalar_tensor_tensor(w2e[:], MM[:, 96:96 + RH + 1], -LR * C, w2e[:], ALU.mult, ALU.add))
                c.step(v.scalar_tensor_tensor(w1T[:], MM[:, 160:160 + RH], -LR, w1T[:], ALU.mult, ALU.add))
                c.step(v.scalar_tensor_tensor(b1[:], MM[0:RH, 200:201], -LR, b1[:], ALU.mult, ALU.add))
                v.sem_inc(s["updc"], 1)
                for k in range(NGB):
                    v.wait_ge(s["o"], b * NGB + (k + 1))
                    xg = x[:, ds(b * NI + GT * k, GT), :].rearrange("p i f -> p (i f)")
                    v.tensor_tensor(xg, OUT if k == 0 else TPB, xg, ALU.add).then_inc(s["x"], 1)
                v.wait_ge(s["x"], b * NGB + NGB)
                c.close()

            v.wait_ge(s["w"], 160)
            v.tensor_tensor(dn[:], tk[:], tv[:], ALU.subtract)
            v.tensor_tensor(dT[:], tkT[:], tvT[:], ALU.subtract).then_inc(s["wc"], 1)
            with v.Fori(0, NB) as b:
                step(b)

        @block.tensor
        def _(t):
            def turn_w2(n):
                t.transpose(DH[0:RH + 1, 0:P], w2e[:], ident[:]).then_inc(s["w2t"], 1)

            def step(b):
                t.wait_ge(s["xn"], b + 1)
                for k in range(NGB):
                    if k:
                        t.wait_ge(s["xT"], b * NGB + k)
                    for i in range(GT):
                        last = t.transpose(TPB[:, P * i:P * i + P], xn[:, GT * k + i, :], ident[:])
                    last.then_inc(s["xt"], 1)
                t.matmul(SM[:, 0:RH], tk[:], w1T[:], start=True, stop=True)
                t.matmul(SM[:, RH:2 * RH], dn[:], w2e[:, 0:RH], start=True, stop=True)
                t.matmul(SM[0:RH + 1, 2 * RH:3 * RH], w2e[:], w2e[:, 0:RH], start=True, stop=True).then_inc(s["par"], 1)
                t.wait_ge(s["parc"], b + 1)
                t.wait_ge(s["xT"], b * NGB + NGB)
                for k, bank in enumerate((PRE, DH)):
                    last = t.matmul(bank[0:RH, :], par[:, 0:RH], xT[:, GN * k:GN * k + GN], start=True, stop=True)
                last.then_inc(s["pre"], 1)
                t.wait_ge(s["vs"], b + 1)
                t.wait_ge(s["ge"], b + 1)
                for k, bank in enumerate((PRE, DH)):
                    t.matmul(bank[0:RH, :], par[:, RH:2 * RH], xT[:, GN * k:GN * k + GN], start=True, stop=False)
                    last = t.matmul(bank[0:RH, :], hh[:], hd[0:RH + 1, GN * k:GN * k + GN], start=False, stop=True)
                last.then_inc(s["dh"], 1)
                t.wait_ge(s["dp"], b + 1)
                for k in range(NGB):
                    if k:
                        t.wait_ge(s["hdc"], b * NGB + k)
                    apart(t, s["tickt"])
                    for i in range(GT):
                        n = GT * k + i
                        last = t.transpose(HDT[:, 96 * i:96 * i + 96], hd[:, P * n:P * n + P], ident[0:96, 0:96])
                    last.then_inc(s["hdt"], 1)
                t.wait_ge(s["hdc"], b * NGB + NGB)
                for i in range(NI):
                    t.matmul(MM[:, 0:96], xn[:, i, :], hdt[:, i, :], start=(i == 0), stop=(i == NI - 1))
                for i in range(NI):
                    last = t.matmul(SM[0:RH + 1, 96:96 + RH + 1], hdt[:, i, 0:RH + 1], hdt[:, i, 0:RH + 1],
                                    start=(i == 0), stop=(i == NI - 1))
                last.then_inc(s["m"], 1)
                t.wait_ge(s["mc"], b + 1)
                t.matmul(MM[:, 96:96 + RH + 1], dT[:], M[:, 0:RH + 1], start=True, stop=False)
                t.matmul(MM[:, 96:96 + RH + 1], w2eT[:], gram[:], start=False, stop=True)
                t.matmul(MM[:, 160:160 + RH], tkT[:], M[:, 64:96], start=True, stop=True)
                for i in range(NI):
                    last = t.matmul(MM[0:RH, 200:201], hdt[:, i, 64:96], hdt[:, i, RH:RH + 1],
                                    start=(i == 0), stop=(i == NI - 1))
                last.then_inc(s["upd"], 1)
                t.wait_ge(s["updc"], b + 1)
                apart(t, s["tickt"])
                turn_w2(b)
                t.matmul(SM[:, 160:160 + RH], tq[:], w1T[:], start=True, stop=True).then_inc(s["q"], 1)
                t.wait_ge(s["qc"], b + 1)
                t.wait_ge(s["w2c"], b + 2)
                for k, bank in enumerate((PRE, DH)):
                    t.matmul(bank[0:RH, :], qpar[:], xT[:, GN * k:GN * k + GN], start=True, stop=True)\
                        .then_inc(s["pq"], 1)
                for k in range(NGB):
                    t.wait_ge(s["h2"], b * NGB + (k + 1))
                    for i in range(GT):
                        n = GT * k + i
                        o = (OUT if k == 0 else TPB)[:, P * i:P * i + P]
                        t.matmul(o, xT[:, P * n:P * n + P], tqT[:], start=True, stop=False)
                        last = t.matmul(o, h2[:, P * n:P * n + P], w2eT[:], start=False, stop=True)
                    last.then_inc(s["o"], 1)
                t.wait_ge(s["x"], b * NGB + NGB)

            t.wait_ge(s["w"], 160)
            t.wait_ge(s["mem"], 2)
            turn_w2(-1)
            t.wait_ge(s["wc"], 1)
            t.wait_ge(s["w2c"], 1)
            with t.Fori(0, NB) as b:
                step(b)



def kernel(**inputs):
    import numpy as _np
    import concourse.bacc as _bacc
    from concourse import mybir as _mybir
    from concourse.bass_utils import run_bass_kernel_spmd as _run

    nc = _bacc.Bacc("TRN2", target_bir_lowering=False, num_devices=1)
    arrays = lay_out(inputs)
    args = {n: nc.dram_tensor("in_" + n, a.shape, _mybir.dt.from_np(a.dtype), kind="ExternalInput").ap()
            for n, a in arrays.items()}
    out = nc.dram_tensor("out_0", (NB, NI * P, P), _mybir.dt.float32, kind="ExternalOutput").ap()
    build(nc, args, out)
    r = _run(nc, [{"in_" + n: a for n, a in arrays.items()}], core_ids=[0])
    return r.results[0]["out_0"]


def lay_out(inputs):
    a, r, f = "L0_attn_a_", "L0_attn_b_", "L0_ffn_"
    c = np.ascontiguousarray

    def units(w, shared):
        return c(np.concatenate([w.reshape(UNITS, P, P), shared[None]]).transpose(2, 0, 1))

    I = {n: np.asarray(v) for n, v in inputs.items()}
    down = I[f + "down_w"].reshape(UNITS, 2, P, INNER).transpose(1, 3, 0, 2).reshape(P, UNITS, P)
    lo_q, lo_k = np.zeros((2, P), np.float32)
    for j in range(HC):
        lo_q[32 * j + 8:32 * j + 16] = -1
        lo_k[32 * j + 16:32 * j + 24] = -1
    sel = np.zeros((3, EXPERTS, UNITS, 2, INNER), np.float32)
    for e in range(EXPERTS):
        sel[:, e, e // 2, e % 2] = 1
    return {
        "x": c(I[a + "x"]),
        "wqT": c(I[a + "Wq"].T), "wkT": c(I[a + "Wk"].T), "wvT": c(I[a + "Wv"].T), "wk": c(I[a + "Wk"]),
        "woT": c(I[a + "Wo"].T), "bo": c(I[a + "bo"]), "planes": c(I[a + "planes_T"]),
        "protos": c(I[a + "protos_T"]), "temp": c(I[a + "logit_temp"].reshape(1)),
        "rwT": c(I[f + "router_weight"].T), "rbias": c(I[f + "router_bias"]),
        "w_g": units(I[f + "gate_w"], I[f + "shared_gate_w"]),
        "w_u": units(I[f + "up_w"], I[f + "shared_up_w"]),
        "w_d": c(np.concatenate([down, I[f + "shared_down_w"].T[:, None]], axis=1)),
        "tk": c(I[r + "t_k"]), "tv": c(I[r + "t_v"]), "tq": c(I[r + "t_q"]), "tkT": c(I[r + "t_k"].T),
        "tvT": c(I[r + "t_v"].T), "tqT": c(I[r + "t_q"].T), "w1T": c(I[r + "W1"].T), "w2": c(I[r + "W2"]),
        "b1": c(I[r + "b1"]), "b2": c(I[r + "b2"]),
        "ident": np.eye(P, dtype=np.float32), "msk": c(np.stack([lo_q, lo_k], axis=1)),
        "sel": sel.reshape(96, UNITS, P),
    }
```

```python
from contextlib import ExitStack

import numpy as np
import concourse.bass as bass
from concourse import mybir

F32 = mybir.dt.float32
F32R = mybir.dt.float32r
BF16 = mybir.dt.bfloat16
ALU = mybir.AluOpType
ACT = mybir.ActivationFunctionType
AX = mybir.AxisListType
ds = bass.ds

P = 128
NB = 4
NI = 8
GT = 4
GN = GT * P
NG = NB * NI // GT
HEADS, HD = 16, 8
TABLES, BITS, CORNERS = 8, 4, 16
NP = TABLES * BITS
S = TABLES * CORNERS
HC = 4
NC = HEADS // HC
EXPERTS, INNER, TOPK, NGROUP = 32, 64, 4, 4
GE = EXPERTS // NGROUP
UNITS = EXPERTS * INNER // P
ROUTE_SCALE = 2.5
LN_EPS = 1e-5
LR = 1e-3
RH = 32
LOWEST = -3.0e38
SMALL = 30.0


class Chain:

    def __init__(self, eng, sem, per_turn=0, turn=0):
        self.eng, self.sem, self.base, self.n, self.per_turn = eng, sem, turn * per_turn, 0, per_turn

    def step(self, ins):
        self.n += 1
        ins.then_inc(self.sem, 1)
        self.eng.wait_ge(self.sem, self.base + self.n)

    def close(self):
        assert self.n == self.per_turn, (self.n, self.per_turn)


def apart(eng, tick):
    eng.sem_inc(tick, 1)


def split_rows(v, c, hi, lo, src, tmp=None):
    c.step(v.tensor_copy(hi, src))
    c.step(v.tensor_tensor(lo, src, hi.bitcast(F32), ALU.subtract))


def three_pass(t, out, lhs, rhs, start=True, stop=True):
    t.matmul(out, lhs[0], rhs[0], start=start, stop=False, skip_group_check=True)
    t.matmul(out, lhs[1], rhs[0], start=False, stop=False, skip_group_check=True)
    return t.matmul(out, lhs[0], rhs[1], start=False, stop=stop, skip_group_check=True)


def build(nc, A, out, stages=4):
    top = ExitStack()
    with top:
        def mk(ctx):
            return (lambda n, s, d: ctx.enter_context(nc.sbuf_tensor(n, s, d)),
                    lambda n: ctx.enter_context(nc.semaphore(n)))
        sb, sem = mk(top)
        PS = top.enter_context(nc.psum_tensor("PS", [P, 8, 512], F32))
        x = sb("x", [P, NB * NI + GT, P], F32)
        ident = sb("ident", [P, P], F32)
        raw = {n: sb("raw_" + n, [P, UNITS + 1, P], F32) for n in "gud"}
        rwH, rwL = sb("rwH", [P, EXPERTS], F32R), sb("rwL", [P, EXPERTS], F32R)
        rbias = sb("rbias", [P, EXPERTS], F32)
        s_done = sem("s_done")
        ticks = {n: sem(n) for n in ("tick", "tickp", "tickt")}

        attention(nc, A, mk, x, ident, PS, raw, rwH, rwL, ticks)
        W = {n: sb(n, [P, UNITS + 1, P], F32R) for n in ("gH", "gL", "uH", "uL", "dH", "dL")}
        sel = sb("sel", [96, UNITS, P], BF16)
        split_experts(nc, A, mk, raw, W, rbias, sel)
        if stages >= 2:
            ffn(nc, A, mk, ticks, "f1", x, ident, W, rwH, rwL, rbias, sel, PS)
        if stages >= 3:
            recon(nc, A, mk, ticks, x, ident, PS)
        if stages >= 4:
            ffn(nc, A, mk, ticks, "f2", x, ident, W, rwH, rwL, rbias, sel, PS)
        block = top.enter_context(nc.Block())

        @block.sync
        def _(sp):
            o = out.rearrange("b (p i) d -> p b i d", i=NI)
            for b in range(NB):
                sp.dma_start(o[:, b], x[:, b * NI:(b + 1) * NI, :]).then_inc(s_done, 16)
            sp.wait_ge(s_done, 16 * NB)


def split_experts(nc, A, mk, raw, W, rbias, sel):
    ctx = ExitStack()
    with ctx:
        sb, sem = mk(ctx)
        selF = sb("selF", [96, UNITS, P], F32)
        s_w, s_h, s_c = sem("p_w"), sem("p_h"), sem("p_c")
        block = ctx.enter_context(nc.Block())

        @block.sync
        def _(sp):
            sp.dma_start(selF[:], A["sel"]).then_inc(s_w, 16)
            sp.dma_start(rbias[:], A["rbias"].partition_broadcast(P)).then_inc(s_w, 16)

        @block.scalar
        def _(a):
            for n in "gud":
                a.activation(W[n + "H"][:], raw[n][:], ACT.Copy).then_inc(s_h, 1)

        @block.vector
        def _(v):
            c = Chain(v, s_c)
            for k, n in enumerate("gud"):
                v.wait_ge(s_h, k + 1)
                v.tensor_tensor(W[n + "L"][:], raw[n][:], W[n + "H"][:].bitcast(F32), ALU.subtract)
            v.wait_ge(s_w, 32)
            c.step(v.tensor_copy(sel[:], selF[:]))



def attention(nc, A, mk, x, ident, PS, raw, rwH, rwL, ticks):
    ctx = ExitStack()
    with ctx:
        sb0, sem = mk(ctx)

        def sb(n, shape, d=F32):
            return sb0("a_" + n, shape, d)

        wqH, wqL = sb("wqH", [P, NC, P], F32R), sb("wqL", [P, NC, P], F32R)
        wkvH, wkvL = sb("wkvH", [P, 512], F32R), sb("wkvL", [P, 512], F32R)
        m1H, m1L = sb("m1H", [P, 512], F32R), sb("m1L", [P, 512], F32R)
        prH, prL = sb("prH", [P, 512], F32R), sb("prL", [P, 512], F32R)
        wo, bo = sb("wo", [P, P]), sb("bo", [P, P])
        msk = sb("msk", [P, 2])
        temp = sb("temp", [P, 4])
        st, mv = sb("st", [P, GT, 6]), sb("mv", [P, GT, 2])
        half_neg, rstd, var_e = (sb(n, [P, GT]) for n in ("hn", "rstd", "vare"))
        xn = sb("xn", [P, GT, P])
        xH, xL = sb("xH", [P, 2, GN], F32R), sb("xL", [P, 2, GN], F32R)
        af = sb("af", [P, 2, GN])
        aH, aL = sb("aH", [P, 2, NC, GN], F32R), sb("aL", [P, 2, NC, GN], F32R)
        kv = sb("kv", [P, GT, HEADS, 32])
        qH = sb("qH", [P, GN], F32R)
        qs = sb("qs", [P, 2, NC, GN], F32R)
        ee, pn = sb("ee", [P, 4, 512]), sb("pn", [P, 4, 512])
        sm, ri = sb("sm", [P, 2, 32]), sb("ri", [P, 4, 32])
        mx, dd = sb("mx", [P, 2, 32]), sb("dd", [P, 2, 512])
        bound = sb("bound", [1, 2 * BITS * CORNERS + CORNERS + 2])
        small = sb0("a_small", [1, 1], mybir.dt.int32)
        bT, bH = sb("bT", [P, 512]), sb("bH", [P, 512], F32R)
        kst = sb("kst", [P, NC, HC, S], F32R)
        bv = sb("bv", [P, HEADS, 32])
        nm = sb("nm", [P, GT, HEADS])
        nmH = sb("nmH", [P, GT, HEADS], F32R)
        nmp = sb("nmp", [P, GT, HEADS, 32])
        e2 = sb("e2", [P, 2, HC, GN])
        nT = sb("nT", [P, NC, GN])
        rden = sb("rden", [P, GT, HEADS])
        on = sb("on", [P, GT, P])
        oT = sb("oT", [P, GN])
        raws = raw["g"][:].rearrange("p u n -> p (u n)")
        wq, wkv, plane, proto = (raws[:, 512 * n:512 * n + 512] for n in range(4))
        wk = raws[:, 2048:2048 + P]
        rw = sb("rw", [P, EXPERTS])

        s_x0, s_x, s_w, s_wc, s_m1, s_raw, s_rawd, s_temp = (
            sem("a_" + n) for n in ("x0", "x", "w", "wc", "m1", "raw", "rawd", "temp"))
        names = ("xb mb st stat rstd xn xt xh xl ap af ah al kp kc qp qh qs lg d e sm ri pn bk bt bvt bv bh stk sc mx nmh "
                 "nmp nmt qf ss e2 pv nc ot rd on ht oc y x pc").split()
        s = {n: sem("a_s_" + n) for n in names}
        s.update(ticks)
        TPB, PJ, BK, NV = (PS[:, n, :] for n in (0, 1, 6, 7))

        def LG(n):
            return PS[:, 2 + n % 2, :]

        def SC(n):
            return PS[:, 4 + n % 2, :]

        def after(eng, name, value):
            if not isinstance(value, int) or value > 0:
                eng.wait_ge(s[name], value)

        def tokens(g):
            return x[:, ds(g * GT, GT), :].rearrange("p i f -> p (i f)")

        def spread(n, first, last, total=16):
            m = last - first + 1
            k = min(max(n - first, 0), m)
            return range(total * k // m, total * min(max(n - first + 1, 0), m) // m)

        OUT = 13
        LAG = 4
        A2 = (0, 5)
        A3 = (6, 12)

        def pipeline(eng, step):
            for z in range(2):
                step(0, z, True, False)
            with eng.Fori(1, NG // 2) as i:
                for z in range(2):
                    step(i, z, True, True)
            for z in range(2):
                step(NG // 2, z, False, True)

        block = ctx.enter_context(nc.Block())
        NW = 3 * NC + 4 * NC + HEADS + HC * TABLES + 6
        WC = 1 + HC + 3 + 6 + 2 * 5

        @block.sync
        def _(sp):
            xi = A["x"].rearrange("b (p i) d -> p b i d", i=NI)
            sp.dma_start(x[:, 0:NI, :], xi[:, 0]).then_inc(s_x0, 16)
            sp.dma_start(ident[:], A["ident"]).then_inc(s_x0, 16)
            sp.wait_ge(s_m1, 1)
            sp.dma_start(wk, A["wk"]).then_inc(s_w, 16)
            for h in range(HEADS):
                sp.dma_start(plane[HD * h:HD * h + HD, NP * h:NP * h + NP], A["planes"]).then_inc(s_w, 16)
            sp.dma_start(temp[:, 0:1], A["temp"].partition_broadcast(P)).then_inc(s_w, 16)
            sp.dma_start(msk[:], A["msk"]).then_inc(s_w, 16)
            for n in range(HC * TABLES):
                sp.dma_start(proto[BITS * n:BITS * n + BITS, CORNERS * n:CORNERS * n + CORNERS],
                             A["protos"]).then_inc(s_w, 16)
            sp.dma_start(bound[:, 0:BITS * CORNERS], A["protos"].rearrange("k r -> (k r)").unsqueeze(0)).then_inc(s_w, 16)
            sp.dma_start(wo[:], A["woT"]).then_inc(s_w, 16)
            sp.dma_start(bo[:], A["bo"].partition_broadcast(P)).then_inc(s_w, 16)
            for b in range(1, NB):
                sp.dma_start(x[:, b * NI:(b + 1) * NI, :], xi[:, b]).then_inc(s_x, 16)
            sp.dma_start(rw[:], A["rwT"]).then_inc(s_x, 16)
            for name in "udg":
                if name == "g":
                    sp.wait_ge(s_rawd, 1)
                sp.dma_start(raw[name][:], A["w_" + name]).then_inc(s_raw, 16)
            sp.wait_ge(s_raw, 48)

        def project_pool_rstd(g, G):
            after(g, "stat", G + 1)
            apart(g, s["tickp"])
            g.tensor_scalar(var_e[:], mv[:, :, 1], LN_EPS, None, ALU.add).then_inc(s["pc"], 1)
            g.wait_ge(s["pc"], G + 1)
            g.tensor_tensor(rstd[:], var_e[:], half_neg[:], ALU.pow).then_inc(s["rstd"], 1)

        def project_pool_low(g, G, z, c):
            g.wait_ge(s["ah"], 4 * G + (c + 1))
            g.tensor_tensor(aL[:, z, c, :], af[:, c % 2, :], aH[:, z, c, :].bitcast(F32),
                            ALU.subtract).then_inc(s["al"], 1)

        @block.gpsimd
        def _(g):
            g.memset(raws[:, 0:2048], 0.0).then_inc(s_m1, 1)
            g.memset(half_neg[:], -0.5)
            g.memset(nmp[:], 0.0)
            g.memset(bv[:], 0.0)
            g.memset(x[:, NB * NI:, :], 0.0).then_inc(s_m1, 1)
            g.wait_ge(s_m1, 2)
            g.memset(bv[:, :, HD:HD + 1], 1.0).then_inc(s_m1, 1)
            project_pool_rstd(g, 0)
            g.wait_ge(s_w, 16 * NW)
            for c in range(NC):
                project_pool_low(g, 0, 0, c)

            def step(half, z, buckets, attends):
                G = 2 * half + z
                if attends:
                    x4 = x[:, ds((G - 2) * GT, GT), :]
                    g.tensor_tensor(x4, x4, bo[:].unsqueeze(1).to_broadcast([P, GT, P]), ALU.add).then_inc(s["xb"], 1)
                if not buckets:
                    return
                for n in range(16):
                    g.wait_ge(s["ri"], 16 * G + (n + 1))
                    after(g, "bk", 16 * G + (n - 3))
                    g.tensor_tensor(pn[:, n % 4, :].rearrange("p (q r) -> p q r", r=CORNERS),
                                    ee[:, n % 4, :].rearrange("p (q r) -> p q r", r=CORNERS),
                                    ri[:, n % 4, :].unsqueeze(2).to_broadcast([P, 32, CORNERS]),
                                    ALU.mult).then_inc(s["pn"], 1)
                    if n == 1:
                        project_pool_rstd(g, G + 1)
                    if 7 <= n < 11:
                        project_pool_low(g, G + 1, 1 - z, n - 7)

            pipeline(g, step)

        @block.scalar
        def _(a):
            for n in range(3):
                for c in range(NC):
                    if n == 0 and c == 0:
                        a.wait_ge(s_m1, 1)
                    a.dma_start(wq.rearrange("p (c j k) -> p c j k", c=NC, j=HC)[:, c, :, 8 * n:8 * n + 8],
                                A["wqT"].rearrange("f (c j d) -> f c j d", c=NC, j=HC)[:, c]).then_inc(s_w, 16)
            for n, w in enumerate(("wkT", "wkT", "wkT", "wvT")):
                for c in range(NC):
                    a.dma_start(wkv.rearrange("p (c j k) -> p c j k", c=NC, j=HC)[:, c, :, 8 * n:8 * n + 8],
                                A[w].rearrange("f (c j d) -> f c j d", c=NC, j=HC)[:, c]).then_inc(s_w, 16)

            def high_x(G, z):
                a.wait_ge(s["xt"], G + 1)
                a.activation(xH[:, z, :], PJ, ACT.Copy).then_inc(s["xh"], 1)

            def planes(G, z, c):
                a.wait_ge(s["ap"], 4 * G + (c + 1))
                after(a, "al", 4 * G + (c - 1))
                a.activation(af[:, c % 2, :], PJ, ACT.Tanh).then_inc(s["af"], 1)

            def keys(G, i):
                a.wait_ge(s["kp"], 4 * G + (i + 1))
                a.activation(kv[:, i, :, :], TPB.rearrange("p (h k) -> p h k", k=32), ACT.Copy).then_inc(s["kc"], 1)

            def high_q(G, c):
                a.wait_ge(s["qp"], 4 * G + (c + 1))
                after(a, "qs", 4 * G + c)
                a.activation(qH[:], PJ, ACT.Copy).then_inc(s["qh"], 1)

            def step(half, z, buckets, attends, guarded):
                G = 2 * half + z
                H = G - 2
                for n in range(16):
                    if attends and z == 0 and n == 0:
                        a.wait_ge(s["bk"], 16 * G)
                        a.activation(bT[:], BK, ACT.Copy).then_inc(s["bt"], 1)
                    if buckets:
                        if guarded:
                            a.wait_ge(s["d"], 16 * G + (n + 1))
                            src = dd[:, n % 2, :]
                        else:
                            a.wait_ge(s["lg"], 16 * G + (n + 1))
                            src = LG(n)
                        after(a, "pn", 16 * G + (n - 3))
                        a.activation(ee[:, n % 4, :], src, ACT.Exp).then_inc(s["e"], 1)
                    if buckets:
                        if n == 5:
                            high_x(G + 1, 1 - z)
                        if 7 <= n < 11:
                            planes(G + 1, 1 - z, n - 7)
                    if buckets and 1 <= n <= GT:
                        keys(G, n - 1)
                    if attends:
                        for m in spread(n, *A3):
                            a.wait_ge(s["ss"], 16 * H + (m + 1))
                            if m >= 8:
                                a.wait_ge(s["pv"], 4 * H + (m // 4 - 1))
                            a.activation(e2[:, m // 4 % 2, m % 4, :], SC(m), ACT.Exp, scale=float(HD) ** -0.5).then_inc(s["e2"], 1)
                            if m % 4 == 2 and m >= 6:
                                numerators(a, H, m // 4 - 1)
                        if n == A3[1]:
                            numerators(a, H, NC - 1)
                    if n < 4 and (attends and (buckets or z == 0) or z == 1 and buckets):
                        high_q(G - 1, n)
                if attends:
                    a.wait_ge(s["ht"], H + 1)
                    a.activation(oT[:], TPB, ACT.Copy).then_inc(s["oc"], 1)

            def numerators(a, H, c):
                a.wait_ge(s["pv"], 4 * H + (c + 1))
                a.activation(nT[:, c, :], NV, ACT.Copy).then_inc(s["nc"], 1)

            a.wait_ge(s_w, 16 * NW)
            a.activation(temp[:, 1:2], temp[:, 0:1], ACT.Exp).then_inc(s_temp, 1)
            high_x(0, 0)
            for c in range(NC):
                planes(0, 0, c)
            a.wait_ge(s_temp, 2)
            flag = a.value_load(small[:], min_val=0, max_val=1)
            with a.If(flag == 1):
                pipeline(a, lambda *where: step(*where, guarded=False))
            with a.Else():
                pipeline(a, lambda *where: step(*where, guarded=True))

        @block.vector
        def _(v):
            def stats(G):
                for i in range(GT):
                    last = v.bn_stats(st[:, i, :], x[:, ds(G * GT + i, 1), :].rearrange("p o f -> p (o f)"))
                last.then_inc(s["st"], 1)

            def stats2(G):
                v.wait_ge(s["st"], G + 1)
                apart(v, s["tick"])
                for i in range(GT):
                    last = v.bn_aggr(mv[:, i, :], st[:, i, :])
                last.then_inc(s["stat"], 1)

            def norm(G):
                v.wait_ge(s["rstd"], G + 1)
                for i in range(GT):
                    last = v.tensor_scalar(xn[:, i, :], x[:, ds(G * GT + i, 1), :].rearrange("p o f -> p (o f)"),
                                           mv[:, i, 0:1], rstd[:, i:i + 1], ALU.subtract, ALU.mult)
                last.then_inc(s["xn"], 1)

            def low_x(G, z):
                v.wait_ge(s["xh"], G + 1)
                v.tensor_tensor(xL[:, z, :], PJ, xH[:, z, :].bitcast(F32), ALU.subtract).then_inc(s["xl"], 1)

            def high_a(G, z, c):
                v.wait_ge(s["af"], 4 * G + (c + 1))
                v.tensor_copy(aH[:, z, c, :], af[:, c % 2, :]).then_inc(s["ah"], 1)

            def stack_q(G, z, c):
                v.wait_ge(s["qh"], 4 * G + (c + 1))
                v.scalar_tensor_tensor(qs[:, z, c, :], qH[:].bitcast(F32), msk[:, 0:1], PJ,
                                       ALU.mult, ALU.add).then_inc(s["qs"], 1)

            def sums(G, n):
                v.wait_ge(s["e"], 16 * G + (n + 1))
                v.tensor_reduce(sm[:, n % 2, :], ee[:, n % 4, :].rearrange("p (q r) -> p q r", r=CORNERS),
                                AX.X, ALU.add).then_inc(s["sm"], 1)
                v.wait_ge(s["sm"], 16 * G + (n + 1))
                after(v, "pn", 16 * G + (n - 3))
                v.reciprocal(ri[:, n % 4, :], sm[:, n % 2, :]).then_inc(s["ri"], 1)

            def step(half, z, buckets, attends, guarded):
                G = 2 * half + z
                H = G - 2

                def outputs(i):
                    bank = (TPB, NV)[i % 2].rearrange("p (h k) -> p h k", k=32)
                    v.wait_ge(s["ot"], 4 * H + (i + 1))
                    v.reciprocal(rden[:, i, :], bank[:, :, HD]).then_inc(s["rd"], 1)
                    v.wait_ge(s["rd"], 4 * H + (i + 1))
                    v.tensor_tensor(on[:, i, :].rearrange("p (h d) -> p h d", d=HD), bank[:, :, 0:HD],
                                    rden[:, i, :].unsqueeze(2).to_broadcast([P, HEADS, HD]),
                                    ALU.mult).then_inc(s["on"], 1)

                for n in range(16):
                    if attends and z == 0 and n == 0:
                        stack_keys(half)
                    if buckets:
                        if guarded:
                            lg = LG(n).rearrange("p (q r) -> p q r", r=CORNERS)
                            v.wait_ge(s["lg"], 16 * G + (n + 1))
                            v.tensor_reduce(mx[:, n % 2, :], lg, AX.X, ALU.max).then_inc(s["mb"], 1)
                            v.wait_ge(s["mb"], 16 * G + (n + 1))
                            after(v, "e", 16 * G + (n - 1))
                            v.tensor_tensor(dd[:, n % 2, :].rearrange("p (q r) -> p q r", r=CORNERS), lg,
                                            mx[:, n % 2, :].unsqueeze(2).to_broadcast([P, 32, CORNERS]),
                                            ALU.subtract).then_inc(s["d"], 1)
                        if n >= 1:
                            sums(G, n - 1)
                        if 8 <= n < 12:
                            high_a(G + 1, 1 - z, n - 8)
                        if n == 0:
                            stats(G + 1)
                            stats2(G + 1)
                        if n == 3:
                            norm(G + 1)
                        if n == 5:
                            low_x(G + 1, 1 - z)
                    if attends:
                        for m in spread(n, *A2):
                            v.wait_ge(s["sc"], 16 * H + (m + 1))
                            v.tensor_reduce(nm[:, m // 4, 4 * (m % 4):4 * (m % 4) + 4],
                                            SC(m).rearrange("p (j s) -> p j s", s=S), AX.X, ALU.max,
                                            negate=True).then_inc(s["mx"], 1)
                        if n == A2[1]:
                            v.wait_ge(s["mx"], 16 * H + 16)
                            v.tensor_copy(nmH[:], nm[:]).then_inc(s["nmh"], 1)
                            v.wait_ge(s["nmh"], H + 1)
                            v.tensor_copy(nmp[:, :, :, 24], nmH[:].bitcast(F32))
                            v.tensor_tensor(nmp[:, :, :, 25], nm[:], nmH[:].bitcast(F32),
                                            ALU.subtract).then_inc(s["nmp"], 1)
                        for m in spread(n, *A3):
                            if m % 4 == 0:
                                c = m // 4
                                v.wait_ge(s["nmt"], 4 * H + (c + 1))
                                v.tensor_tensor(qs[:, z, c, :], qs[:, z, c, :].bitcast(F32), TPB,
                                                ALU.add).then_inc(s["qf"], 1)
                    if n < 4 and (attends and (buckets or z == 0) or z == 1 and buckets):
                        stack_q(G - 1, 1 - z, n)
                    if attends and n in range(OUT, OUT + GT):
                        outputs(n - OUT)
                if buckets:
                    sums(G, 15)
                if attends:
                    outputs(3)
                    v.wait_ge(s["xb"], H + 1)
                    v.wait_ge(s["y"], H + 1)
                    v.tensor_tensor(tokens(H), NV, tokens(H), ALU.add).then_inc(s["x"], 1)

            def stack_keys(half):
                v.wait_ge(s["bt"], half)
                v.tensor_copy(bH[:], bT[:]).then_inc(s["bh"], 1)
                v.wait_ge(s["bh"], half)
                for j in range(HC):
                    r = slice(32 * j, 32 * j + 24)
                    last = v.scalar_tensor_tensor(kst[r, :, j, :],
                                                  bH[r, :].bitcast(F32).rearrange("p (c s) -> p c s", c=NC),
                                                  msk[r, 1:2], bT[r, :].rearrange("p (c s) -> p c s", c=NC),
                                                  ALU.mult, ALU.add)
                last.then_inc(s["stk"], 1)
                v.wait_ge(s["bvt"], half)
                v.tensor_copy(bv[:, :, 0:HD],
                              TPB.rearrange("p (h k) -> p h k", k=32)[:, :, 24:32]).then_inc(s["bv"], 1)

            c = Chain(v, s_wc)
            c.step(v.memset(kst[:].bitcast(F32), 0.0))
            for j in range(HC):
                c.step(v.memset(kst[32 * j:32 * j + 32, :, j, :].bitcast(F32), 1.0))
            v.wait_ge(s_x0, 32)
            stats(0)
            stats2(0)
            norm(0)
            v.wait_ge(s_w, 16 * NW)
            v.wait_ge(s_temp, 1)
            c.step(v.tensor_scalar(temp[:, 2:3], temp[:, 1:2], 0.01, 20.0, ALU.max, ALU.min))
            c.step(v.reciprocal(temp[:, 3:4], temp[:, 2:3]))
            c.step(v.tensor_scalar(proto, proto, temp[:, 3:4], None, ALU.mult))
            n = BITS * CORNERS
            b0, b1, b2, b3 = bound[:, 0:n], bound[:, n:2 * n], bound[:, 2 * n:2 * n + CORNERS], bound[:, 2 * n + CORNERS:]
            c.step(v.tensor_scalar(b1, b0, -1.0, None, ALU.mult))
            c.step(v.tensor_tensor(b0, b0, b1, ALU.max))
            c.step(v.tensor_reduce(b2, b0.rearrange("p (k r) -> p r k", r=CORNERS), AX.X, ALU.add))
            c.step(v.tensor_reduce(b3[:, 0:1], b2, AX.X, ALU.max))
            c.step(v.tensor_tensor(b3[:, 1:2], b3[:, 0:1], temp[0:1, 3:4], ALU.mult))
            c.step(v.tensor_scalar(small[:], b3[:, 1:2], SMALL, None, ALU.is_le))
            v.sem_inc(s_temp, 1)
            v.wait_ge(s["rstd"], 1)
            low_x(0, 0)
            v.wait_ge(s_m1, 4)
            split_rows(v, c, m1H[:], m1L[:], LG(0))
            split_rows(v, c, wkvH[:], wkvL[:], wkv)
            split_rows(v, c, prH[:], prL[:], proto)
            split_rows(v, c, wqH[:].rearrange("p c n -> p (c n)"), wqL[:].rearrange("p c n -> p (c n)"), wq)
            v.wait_ge(s_x, 16 * NB)
            split_rows(v, c, rwH[:], rwL[:], rw[:])
            v.sem_inc(s_rawd, 1)
            v.sem_inc(s["x"], 1)
            for c in range(NC):
                high_a(0, 0, c)
            flag = v.value_load(small[:], min_val=0, max_val=1)
            with v.If(flag == 1):
                pipeline(v, lambda *where: step(*where, guarded=False))
            with v.Else():
                pipeline(v, lambda *where: step(*where, guarded=True))

        @block.tensor
        def _(t):
            def transpose_x(G):
                t.wait_ge(s["xn"], G + 1)
                after(t, "qs", 4 * (G - 1))
                after(t, "af", 4 * G)
                apart(t, s["tickt"])
                for i in range(GT):
                    last = t.transpose(PJ[:, P * i:P * i + P], xn[:, i, :], ident[:])
                last.then_inc(s["xt"], 1)

            def planes(G, z, c):
                if c == 0:
                    t.wait_ge(s["xl"], G + 1)
                else:
                    t.wait_ge(s["af"], 4 * G + c)
                three_pass(t, PJ, (m1H[:, P * c:P * c + P], m1L[:, P * c:P * c + P]),
                           (xH[:, z, :], xL[:, z, :])).then_inc(s["ap"], 1)

            def keys(G, z, i):
                if i:
                    t.wait_ge(s["kc"], 4 * G + i)
                tok = slice(P * i, P * i + P)
                three_pass(t, TPB, (xH[:, z, tok], xL[:, z, tok]), (wkvH[:], wkvL[:])).then_inc(s["kp"], 1)

            def logits(G, z, n):
                if n == 16:
                    z = 1 - z
                i, c = n // 4 % GT, n % 4
                tok = slice(P * i, P * i + P)
                if n % 16 < NC:
                    t.wait_ge(s["al"], 4 * G + (n // 4 + c + 1))
                after(t, "e", 16 * G + (n - 1))
                three_pass(t, LG(n), (aH[:, z, c, tok], aL[:, z, c, tok]), (prH[:], prL[:])).then_inc(s["lg"], 1)

            def queries(G, z, c):
                if c == 0:
                    t.wait_ge(s["af"], 4 * G + 8)
                else:
                    t.wait_ge(s["qs"], 4 * G + c)
                three_pass(t, PJ, (wqH[:, c, :], wqL[:, c, :]), (xH[:, z, :], xL[:, z, :])).then_inc(s["qp"], 1)

            def step(half, z, buckets, attends):
                G = 2 * half + z
                H = G - 2

                def add(n):
                    i, c = n // 4, n % 4
                    if c == 0:
                        t.wait_ge(s["kc"], 4 * G + (i + 1))
                    t.wait_ge(s["pn"], 16 * G + (n + 1))
                    for j in range(HC):
                        last = t.matmul(BK[32 * j:32 * j + 32, S * c:S * c + S], kv[:, i, HC * c + j, :],
                                        pn[:, n % 4, S * j:S * j + S], start=(z == 0 and n == 0),
                                        stop=(z == 1 and i == GT - 1), skip_group_check=True)
                    last.then_inc(s["bk"], 1)

                def scores(m):
                    if m == 0 and z == 0:
                        t.wait_ge(s["stk"], half)
                    if m >= 2:
                        t.wait_ge(s["mx"], 16 * H + (m - 1))
                    t.matmul(SC(m), qs[:, z, m % 4, P * (m // 4):P * (m // 4) + P],
                             kst[:, m % 4, :, :].rearrange("p j s -> p (j s)"),
                             start=True, stop=True).then_inc(s["sc"], 1)

                def outputs(i):
                    bank = (TPB, NV)[i % 2]
                    if i == 0:
                        t.wait_ge(s["nc"], 4 * H + 4)
                    if i >= 2:
                        t.wait_ge(s["on"], 4 * H + (i - 1))
                    for c in range(NC):
                        last = t.transpose(bank[:, P * c:P * c + P], nT[:, c, P * i:P * i + P], ident[:])
                    last.then_inc(s["ot"], 1)

                def values(c):
                    t.wait_ge(s["e2"], 16 * H + (4 * c + 4))
                    if c == 0:
                        t.wait_ge(s["x"], H + 1)
                    else:
                        t.wait_ge(s["nc"], 4 * H + c)
                    for j in range(HC):
                        last = t.matmul(NV[32 * j:32 * j + 32, :], bv[:, HC * c + j, :], e2[:, c % 2, j, :],
                                        start=True, stop=True)
                    last.then_inc(s["pv"], 1)

                for n in range(16):
                    if attends and z == 0 and n == 0:
                        t.wait_ge(s["bt"], half)
                        for k in range(NC):
                            last = t.transpose(TPB[:, P * k:P * k + P], bT[:, P * k:P * k + P], ident[:])
                        last.then_inc(s["bvt"], 1)
                    if attends:
                        for m in spread(n, *A2)[:2]:
                            scores(m)
                    if n < 4 and (attends and (buckets or z == 0) or z == 1 and buckets):
                        queries(G - 1, 1 - z, n)
                    if buckets:
                        logits(G, z, n + 1)
                        if n == 1 and z == 0 and attends:
                            t.wait_ge(s["bv"], half)
                        if 1 <= n <= GT:
                            keys(G, z, n - 1)
                        if n >= LAG:
                            add(n - LAG)
                        if n == 4:
                            transpose_x(G + 1)
                        if 7 <= n < 11:
                            planes(G + 1, 1 - z, n - 7)
                    if attends:
                        for m in spread(n, *A2)[2:]:
                            scores(m)
                        for m in spread(n, *A3):
                            k, j = m // 4, m % 4
                            if j == 0:
                                if k == 0:
                                    if buckets:
                                        t.wait_ge(s["kc"], 4 * G + 4)
                                    t.wait_ge(s["nmp"], H + 1)
                                    t.wait_ge(s["mx"], 16 * H + 16)
                                    turn_max(t, k)
                                t.wait_ge(s["qf"], 4 * H + (k + 1))
                                if k < NC - 1:
                                    turn_max(t, k + 1)
                            if m >= 2:
                                t.wait_ge(s["e2"], 16 * H + (m - 1))
                            t.matmul(SC(m), kst[:, k, j, :], qs[:, z, k, :], start=True, stop=True).then_inc(s["ss"], 1)
                            if m % 4 == 1 and m > 4:
                                values(m // 4 - 1)
                        if n == A3[1]:
                            values(NC - 1)
                        if n in range(OUT, OUT + GT):
                            outputs(n - OUT)
                if attends:
                    outputs(3)
                if buckets:
                    for n in range(16 - LAG, 16):
                        add(n)
                if attends:
                    t.wait_ge(s["on"], 4 * H + 4)
                    for i in range(GT):
                        last = t.transpose(TPB[:, P * i:P * i + P], on[:, i, :], ident[:])
                    last.then_inc(s["ht"], 1)
                    t.wait_ge(s["oc"], H + 1)
                    for i in range(GT):
                        last = t.matmul(NV[:, P * i:P * i + P], oT[:, P * i:P * i + P], wo[:],
                                        start=True, stop=True)
                    last.then_inc(s["y"], 1)

            def turn_max(t, c):
                for i in range(GT):
                    last = t.transpose(TPB[:, P * i:P * i + P],
                                       nmp[:, i, HC * c:HC * c + HC, :].rearrange("p j k -> p (j k)"), ident[:])
                last.then_inc(s["nmt"], 1)

            t.wait_ge(s_x0, 32)
            transpose_x(0)
            t.wait_ge(s_m1, 3)
            t.wait_ge(s_w, 16 * NW)
            t.matmul(LG(0), wk, plane, start=True, stop=True).then_inc(s_m1, 1)
            t.wait_ge(s_wc, WC)
            for c in range(NC):
                planes(0, 0, c)
            logits(0, 0, 0)
            pipeline(t, step)



def ffn(nc, A, mk, ticks, tag, x, ident, W, rwH, rwL, rbias, sel, PS):
    ctx = ExitStack()
    with ctx:
        sb0, sem = mk(ctx)

        def sb(n, shape, d):
            return sb0(tag + n, shape, d)

        identb = sb("identb", [P, P], BF16)
        st, mv = sb("st", [P, GT, 6], F32), sb("mv", [P, GT, 2], F32)
        half_neg, rstd, var_e = (sb(n, [P, GT], F32) for n in ("hn", "rstd", "vare"))
        xn = sb("xn", [P, GT, P], F32)
        xH, xL = sb("xH", [P, 2, GN], F32R), sb("xL", [P, 2, GN], F32R)
        wT = sb("wT", [96, 2, GN], BF16)
        lg, near0, lgs, sil, rec, sc, wgt, w, r1, r2 = (
            sb(n, [P, GT, EXPERTS], F32) for n in "lg near0 lgs sil rec sc wgt w r1 r2".split())
        top8 = sb("top8", [P, GT, NGROUP, 8], F32)
        gsum = sb("gsum", [P, GT, 10], F32)
        g8, e8 = sb("g8", [P, GT, 8], F32), sb("e8", [P, GT, 8], F32)
        gsel = sb("gsel", [P, GT, 10], F32)
        gmask = sb("gmask", [P, GT, NGROUP], F32)
        sfc = sb("sfc", [P, GT, EXPERTS], F32)
        cand = sb("cand", [P, GT, EXPERTS + 4], F32)
        esel = sb("esel", [P, GT, EXPERTS + 4], F32)
        den, rden = sb("den", [P, GT], F32), sb("rden", [P, GT], F32)
        w3 = sb("w3", [P, GT, 96], BF16)
        sg, at = (sb(n, [P, 2, GN], F32) for n in ("sg", "at"))
        bt = sb("bt", [P, 3, GN], F32)
        bH, bL = sb("bH", [P, 3, GN], F32R), sb("bL", [P, 3, GN], F32R)
        yT = sb("yT", [P, GN], F32)
        names = ("stat rstd xn xt xh xl rt lgs sil w3 wt wtc G U WB sg a b bh bl dn yt yo vc init iv").split()
        s = {n: sem(tag + "_" + n) for n in names}
        s.update(ticks)
        NU = UNITS + 1
        TPB, Y = PS[:, 0, :], PS[:, 7, :]
        BANKS = {"G": (2, 3), "U": (4, 5), "WB": (1, 6)}
        block = ctx.enter_context(nc.Block())

        def tokens(g):
            return x[:, ds(g * GT, GT), :]

        def bank(name, u, z):
            return PS[:, BANKS[name][(u + z) % 2], :]

        def buf(u):
            return u % NU % 3

        def reuse(eng, name, k, u):
            if not isinstance(k, int) or k >= 3:
                eng.wait_ge(s[name], k - 2 + (u % NU < 2))

        def run_groups(eng, main):
            main(0, False, True, 0)
            with eng.Fori(0, NG // 2 - 1) as i:
                main(2 * i + 1, True, True, 1)
                main(2 * i + 2, True, True, 0)
            main(NG - 1, True, False, 1)

        @block.gpsimd
        def _(p):
            p.memset(half_neg[:], -0.5).then_inc(s["init"], 1)
            p.wait_ge(s["init"], 1)

            def prologue(g):
                p.wait_ge(s["stat"], g + 1)
                apart(p, s["tickp"])
                p.tensor_scalar(var_e[:], mv[:, :, 1], LN_EPS, None, ALU.add).then_inc(s["init"], 1)
                p.wait_ge(s["init"], g + 2)
                p.tensor_tensor(rstd[:], var_e[:], half_neg[:], ALU.pow).then_inc(s["rstd"], 1)

            def low(g, u, z):
                k, n = g * NU + u, buf(u)
                p.wait_ge(s["bh"], k + 1)
                reuse(p, "dn", k, u)
                p.tensor_tensor(bL[:, n, :], bt[:, n, :], bH[:, n, :].bitcast(F32),
                                ALU.subtract).then_inc(s["bl"], 1)

            def main(g, before, more, z):
                for u in range(NU):
                    if more and u == 1:
                        prologue(g + 1)
                    low(g, u, z)

            prologue(0)
            run_groups(p, main)

        @block.scalar
        def _(a):
            def copy_x(g, z):
                a.wait_ge(s["xt"], g + 1)
                a.activation(xH[:, z, :], TPB, ACT.Copy).then_inc(s["xh"], 1)

            def silu_route(g):
                a.wait_ge(s["lgs"], g + 1)
                a.activation(sil[:], lgs[:], ACT.Silu).then_inc(s["sil"], 1)

            def copy_w(g, z):
                a.wait_ge(s["wt"], g + 1)
                a.activation(wT[:, z, :], TPB[0:96, :].bitcast(BF16)[:, 0:GN], ACT.Copy).then_inc(s["wtc"], 1)

            def silu(g, u, z):
                k = g * NU + u
                a.wait_ge(s["G"], k + 1)
                if not isinstance(k, int) or k >= 2:
                    a.wait_ge(s["a"], k - 1)
                a.activation(sg[:, (u + z) % 2, :], bank("G", u, z), ACT.Silu).then_inc(s["sg"], 1)

            def high(g, u, z):
                k, n = g * NU + u, buf(u)
                a.wait_ge(s["b"], k + 1)
                reuse(a, "dn", k, u)
                a.activation(bH[:, n, :], bt[:, n, :], ACT.Copy).then_inc(s["bh"], 1)

            def copy_y(g):
                a.wait_ge(s["dn"], g * NU + NU)
                a.activation(yT[:], Y, ACT.Copy).then_inc(s["yt"], 1)

            def main(g, before, more, z):
                for u in range(1, NU + more):
                    silu(g, u, z)
                    if more and u == NU:
                        copy_w(g + 1, 1 - z)
                    if before and u == LAG:
                        copy_y(g - 1)
                    if before or u >= 2:
                        high(g, u - 2, z)
                    if more and u == X_AT + 1:
                        copy_x(g + 1, 1 - z)
                    if more and u == ROUTE_AT + 1:
                        silu_route(g + 1)
                if not more:
                    for u in range(NU - 2, NU):
                        high(g, u, z)
                    copy_y(g)

            copy_x(0, 0)
            silu_route(0)
            copy_w(0, 0)
            silu(0, 0, 0)
            run_groups(a, main)

        @block.vector
        def _(v):
            c = Chain(v, s["iv"])
            c.step(v.tensor_copy(identb[:], ident[:]))
            c.step(v.memset(gsum[:], LOWEST))
            c.step(v.memset(cand[:], LOWEST))
            PER = 27

            def parts(g, z):
                c = Chain(v, s["vc"], PER, g)
                xg = tokens(g)

                def stats():
                    for i in range(GT):
                        last = v.bn_stats(st[:, i, :], x[:, ds(g * GT + i, 1), :].rearrange("p o f -> p (o f)"))
                    c.step(last)
                    apart(v, s["tick"])
                    for i in range(GT):
                        last = v.bn_aggr(mv[:, i, :], st[:, i, :])
                    last.then_inc(s["stat"], 1)

                def norm():
                    v.wait_ge(s["rstd"], g + 1)
                    for i in range(GT):
                        last = v.tensor_scalar(xn[:, i, :], x[:, ds(g * GT + i, 1), :].rearrange("p o f -> p (o f)"),
                                               mv[:, i, 0:1], rstd[:, i:i + 1], ALU.subtract, ALU.mult)
                    last.then_inc(s["xn"], 1)

                def low_x():
                    v.wait_ge(s["xh"], g + 1)
                    v.tensor_tensor(xL[:, z, :], TPB, xH[:, z, :].bitcast(F32), ALU.subtract).then_inc(s["xl"], 1)

                def logits():
                    v.wait_ge(s["rt"], g + 1)
                    c.step(v.tensor_copy(lg[:], TPB[:, 0:GT * EXPERTS].rearrange("p (i e) -> p i e", i=GT)))
                    c.step(v.tensor_tensor(near0[:], lg[:], lg[:], ALU.mult))
                    c.step(v.tensor_scalar(near0[:], near0[:], 1e-24, 4e-12, ALU.is_lt, ALU.mult))
                    v.tensor_tensor(lgs[:], near0[:], lg[:], ALU.add).then_inc(s["lgs"], 1)

                def recip():
                    v.wait_ge(s["lgs"], g + 1)
                    c.step(v.reciprocal(rec[:], lgs[:]))

                def scores():
                    v.wait_ge(s["sil"], g + 1)
                    c.step(v.tensor_tensor(sc[:], sil[:], rec[:], ALU.mult))
                    c.step(v.tensor_tensor(sfc[:], sc[:], rbias[:].unsqueeze(1).to_broadcast([P, GT, EXPERTS]),
                                           ALU.add))

                def best(tiles):
                    for i in tiles:
                        for q in range(NGROUP):
                            last = v.max(top8[:, i, q, :], sfc[:, i, GE * q:GE * q + GE])
                    return last

                def best_first():
                    best(range(0, GT // 2))

                def best_second():
                    c.step(best(range(GT // 2, GT)))

                def groups():
                    c.step(v.tensor_tensor(gsum[:, :, 0:NGROUP], top8[:, :, :, 0], top8[:, :, :, 1], ALU.add))
                    apart(v, s["tick"])
                    for i in range(GT):
                        last = v.max(g8[:, i, :], gsum[:, i, :])
                    c.step(last)
                    c.step(v.memset(g8[:, :, 2:8], LOWEST))

                def group_mask():
                    apart(v, s["tick"])
                    for i in range(GT):
                        last = v.match_replace(gsel[:, i, :], g8[:, i, :], gsum[:, i, :], -LOWEST)
                    c.step(last)
                    c.step(v.tensor_scalar(gmask[:], gsel[:, :, 0:NGROUP], -LOWEST, None, ALU.is_equal))

                def experts():
                    cv = cand[:, :, 0:EXPERTS].rearrange("p i (q e) -> p i q e", q=NGROUP)
                    for i in range(GT):
                        last = v.tensor_tensor(cv[:, i], sfc[:, i, :].rearrange("p (q e) -> p q e", q=NGROUP),
                                               gmask[:, i, :].unsqueeze(2).to_broadcast([P, NGROUP, GE]), ALU.mult)
                    c.step(last)
                    c.step(v.tensor_scalar(cand[:, :, 0:EXPERTS], cand[:, :, 0:EXPERTS], 0.0, None, ALU.add))

                def best_experts():
                    apart(v, s["tick"])
                    for i in range(GT):
                        last = v.max(e8[:, i, :], cand[:, i, :])
                    c.step(last)
                    c.step(v.memset(e8[:, :, TOPK:8], LOWEST))

                def chosen():
                    apart(v, s["tick"])
                    for i in range(GT):
                        last = v.match_replace(esel[:, i, :], e8[:, i, :], cand[:, i, :], -LOWEST)
                    c.step(last)

                def weights():
                    c.step(v.scalar_tensor_tensor(wgt[:], esel[:, :, 0:EXPERTS], -LOWEST, sc[:], ALU.is_equal,
                                                  ALU.mult))
                    c.step(v.tensor_reduce(den[:], wgt[:], AX.X, ALU.add))
                    c.step(v.tensor_scalar(den[:], den[:], 1e-20, None, ALU.add))
                    c.step(v.reciprocal(rden[:], den[:]))
                    c.step(v.scalar_tensor_tensor(w[:], rden[:].unsqueeze(2).to_broadcast([P, GT, EXPERTS]),
                                                  ROUTE_SCALE, wgt[:], ALU.mult, ALU.mult))

                def thirds():
                    c.step(v.tensor_copy(w3[:, :, 0:32], w[:]))
                    c.step(v.tensor_tensor(r1[:], w[:], w3[:, :, 0:32], ALU.subtract))
                    c.step(v.tensor_copy(w3[:, :, 32:64], r1[:]))
                    c.step(v.tensor_tensor(r2[:], r1[:], w3[:, :, 32:64], ALU.subtract))
                    v.tensor_copy(w3[:, :, 64:96], r2[:]).then_inc(s["w3"], 1)
                    assert c.n == PER, c.n

                return [stats, norm, low_x, logits, recip, scores, best_first, best_second, groups, group_mask, experts,
                        best_experts, chosen, weights, thirds]

            def hidden(g, u, z):
                k, n = g * NU + u, (u + z) % 2
                v.wait_ge(s["U"], k + 1)
                v.wait_ge(s["sg"], k + 1)
                if not isinstance(k, int) or k >= 2:
                    v.wait_ge(s["b"], k - 1)
                shared = u == UNITS
                if shared:
                    reuse(v, "bl", k, u)
                v.tensor_tensor(bt[:, buf(u), :] if shared else at[:, n, :], sg[:, n, :], bank("U", u, z),
                                ALU.mult).then_inc(s["a"], 1)

            def add_y(g):
                v.wait_ge(s["yo"], g + 1)
                xg = tokens(g).rearrange("p i f -> p (i f)")
                v.tensor_tensor(xg, TPB, xg, ALU.add).then_inc(s["iv"], 1)
                v.wait_ge(s["iv"], g + 4)

            def weigh(g, u, z):
                k, n = g * NU + u, (u + z) % 2
                v.wait_ge(s["a"], k + 1)
                if u == UNITS:
                    v.wait_ge(s["b"], k)
                    v.sem_inc(s["b"], 1)
                else:
                    v.wait_ge(s["WB"], g * UNITS + (u + (u < UNITS)))
                    reuse(v, "bl", k, u)
                    v.tensor_tensor(bt[:, buf(u), :], at[:, n, :], bank("WB", u, z), ALU.mult).then_inc(s["b"], 1)

            def main(g, before, more, z):
                after = {}
                if more:
                    for u, part in zip(PART_AT, parts(g + 1, 1 - z)):
                        after.setdefault(u, []).append(part)
                for u in range(1, NU + more):
                    hidden(g, u, z)
                    if u - 1 < UNITS:
                        weigh(g, u - 1, z)
                    if u == UNITS:
                        weigh(g, u, z)
                    if before and u == Y_AT + 2:
                        add_y(g - 1)
                    for part in after.get(u, ()):
                        part()
                if not more:
                    add_y(g)

            for part in parts(0, 0):
                part()
            hidden(0, 0, 0)
            run_groups(v, main)

        @block.tensor
        def _(t):
            def transpose_x(g):
                t.wait_ge(s["xn"], g + 1)
                for i in range(GT):
                    last = t.transpose(TPB[:, P * i:P * i + P], xn[:, i, :], ident[:])
                last.then_inc(s["xt"], 1)

            def route(g, z):
                t.wait_ge(s["xl"], g + 1)
                for i in range(GT):
                    tok = slice(P * i, P * i + P)
                    last = three_pass(t, TPB[:, EXPERTS * i:EXPERTS * i + EXPERTS], (xH[:, z, tok], xL[:, z, tok]),
                                      (rwH[:], rwL[:]))
                last.then_inc(s["rt"], 1)

            def transpose_w(g):
                t.wait_ge(s["w3"], g + 1)
                apart(t, s["tickt"])
                for i in range(GT):
                    last = t.transpose(TPB[0:96, :].bitcast(BF16)[:, P * i:P * i + P], w3[:, i, :], identb[:])
                last.then_inc(s["wt"], 1)

            def products(g, u, z):
                k, n, zu = g * NU + u, u % NU, (z + u // NU) % 2
                later = not isinstance(k, int) or k >= 2
                xs = (xH[:, zu, :], xL[:, zu, :])
                if later:
                    t.wait_ge(s["sg"], k - 1)
                three_pass(t, bank("G", u, z), (W["gH"][:, n, :], W["gL"][:, n, :]), xs).then_inc(s["G"], 1)
                if later:
                    t.wait_ge(s["a"], k - 1)
                three_pass(t, bank("U", u, z), (W["uH"][:, n, :], W["uL"][:, n, :]), xs).then_inc(s["U"], 1)

            def weight(g, u, z):
                k, n, zu = g * NU + u, u % NU, (z + u // NU) % 2
                if n == UNITS:
                    return
                if n == 0:
                    t.wait_ge(s["wtc"], g + (1 + u // NU))
                if not isinstance(k, int) or k >= 2:
                    t.wait_ge(s["b"], k - 1)
                t.matmul(bank("WB", u, z), sel[:, n, :], wT[:, zu, :], start=True, stop=True).then_inc(s["WB"], 1)

            def main(g, before, more, z):
                def down(u):
                    k, n, w = g * NU + u, buf(u % NU), u % NU
                    t.wait_ge(s["bl"], k + 1)
                    if u == 0 and before:
                        t.wait_ge(s["yt"], g)
                    last = three_pass(t, Y, (W["dH"][:, w, :], W["dL"][:, w, :]), (bH[:, n, :], bL[:, n, :]),
                                      start=(w == 0), stop=(w == UNITS))
                    last.then_inc(s["dn"], 1)

                for u in range(1, NU + more):
                    if more or u + 1 < NU:
                        products(g, u + 1, z)
                    weight(g, u - 1, z)
                    if more and u == NU:
                        transpose_w(g + 1)
                    if before or u >= LAG:
                        down(u - LAG)
                    if more and u == X_AT:
                        transpose_x(g + 1)
                    if more and u == ROUTE_AT:
                        route(g + 1, 1 - z)
                    if before and u == Y_AT:
                        if more:
                            t.wait_ge(s["lgs"], g + 2)
                        transpose_y(g - 1)
                if not more:
                    for u in range(NU - LAG, NU):
                        down(u)
                    transpose_y(g)

            def transpose_y(g):
                t.wait_ge(s["yt"], g + 1)
                for i in range(GT):
                    last = t.transpose(TPB[:, P * i:P * i + P], yT[:, P * i:P * i + P], ident[:])
                last.then_inc(s["yo"], 1)

            transpose_x(0)
            route(0, 0)
            t.wait_ge(s["iv"], 3)
            transpose_w(0)
            for u in range(2):
                products(0, u, 0)
            run_groups(t, main)


LAG = 4
X_AT, ROUTE_AT, Y_AT = 4, 6, 9
PART_AT = (1, 3, 5, 7, 7, 8, 9, 10, 12, 12, 13, 13, 14, 14, 15)



def recon(nc, A, mk, ticks, x, ident, PS):
    ctx = ExitStack()
    with ctx:
        sb0, sem = mk(ctx)

        def sb(n, shape, d=F32):
            return sb0("r_" + n, shape, d)

        tk, tv, tq, tkT, tvT, tqT, dn, dT = (sb(n, [P, P]) for n in "tk tv tq tkT tvT tqT dn dT".split())
        w1T = sb("w1T", [P, RH])
        w2e = sb("w2e", [P, RH + 1])
        w2eT = sb("w2eT", [RH + 1, P])
        b1 = sb("b1", [RH, 1])
        st, mv = sb("st", [P, NI, 6]), sb("mv", [P, NI, 2])
        half_neg, rstd, var_e = (sb(n, [P, NI]) for n in ("hn", "rstd", "vare"))
        xn = sb("xn", [P, NI, P])
        xT = sb("xT", [P, NI * P])
        par = sb("par", [P, 2 * RH])
        hh = sb("hh", [RH + 1, RH])
        qpar = sb("qpar", [P, RH])
        N2 = NI * P
        v0, v1, vs, rv, cdf, ex, gp = (sb(n, [RH, N2]) for n in "v0 v1 vs rv cdf ex gp".split())
        hd = sb("hd", [96, N2])
        h2 = sb("h2", [RH + 1, N2])
        hdt = sb("hdt", [P, NI, 96])
        M = sb("M", [P, 96])
        gram = sb("gram", [RH + 1, RH + 1])
        names = "w wc stat rstd xn xt xT par parc pre vs ge v1 ex dh dp hdt hdc m mc upd updc w2t w2c q qc pq h2 o x vc ac mem g1".split()
        s = {n: sem("r_" + n) for n in names}
        s.update(ticks)
        TPB, PRE, DH, HDT, MM, SM, OUT = (PS[:, n, :] for n in (0, 1, 2, 3, 4, 5, 7))
        C = 2.0 / (NI * P * P)
        SQ = 0.3989422804014327
        block = ctx.enter_context(nc.Block())
        NGB = NI // GT

        @block.sync
        def _(sp):
            for dst, n in ((tk, "tk"), (tv, "tv"), (tq, "tq"), (tkT, "tkT"), (tvT, "tvT"), (tqT, "tqT"), (w1T, "w1T")):
                sp.dma_start(dst[:], A[n]).then_inc(s["w"], 16)
            sp.dma_start(w2e[:, 0:RH], A["w2"]).then_inc(s["w"], 16)
            sp.dma_start(w2e[:, RH:RH + 1], A["b2"].unsqueeze(1)).then_inc(s["w"], 16)
            sp.dma_start(b1[:], A["b1"].unsqueeze(1)).then_inc(s["w"], 16)

        @block.gpsimd
        def _(p):
            p.memset(half_neg[:], -0.5)
            p.memset(hd[0:64, :], 0.0).then_inc(s["mem"], 1)
            p.wait_ge(s["mem"], 1)
            p.memset(hd[32:33, :], 1.0)
            p.memset(h2[32:33, :], 1.0).then_inc(s["mem"], 1)
            p.wait_ge(s["mem"], 2)
            with p.Fori(0, NB) as b:
                p.wait_ge(s["stat"], b + 1)
                apart(p, s["tickp"])
                p.tensor_scalar(var_e[:], mv[:, :, 1], LN_EPS, None, ALU.add).then_inc(s["g1"], 1)
                p.wait_ge(s["g1"], b + 1)
                p.tensor_tensor(rstd[:], var_e[:], half_neg[:], ALU.pow).then_inc(s["rstd"], 1)

        @block.scalar
        def _(a):
            def step(b):
                for k in range(NGB):
                    a.wait_ge(s["xt"], b * NGB + (k + 1))
                    a.activation(xT[:, GN * k:GN * k + GN], TPB, ACT.Copy).then_inc(s["xT"], 1)
                a.wait_ge(s["par"], b + 1)
                a.activation(par[:], SM[:, 0:2 * RH], ACT.Copy).then_inc(s["ac"], 1)
                a.activation(hh[:], SM[0:RH + 1, 2 * RH:3 * RH], ACT.Copy).then_inc(s["parc"], 1)
                a.wait_ge(s["vs"], b + 1)
                a.activation(hd[0:RH, :], vs[:], ACT.Gelu).then_inc(s["ge"], 1)
                a.activation(ex[:], v1[:], ACT.Exp, scale=-0.5).then_inc(s["ex"], 1)
                for k in range(NGB):
                    a.wait_ge(s["hdt"], b * NGB + (k + 1))
                    a.activation(hdt[:, GT * k:GT * k + GT, :], HDT[:, 0:GT * 96].rearrange("p (i c) -> p i c", i=GT),
                                 ACT.Copy).then_inc(s["hdc"], 1)
                a.wait_ge(s["m"], b + 1)
                a.activation(M[:], MM[:, 0:96], ACT.Copy).then_inc(s["ac"], 1)
                a.activation(gram[:], SM[0:RH + 1, 96:96 + RH + 1], ACT.Copy).then_inc(s["mc"], 1)
                a.wait_ge(s["w2t"], b + 2)
                a.activation(w2eT[:], DH[0:RH + 1, 0:P], ACT.Copy).then_inc(s["w2c"], 1)
                a.wait_ge(s["q"], b + 1)
                a.activation(qpar[:], SM[:, 160:160 + RH], ACT.Copy).then_inc(s["qc"], 1)
                for k in range(NGB):
                    a.wait_ge(s["pq"], b * NGB + (k + 1))
                    a.activation(h2[0:RH, GN * k:GN * k + GN], (PRE if k == 0 else DH)[0:RH, :], ACT.Gelu,
                                 bias=b1[:, 0:1]).then_inc(s["h2"], 1)

            a.wait_ge(s["w2t"], 1)
            a.activation(w2eT[:], DH[0:RH + 1, 0:P], ACT.Copy).then_inc(s["w2c"], 1)
            a.wait_ge(s["w2c"], 1)
            with a.Fori(0, NB) as b:
                step(b)

        @block.vector
        def _(v):
            PER = 1 + 2 + 1 + 2 + 2 + 3
            def step(b):
                c = Chain(v, s["vc"], PER, b)
                for i in range(NI):
                    last = v.bn_stats(st[:, i, :], x[:, ds(b * NI + i, 1), :].rearrange("p o f -> p (o f)"))
                c.step(last)
                apart(v, s["tick"])
                for i in range(NI):
                    last = v.bn_aggr(mv[:, i, :], st[:, i, :])
                last.then_inc(s["stat"], 1)
                v.wait_ge(s["rstd"], b + 1)
                for i in range(NI):
                    last = v.tensor_scalar(xn[:, i, :], x[:, ds(b * NI + i, 1), :].rearrange("p o f -> p (o f)"),
                                           mv[:, i, 0:1], rstd[:, i:i + 1], ALU.subtract, ALU.mult)
                last.then_inc(s["xn"], 1)
                v.wait_ge(s["pre"], b + 1)
                for k, bank in enumerate((PRE, DH)):
                    c.step(v.tensor_scalar(v0[:, GN * k:GN * k + GN], bank[0:RH, :], b1[:, 0:1], None, ALU.add))
                v.tensor_tensor(v1[:], v0[:], v0[:], ALU.mult).then_inc(s["v1"], 1)
                v.wait_ge(s["v1"], b + 1)
                c.step(v.tensor_scalar(rv[:], v1[:], 1e-24, 4e-12, ALU.is_lt, ALU.mult))
                v.tensor_tensor(vs[:], v0[:], rv[:], ALU.add).then_inc(s["vs"], 1)
                v.wait_ge(s["vs"], b + 1)
                c.step(v.reciprocal(rv[:], vs[:]))
                v.wait_ge(s["ge"], b + 1)
                c.step(v.tensor_tensor(cdf[:], hd[0:RH, :], rv[:], ALU.mult))
                v.wait_ge(s["ex"], b + 1)
                c.step(v.scalar_tensor_tensor(gp[:], v0[:], SQ, ex[:], ALU.mult, ALU.mult))
                c.step(v.tensor_tensor(gp[:], gp[:], cdf[:], ALU.add))
                v.wait_ge(s["dh"], b + 1)
                for k, bank in enumerate((PRE, DH)):
                    last = v.scalar_tensor_tensor(hd[64:96, GN * k:GN * k + GN], bank[0:RH, :], C,
                                                  gp[:, GN * k:GN * k + GN], ALU.mult, ALU.mult)
                last.then_inc(s["dp"], 1)
                v.wait_ge(s["upd"], b + 1)
                c.step(v.scalar_tensor_tensor(w2e[:], MM[:, 96:96 + RH + 1], -LR * C, w2e[:], ALU.mult, ALU.add))
                c.step(v.scalar_tensor_tensor(w1T[:], MM[:, 160:160 + RH], -LR, w1T[:], ALU.mult, ALU.add))
                c.step(v.scalar_tensor_tensor(b1[:], MM[0:RH, 200:201], -LR, b1[:], ALU.mult, ALU.add))
                v.sem_inc(s["updc"], 1)
                for k in range(NGB):
                    v.wait_ge(s["o"], b * NGB + (k + 1))
                    xg = x[:, ds(b * NI + GT * k, GT), :].rearrange("p i f -> p (i f)")
                    v.tensor_tensor(xg, OUT if k == 0 else TPB, xg, ALU.add).then_inc(s["x"], 1)
                v.wait_ge(s["x"], b * NGB + NGB)
                c.close()

            v.wait_ge(s["w"], 160)
            v.tensor_tensor(dn[:], tk[:], tv[:], ALU.subtract)
            v.tensor_tensor(dT[:], tkT[:], tvT[:], ALU.subtract).then_inc(s["wc"], 1)
            with v.Fori(0, NB) as b:
                step(b)

        @block.tensor
        def _(t):
            def turn_w2(n):
                t.transpose(DH[0:RH + 1, 0:P], w2e[:], ident[:]).then_inc(s["w2t"], 1)

            def step(b):
                t.wait_ge(s["xn"], b + 1)
                for k in range(NGB):
                    if k:
                        t.wait_ge(s["xT"], b * NGB + k)
                    for i in range(GT):
                        last = t.transpose(TPB[:, P * i:P * i + P], xn[:, GT * k + i, :], ident[:])
                    last.then_inc(s["xt"], 1)
                t.matmul(SM[:, 0:RH], tk[:], w1T[:], start=True, stop=True)
                t.matmul(SM[:, RH:2 * RH], dn[:], w2e[:, 0:RH], start=True, stop=True)
                t.matmul(SM[0:RH + 1, 2 * RH:3 * RH], w2e[:], w2e[:, 0:RH], start=True, stop=True).then_inc(s["par"], 1)
                t.wait_ge(s["parc"], b + 1)
                t.wait_ge(s["xT"], b * NGB + NGB)
                for k, bank in enumerate((PRE, DH)):
                    last = t.matmul(bank[0:RH, :], par[:, 0:RH], xT[:, GN * k:GN * k + GN], start=True, stop=True)
                last.then_inc(s["pre"], 1)
                t.wait_ge(s["vs"], b + 1)
                t.wait_ge(s["ge"], b + 1)
                for k, bank in enumerate((PRE, DH)):
                    t.matmul(bank[0:RH, :], par[:, RH:2 * RH], xT[:, GN * k:GN * k + GN], start=True, stop=False)
                    last = t.matmul(bank[0:RH, :], hh[:], hd[0:RH + 1, GN * k:GN * k + GN], start=False, stop=True)
                last.then_inc(s["dh"], 1)
                t.wait_ge(s["dp"], b + 1)
                for k in range(NGB):
                    if k:
                        t.wait_ge(s["hdc"], b * NGB + k)
                    apart(t, s["tickt"])
                    for i in range(GT):
                        n = GT * k + i
                        last = t.transpose(HDT[:, 96 * i:96 * i + 96], hd[:, P * n:P * n + P], ident[0:96, 0:96])
                    last.then_inc(s["hdt"], 1)
                t.wait_ge(s["hdc"], b * NGB + NGB)
                for i in range(NI):
                    t.matmul(MM[:, 0:96], xn[:, i, :], hdt[:, i, :], start=(i == 0), stop=(i == NI - 1))
                for i in range(NI):
                    last = t.matmul(SM[0:RH + 1, 96:96 + RH + 1], hdt[:, i, 0:RH + 1], hdt[:, i, 0:RH + 1],
                                    start=(i == 0), stop=(i == NI - 1))
                last.then_inc(s["m"], 1)
                t.wait_ge(s["mc"], b + 1)
                t.matmul(MM[:, 96:96 + RH + 1], dT[:], M[:, 0:RH + 1], start=True, stop=False)
                t.matmul(MM[:, 96:96 + RH + 1], w2eT[:], gram[:], start=False, stop=True)
                t.matmul(MM[:, 160:160 + RH], tkT[:], M[:, 64:96], start=True, stop=True)
                for i in range(NI):
                    last = t.matmul(MM[0:RH, 200:201], hdt[:, i, 64:96], hdt[:, i, RH:RH + 1],
                                    start=(i == 0), stop=(i == NI - 1))
                last.then_inc(s["upd"], 1)
                t.wait_ge(s["updc"], b + 1)
                apart(t, s["tickt"])
                turn_w2(b)
                t.matmul(SM[:, 160:160 + RH], tq[:], w1T[:], start=True, stop=True).then_inc(s["q"], 1)
                t.wait_ge(s["qc"], b + 1)
                t.wait_ge(s["w2c"], b + 2)
                for k, bank in enumerate((PRE, DH)):
                    t.matmul(bank[0:RH, :], qpar[:], xT[:, GN * k:GN * k + GN], start=True, stop=True)\
                        .then_inc(s["pq"], 1)
                for k in range(NGB):
                    t.wait_ge(s["h2"], b * NGB + (k + 1))
                    for i in range(GT):
                        n = GT * k + i
                        o = (OUT if k == 0 else TPB)[:, P * i:P * i + P]
                        t.matmul(o, xT[:, P * n:P * n + P], tqT[:], start=True, stop=False)
                        last = t.matmul(o, h2[:, P * n:P * n + P], w2eT[:], start=False, stop=True)
                    last.then_inc(s["o"], 1)
                t.wait_ge(s["x"], b * NGB + NGB)

            t.wait_ge(s["w"], 160)
            t.wait_ge(s["mem"], 2)
            turn_w2(-1)
            t.wait_ge(s["wc"], 1)
            t.wait_ge(s["w2c"], 1)
            with t.Fori(0, NB) as b:
                step(b)



def kernel(**inputs):
    import numpy as _np
    import concourse.bacc as _bacc
    from concourse import mybir as _mybir
    from concourse.bass_utils import run_bass_kernel_spmd as _run

    nc = _bacc.Bacc("TRN2", target_bir_lowering=False, num_devices=1)
    arrays = lay_out(inputs)
    args = {n: nc.dram_tensor("in_" + n, a.shape, _mybir.dt.from_np(a.dtype), kind="ExternalInput").ap()
            for n, a in arrays.items()}
    out = nc.dram_tensor("out_0", (NB, NI * P, P), _mybir.dt.float32, kind="ExternalOutput").ap()
    build(nc, args, out)
    r = _run(nc, [{"in_" + n: a for n, a in arrays.items()}], core_ids=[0])
    return r.results[0]["out_0"]


def lay_out(inputs):
    a, r, f = "L0_attn_a_", "L0_attn_b_", "L0_ffn_"
    c = np.ascontiguousarray

    def units(w, shared):
        return c(np.concatenate([w.reshape(UNITS, P, P), shared[None]]).transpose(2, 0, 1))

    I = {n: np.asarray(v) for n, v in inputs.items()}
    down = I[f + "down_w"].reshape(UNITS, 2, P, INNER).transpose(1, 3, 0, 2).reshape(P, UNITS, P)
    lo_q, lo_k = np.zeros((2, P), np.float32)
    for j in range(HC):
        lo_q[32 * j + 8:32 * j + 16] = -1
        lo_k[32 * j + 16:32 * j + 24] = -1
    sel = np.zeros((3, EXPERTS, UNITS, 2, INNER), np.float32)
    for e in range(EXPERTS):
        sel[:, e, e // 2, e % 2] = 1
    return {
        "x": c(I[a + "x"]),
        "wqT": c(I[a + "Wq"].T), "wkT": c(I[a + "Wk"].T), "wvT": c(I[a + "Wv"].T), "wk": c(I[a + "Wk"]),
        "woT": c(I[a + "Wo"].T), "bo": c(I[a + "bo"]), "planes": c(I[a + "planes_T"]),
        "protos": c(I[a + "protos_T"]), "temp": c(I[a + "logit_temp"].reshape(1)),
        "rwT": c(I[f + "router_weight"].T), "rbias": c(I[f + "router_bias"]),
        "w_g": units(I[f + "gate_w"], I[f + "shared_gate_w"]),
        "w_u": units(I[f + "up_w"], I[f + "shared_up_w"]),
        "w_d": c(np.concatenate([down, I[f + "shared_down_w"].T[:, None]], axis=1)),
        "tk": c(I[r + "t_k"]), "tv": c(I[r + "t_v"]), "tq": c(I[r + "t_q"]), "tkT": c(I[r + "t_k"].T),
        "tvT": c(I[r + "t_v"].T), "tqT": c(I[r + "t_q"].T), "w1T": c(I[r + "W1"].T), "w2": c(I[r + "W2"]),
        "b1": c(I[r + "b1"]), "b2": c(I[r + "b2"]),
        "ident": np.eye(P, dtype=np.float32), "msk": c(np.stack([lo_q, lo_k], axis=1)),
        "sel": sel.reshape(96, UNITS, P),
    }
```

```python
from contextlib import ExitStack

import numpy as np
import concourse.bass as bass
from concourse import mybir

F32 = mybir.dt.float32
F32R = mybir.dt.float32r
BF16 = mybir.dt.bfloat16
ALU = mybir.AluOpType
ACT = mybir.ActivationFunctionType
AX = mybir.AxisListType
ds = bass.ds

P = 128
NB = 4
NI = 8
GT = 4
GN = GT * P
NG = NB * NI // GT
HEADS, HD = 16, 8
TABLES, BITS, CORNERS = 8, 4, 16
NP = TABLES * BITS
S = TABLES * CORNERS
HC = 4
NC = HEADS // HC
EXPERTS, INNER, TOPK, NGROUP = 32, 64, 4, 4
GE = EXPERTS // NGROUP
UNITS = EXPERTS * INNER // P
ROUTE_SCALE = 2.5
LN_EPS = 1e-5
LR = 1e-3
RH = 32
LOWEST = -3.0e38
SMALL = 30.0


class Chain:

    def __init__(self, eng, sem, per_turn=0, turn=0):
        self.eng, self.sem, self.base, self.n, self.per_turn = eng, sem, turn * per_turn, 0, per_turn

    def step(self, ins):
        self.n += 1
        ins.then_inc(self.sem, 1)
        self.eng.wait_ge(self.sem, self.base + self.n)

    def close(self):
        assert self.n == self.per_turn, (self.n, self.per_turn)


def apart(eng, tick):
    eng.sem_inc(tick, 1)


def split_rows(v, c, hi, lo, src):
    c.step(v.tensor_copy(hi, src))
    c.step(v.tensor_tensor(lo, src, hi.bitcast(F32), ALU.subtract))


def three_pass(t, out, lhs, rhs, start=True, stop=True):
    t.matmul(out, lhs[0], rhs[0], start=start, stop=False, skip_group_check=True)
    t.matmul(out, lhs[1], rhs[0], start=False, stop=False, skip_group_check=True)
    return t.matmul(out, lhs[0], rhs[1], start=False, stop=stop, skip_group_check=True)


def build(nc, A, out):
    top = ExitStack()
    with top:
        def mk(ctx):
            return (lambda n, s, d: ctx.enter_context(nc.sbuf_tensor(n, s, d)),
                    lambda n: ctx.enter_context(nc.semaphore(n)))
        sb, sem = mk(top)
        PS = top.enter_context(nc.psum_tensor("PS", [P, 8, 512], F32))
        x = sb("x", [P, NB * NI + GT, P], F32)
        ident = sb("ident", [P, P], F32)
        raw = {n: sb("raw_" + n, [P, UNITS + 1, P], F32) for n in "gud"}
        rwH, rwL = sb("rwH", [P, EXPERTS], F32R), sb("rwL", [P, EXPERTS], F32R)
        rbias = sb("rbias", [P, EXPERTS], F32)
        s_done = sem("s_done")
        ticks = {n: sem(n) for n in ("tick", "tickp", "tickt")}

        attention(nc, A, mk, x, ident, PS, raw, rwH, rwL, rbias, ticks)
        W = {n: sb(n, [P, UNITS + 1, P], F32R) for n in ("gH", "gL", "uH", "uL", "dH", "dL")}
        sel = sb("sel", [96, UNITS, P], BF16)
        ffn(nc, A, mk, ticks, "f1", x, ident, W, rwH, rwL, rbias, sel, PS, raw=raw)
        recon(nc, A, mk, ticks, x, ident, PS)
        ffn(nc, A, mk, ticks, "f2", x, ident, W, rwH, rwL, rbias, sel, PS, out=out, s_done=s_done)



def attention(nc, A, mk, x, ident, PS, raw, rwH, rwL, rbias, ticks):
    ctx = ExitStack()
    with ctx:
        sb0, sem = mk(ctx)

        def sb(n, shape, d=F32):
            return sb0("a_" + n, shape, d)

        wqH, wqL = sb("wqH", [P, NC, P], F32R), sb("wqL", [P, NC, P], F32R)
        wkvH, wkvL = sb("wkvH", [P, 512], F32R), sb("wkvL", [P, 512], F32R)
        m1H, m1L = sb("m1H", [P, 512], F32R), sb("m1L", [P, 512], F32R)
        prH, prL = sb("prH", [P, 512], F32R), sb("prL", [P, 512], F32R)
        wo, bo = sb("wo", [P, P]), sb("bo", [P, P])
        msk = sb("msk", [P, 2])
        temp = sb("temp", [P, 4])
        st, mv = sb("st", [P, GT, 6]), sb("mv", [P, GT, 2])
        half_neg, rstd, var_e = (sb(n, [P, GT]) for n in ("hn", "rstd", "vare"))
        xn = sb("xn", [P, GT, P])
        xH, xL = sb("xH", [P, 2, GN], F32R), sb("xL", [P, 2, GN], F32R)
        af = sb("af", [P, 2, GN])
        aH, aL = sb("aH", [P, 2, NC, GN], F32R), sb("aL", [P, 2, NC, GN], F32R)
        kv = sb("kv", [P, GT, HEADS, 32])
        qH = sb("qH", [P, GN], F32R)
        qs = sb("qs", [P, 2, NC, GN], F32R)
        ee, pn = sb("ee", [P, 4, 512]), sb("pn", [P, 4, 512])
        sm, ri = sb("sm", [P, 2, 32]), sb("ri", [P, 4, 32])
        mx, dd = sb("mx", [P, 2, 32]), sb("dd", [P, 2, 512])
        bound = sb("bound", [1, 2 * BITS * CORNERS + CORNERS + 2])
        small = sb0("a_small", [1, 1], mybir.dt.int32)
        bT, bH = sb("bT", [P, 512]), sb("bH", [P, 512], F32R)
        kst = sb("kst", [P, NC, HC, S], F32R)
        bv = sb("bv", [P, HEADS, 32])
        nm = sb("nm", [P, GT, HEADS])
        nmH = sb("nmH", [P, GT, HEADS], F32R)
        nmp = sb("nmp", [P, GT, HEADS, 32])
        e2 = sb("e2", [P, 2, HC, GN])
        nT = sb("nT", [P, NC, GN])
        rden = sb("rden", [P, GT, HEADS])
        on = sb("on", [P, GT, P])
        oT = sb("oT", [P, GN])
        raws = raw["g"][:].rearrange("p u n -> p (u n)")
        wq, wkv, plane, proto = (raws[:, 512 * n:512 * n + 512] for n in range(4))
        wk = raws[:, 2048:2048 + P]
        rw = sb("rw", [P, EXPERTS])

        s_x0, s_x, s_w, s_wc, s_m1, s_raw, s_rawd, s_temp = (
            sem("a_" + n) for n in ("x0", "x", "w", "wc", "m1", "raw", "rawd", "temp"))
        names = ("xb mb st stat rstd xn xt xh xl ap af ah al kp kc qp qh qs lg d e sm ri pn bk bt bvt bv bh stk sc mx nmh "
                 "nmp nmt qf ss e2 pv nc ot rd on ht oc y x pc").split()
        s = {n: sem("a_s_" + n) for n in names}
        s.update(ticks)
        TPB, PJ, BK, NV = (PS[:, n, :] for n in (0, 1, 6, 7))

        def LG(n):
            return PS[:, 2 + n % 2, :]

        def SC(n):
            return PS[:, 4 + n % 2, :]

        def after(eng, name, value):
            if not isinstance(value, int) or value > 0:
                eng.wait_ge(s[name], value)

        def tokens(g):
            return x[:, ds(g * GT, GT), :].rearrange("p i f -> p (i f)")

        def spread(n, first, last, total=16):
            m = last - first + 1
            k = min(max(n - first, 0), m)
            return range(total * k // m, total * min(max(n - first + 1, 0), m) // m)

        OUT = 1
        LAG = 4
        A2 = (0, 7)
        A3 = (8, 15)

        def pipeline(eng, step):
            for G in range(3):
                step(G // 2, G % 2, True, G >= 2, False)
            with eng.Fori(1, NG // 2 - 1) as i:
                step(i, 1, True, True, True)
                step(i + 1, 0, True, True, True)
            step(NG // 2 - 1, 1, True, True, True)
            for G in range(NG, NG + 3):
                step(G // 2, G % 2, False, G < NG + 2, True)

        block = ctx.enter_context(nc.Block())
        NW = 7
        WC = 1 + HC + 3 + 6 + 2 * 5

        @block.sync
        def _(sp):
            xi = A["x"].rearrange("b (p i) d -> p b i d", i=NI)
            sp.dma_start(x[:, 0:NI, :], xi[:, 0]).then_inc(s_x0, 16)
            sp.dma_start(ident[:], A["ident"]).then_inc(s_x0, 16)
            sp.dma_start(temp[:, 0:1], A["temp"].partition_broadcast(P)).then_inc(s_w, 16)
            sp.dma_start(msk[:], A["msk"]).then_inc(s_w, 16)
            sp.dma_start(bound[:, 0:BITS * CORNERS], A["protos"].rearrange("k r -> (k r)").unsqueeze(0)).then_inc(s_w, 16)
            sp.dma_start(wo[:], A["woT"]).then_inc(s_w, 16)
            sp.dma_start(bo[:], A["bo"].partition_broadcast(P)).then_inc(s_w, 16)
            for b in range(1, NB):
                sp.dma_start(x[:, b * NI:(b + 1) * NI, :], xi[:, b]).then_inc(s_x, 16)
            sp.dma_start(rw[:], A["rwT"]).then_inc(s_x, 16)
            for name in "udg":
                if name == "g":
                    sp.wait_ge(s_rawd, 1)
                sp.dma_start(raw[name][:], A["w_" + name]).then_inc(s_raw, 16)
            sp.dma_start(rbias[:], A["rbias"].partition_broadcast(P)).then_inc(s_raw, 16)
            sp.wait_ge(s_raw, 64)

        def project_pool_rstd(g, G):
            after(g, "stat", G + 1)
            apart(g, s["tickp"])
            g.tensor_scalar(var_e[:], mv[:, :, 1], LN_EPS, None, ALU.add).then_inc(s["pc"], 1)
            g.wait_ge(s["pc"], G + 1)
            g.tensor_tensor(rstd[:], var_e[:], half_neg[:], ALU.pow).then_inc(s["rstd"], 1)

        def project_pool_low(g, G, z, c):
            g.wait_ge(s["ah"], 4 * G + (c + 1))
            g.tensor_tensor(aL[:, z, c, :], af[:, c % 2, :], aH[:, z, c, :].bitcast(F32),
                            ALU.subtract).then_inc(s["al"], 1)

        @block.gpsimd
        def _(g):
            g.memset(half_neg[:], -0.5)
            g.memset(nmp[:], 0.0)
            g.memset(bv[:], 0.0)
            g.memset(x[:, NB * NI:, :], 0.0).then_inc(s_m1, 1)
            g.wait_ge(s_m1, 1)
            g.memset(bv[:, :, HD:HD + 1], 1.0).then_inc(s_m1, 1)
            project_pool_rstd(g, 0)
            g.wait_ge(s_w, 16 * NW)
            for c in range(NC):
                project_pool_low(g, 0, 0, c)

            def step(half, z, buckets, attends, finishes):
                G = 2 * half + z
                if attends:
                    x4 = x[:, ds((G - 2) * GT, GT), :]
                    g.tensor_tensor(x4, x4, bo[:].unsqueeze(1).to_broadcast([P, GT, P]), ALU.add).then_inc(s["xb"], 1)
                if not buckets:
                    return
                for n in range(16):
                    g.wait_ge(s["ri"], 16 * G + (n + 1))
                    after(g, "bk", 16 * G + (n - 3))
                    g.tensor_tensor(pn[:, n % 4, :].rearrange("p (q r) -> p q r", r=CORNERS),
                                    ee[:, n % 4, :].rearrange("p (q r) -> p q r", r=CORNERS),
                                    ri[:, n % 4, :].unsqueeze(2).to_broadcast([P, 32, CORNERS]),
                                    ALU.mult).then_inc(s["pn"], 1)
                    if n == 1:
                        project_pool_rstd(g, G + 1)
                    if 7 <= n < 11:
                        project_pool_low(g, G + 1, 1 - z, n - 7)

            pipeline(g, step)

        @block.scalar
        def _(a):
            a.dma_start(raws[:, 1024:], A["w_a"][:, 1024:]).then_inc(s_w, 16)
            a.dma_start(raws[:, 0:1024], A["w_a"][:, 0:1024]).then_inc(s_w, 16)

            def high_x(G, z):
                a.wait_ge(s["xt"], G + 1)
                a.activation(xH[:, z, :], PJ, ACT.Copy).then_inc(s["xh"], 1)

            def planes(G, z, c):
                a.wait_ge(s["ap"], 4 * G + (c + 1))
                after(a, "al", 4 * G + (c - 1))
                a.activation(af[:, c % 2, :], PJ, ACT.Tanh).then_inc(s["af"], 1)

            def keys(G, i):
                a.wait_ge(s["kp"], 4 * G + (i + 1))
                a.activation(kv[:, i, :, :], TPB.rearrange("p (h k) -> p h k", k=32), ACT.Copy).then_inc(s["kc"], 1)

            def high_q(G, c):
                a.wait_ge(s["qp"], 4 * G + (c + 1))
                after(a, "qs", 4 * G + c)
                a.activation(qH[:], PJ, ACT.Copy).then_inc(s["qh"], 1)

            def step(half, z, buckets, attends, finishes, guarded):
                G = 2 * half + z
                H = G - 2
                for n in range(16):
                    if finishes and n == 0:
                        numerators(a, H - 1, NC - 1)
                    if finishes and n == 6:
                        a.wait_ge(s["ht"], H)
                        a.activation(oT[:], NV, ACT.Copy).then_inc(s["oc"], 1)
                    if attends and z == 0 and n == 0:
                        a.wait_ge(s["bk"], 16 * G)
                        a.activation(bT[:], BK, ACT.Copy).then_inc(s["bt"], 1)
                    if buckets:
                        if guarded:
                            a.wait_ge(s["d"], 16 * G + (n + 1))
                            src = dd[:, n % 2, :]
                        else:
                            a.wait_ge(s["lg"], 16 * G + (n + 1))
                            src = LG(n)
                        after(a, "pn", 16 * G + (n - 3))
                        a.activation(ee[:, n % 4, :], src, ACT.Exp).then_inc(s["e"], 1)
                    if buckets:
                        if n == 5:
                            high_x(G + 1, 1 - z)
                        if 7 <= n < 11:
                            planes(G + 1, 1 - z, n - 7)
                    if n < 4 and (attends and (buckets or z == 0) or z == 1 and buckets):
                        high_q(G - 1, n)
                    if buckets and 1 <= n <= GT:
                        keys(G, n - 1)
                    if attends:
                        for m in spread(n, *A3):
                            a.wait_ge(s["ss"], 16 * H + (m + 1))
                            if m >= 8:
                                a.wait_ge(s["pv"], 4 * H + (m // 4 - 1))
                            a.activation(e2[:, m // 4 % 2, m % 4, :], SC(m), ACT.Exp, scale=float(HD) ** -0.5).then_inc(s["e2"], 1)
                            if m % 4 == 2 and m >= 6:
                                numerators(a, H, m // 4 - 1)

            def numerators(a, H, c):
                a.wait_ge(s["pv"], 4 * H + (c + 1))
                a.activation(nT[:, c, :], NV, ACT.Copy).then_inc(s["nc"], 1)

            a.wait_ge(s_w, 16 * NW)
            a.activation(temp[:, 1:2], temp[:, 0:1], ACT.Exp).then_inc(s_temp, 1)
            high_x(0, 0)
            for c in range(NC):
                planes(0, 0, c)
            a.wait_ge(s_temp, 2)
            flag = a.value_load(small[:], min_val=0, max_val=1)
            with a.If(flag == 1):
                pipeline(a, lambda *where: step(*where, guarded=False))
            with a.Else():
                pipeline(a, lambda *where: step(*where, guarded=True))

        @block.vector
        def _(v):
            def stats(G):
                for i in range(GT):
                    last = v.bn_stats(st[:, i, :], x[:, ds(G * GT + i, 1), :].rearrange("p o f -> p (o f)"))
                last.then_inc(s["st"], 1)

            def stats2(G):
                v.wait_ge(s["st"], G + 1)
                apart(v, s["tick"])
                for i in range(GT):
                    last = v.bn_aggr(mv[:, i, :], st[:, i, :])
                last.then_inc(s["stat"], 1)

            def norm(G):
                v.wait_ge(s["rstd"], G + 1)
                for i in range(GT):
                    last = v.tensor_scalar(xn[:, i, :], x[:, ds(G * GT + i, 1), :].rearrange("p o f -> p (o f)"),
                                           mv[:, i, 0:1], rstd[:, i:i + 1], ALU.subtract, ALU.mult)
                last.then_inc(s["xn"], 1)

            def low_x(G, z):
                v.wait_ge(s["xh"], G + 1)
                v.tensor_tensor(xL[:, z, :], PJ, xH[:, z, :].bitcast(F32), ALU.subtract).then_inc(s["xl"], 1)

            def high_a(G, z, c):
                v.wait_ge(s["af"], 4 * G + (c + 1))
                v.tensor_copy(aH[:, z, c, :], af[:, c % 2, :]).then_inc(s["ah"], 1)

            def stack_q(G, z, c):
                v.wait_ge(s["qh"], 4 * G + (c + 1))
                v.scalar_tensor_tensor(qs[:, z, c, :], qH[:].bitcast(F32), msk[:, 0:1], PJ,
                                       ALU.mult, ALU.add).then_inc(s["qs"], 1)

            def sums(G, n):
                v.wait_ge(s["e"], 16 * G + (n + 1))
                v.tensor_reduce(sm[:, n % 2, :], ee[:, n % 4, :].rearrange("p (q r) -> p q r", r=CORNERS),
                                AX.X, ALU.add).then_inc(s["sm"], 1)
                v.wait_ge(s["sm"], 16 * G + (n + 1))
                after(v, "pn", 16 * G + (n - 3))
                v.reciprocal(ri[:, n % 4, :], sm[:, n % 2, :]).then_inc(s["ri"], 1)

            def step(half, z, buckets, attends, finishes, guarded):
                G = 2 * half + z
                H = G - 2

                def outputs(i, H):
                    bank = NV.rearrange("p (h k) -> p h k", k=32)
                    v.wait_ge(s["ot"], 4 * H + (i + 1))
                    v.reciprocal(rden[:, i, :], bank[:, :, HD]).then_inc(s["rd"], 1)
                    v.wait_ge(s["rd"], 4 * H + (i + 1))
                    v.tensor_tensor(on[:, i, :].rearrange("p (h d) -> p h d", d=HD), bank[:, :, 0:HD],
                                    rden[:, i, :].unsqueeze(2).to_broadcast([P, HEADS, HD]),
                                    ALU.mult).then_inc(s["on"], 1)

                for n in range(16):
                    if buckets:
                        if guarded:
                            lg = LG(n).rearrange("p (q r) -> p q r", r=CORNERS)
                            v.wait_ge(s["lg"], 16 * G + (n + 1))
                            v.tensor_reduce(mx[:, n % 2, :], lg, AX.X, ALU.max).then_inc(s["mb"], 1)
                            v.wait_ge(s["mb"], 16 * G + (n + 1))
                            after(v, "e", 16 * G + (n - 1))
                            v.tensor_tensor(dd[:, n % 2, :].rearrange("p (q r) -> p q r", r=CORNERS), lg,
                                            mx[:, n % 2, :].unsqueeze(2).to_broadcast([P, 32, CORNERS]),
                                            ALU.subtract).then_inc(s["d"], 1)
                        if n >= 1:
                            sums(G, n - 1)
                        if 8 <= n < 12:
                            high_a(G + 1, 1 - z, n - 8)
                        if n == 0:
                            stats(G + 1)
                            stats2(G + 1)
                        if n == 3:
                            norm(G + 1)
                        if n == 5:
                            low_x(G + 1, 1 - z)
                    if attends and z == 0 and n == 0:
                        stack_keys(half)
                    if finishes and n in range(OUT + 1, OUT + 1 + GT):
                        outputs(n - OUT - 1, H - 1)
                    if finishes and n == 8:
                        v.wait_ge(s["xb"], H)
                        v.wait_ge(s["y"], H)
                        v.tensor_tensor(tokens(H - 1), NV, tokens(H - 1), ALU.add).then_inc(s["x"], 1)
                    if n < 4 and not attends and z == 1 and buckets or n == 0 and attends and z == 0:
                        stack_q(G - 1, 1 - z, n)
                    if attends:
                        for m in spread(n, A2[0] + (z == 0), A2[1]):
                            if m == spread(n, A2[0] + (z == 0), A2[1])[-1] and n < 4 and (buckets or z == 0):
                                stack_q(G - 1, 1 - z, n)
                            v.wait_ge(s["sc"], 16 * H + (m + 1))
                            v.tensor_reduce(nm[:, m // 4, 4 * (m % 4):4 * (m % 4) + 4],
                                            SC(m).rearrange("p (j s) -> p j s", s=S), AX.X, ALU.max,
                                            negate=True).then_inc(s["mx"], 1)
                        if n == A2[1]:
                            v.wait_ge(s["mx"], 16 * H + 16)
                            v.tensor_copy(nmH[:], nm[:]).then_inc(s["nmh"], 1)
                            v.wait_ge(s["nmh"], H + 1)
                            v.tensor_copy(nmp[:, :, :, 24], nmH[:].bitcast(F32))
                            v.tensor_tensor(nmp[:, :, :, 25], nm[:], nmH[:].bitcast(F32),
                                            ALU.subtract).then_inc(s["nmp"], 1)
                        for m in spread(n, *A3):
                            if m % 4 == 0:
                                c = m // 4
                                v.wait_ge(s["nmt"], 4 * H + (c + 1))
                                v.tensor_tensor(qs[:, z, c, :], qs[:, z, c, :].bitcast(F32), TPB,
                                                ALU.add).then_inc(s["qf"], 1)
                if buckets:
                    sums(G, 15)

            def stack_keys(half):
                v.wait_ge(s["bt"], half)
                v.tensor_copy(bH[:], bT[:]).then_inc(s["bh"], 1)
                v.wait_ge(s["bh"], half)
                for j in range(HC):
                    r = slice(32 * j, 32 * j + 24)
                    last = v.scalar_tensor_tensor(kst[r, :, j, :],
                                                  bH[r, :].bitcast(F32).rearrange("p (c s) -> p c s", c=NC),
                                                  msk[r, 1:2], bT[r, :].rearrange("p (c s) -> p c s", c=NC),
                                                  ALU.mult, ALU.add)
                last.then_inc(s["stk"], 1)
                v.wait_ge(s["bvt"], half)
                v.tensor_copy(bv[:, :, 0:HD],
                              TPB.rearrange("p (h k) -> p h k", k=32)[:, :, 24:32]).then_inc(s["bv"], 1)

            c = Chain(v, s_wc)
            c.step(v.memset(kst[:].bitcast(F32), 0.0))
            for j in range(HC):
                c.step(v.memset(kst[32 * j:32 * j + 32, :, j, :].bitcast(F32), 1.0))
            v.wait_ge(s_x0, 32)
            stats(0)
            stats2(0)
            norm(0)
            v.wait_ge(s_w, 16 * NW)
            v.wait_ge(s_temp, 1)
            c.step(v.tensor_scalar(temp[:, 2:3], temp[:, 1:2], 0.01, 20.0, ALU.max, ALU.min))
            c.step(v.reciprocal(temp[:, 3:4], temp[:, 2:3]))
            c.step(v.tensor_scalar(proto, proto, temp[:, 3:4], None, ALU.mult))
            n = BITS * CORNERS
            b0, b1, b2, b3 = bound[:, 0:n], bound[:, n:2 * n], bound[:, 2 * n:2 * n + CORNERS], bound[:, 2 * n + CORNERS:]
            c.step(v.tensor_scalar(b1, b0, -1.0, None, ALU.mult))
            c.step(v.tensor_tensor(b0, b0, b1, ALU.max))
            c.step(v.tensor_reduce(b2, b0.rearrange("p (k r) -> p r k", r=CORNERS), AX.X, ALU.add))
            c.step(v.tensor_reduce(b3[:, 0:1], b2, AX.X, ALU.max))
            c.step(v.tensor_tensor(b3[:, 1:2], b3[:, 0:1], temp[0:1, 3:4], ALU.mult))
            c.step(v.tensor_scalar(small[:], b3[:, 1:2], SMALL, None, ALU.is_le))
            v.sem_inc(s_temp, 1)
            v.wait_ge(s["rstd"], 1)
            low_x(0, 0)
            v.wait_ge(s_m1, 3)
            split_rows(v, c, m1H[:], m1L[:], LG(0))
            split_rows(v, c, wkvH[:], wkvL[:], wkv)
            split_rows(v, c, prH[:], prL[:], proto)
            split_rows(v, c, wqH[:].rearrange("p c n -> p (c n)"), wqL[:].rearrange("p c n -> p (c n)"), wq)
            v.wait_ge(s_x, 16 * NB)
            split_rows(v, c, rwH[:], rwL[:], rw[:])
            v.sem_inc(s_rawd, 1)
            v.sem_inc(s["x"], 1)
            for c in range(NC):
                high_a(0, 0, c)
            flag = v.value_load(small[:], min_val=0, max_val=1)
            with v.If(flag == 1):
                pipeline(v, lambda *where: step(*where, guarded=False))
            with v.Else():
                pipeline(v, lambda *where: step(*where, guarded=True))

        @block.tensor
        def _(t):
            def transpose_x(G):
                t.wait_ge(s["xn"], G + 1)
                after(t, "qs", 4 * (G - 1))
                after(t, "af", 4 * G)
                apart(t, s["tickt"])
                for i in range(GT):
                    last = t.transpose(PJ[:, P * i:P * i + P], xn[:, i, :], ident[:])
                last.then_inc(s["xt"], 1)

            def planes(G, z, c):
                if c == 0:
                    t.wait_ge(s["xl"], G + 1)
                else:
                    t.wait_ge(s["af"], 4 * G + c)
                three_pass(t, PJ, (m1H[:, P * c:P * c + P], m1L[:, P * c:P * c + P]),
                           (xH[:, z, :], xL[:, z, :])).then_inc(s["ap"], 1)

            def keys(G, z, i):
                if i:
                    t.wait_ge(s["kc"], 4 * G + i)
                tok = slice(P * i, P * i + P)
                three_pass(t, TPB, (xH[:, z, tok], xL[:, z, tok]), (wkvH[:], wkvL[:])).then_inc(s["kp"], 1)

            def logits(G, z, n):
                if n == 16:
                    z = 1 - z
                i, c = n // 4 % GT, n % 4
                tok = slice(P * i, P * i + P)
                if n % 16 < NC:
                    t.wait_ge(s["al"], 4 * G + (n // 4 + c + 1))
                after(t, "e", 16 * G + (n - 1))
                three_pass(t, LG(n), (aH[:, z, c, tok], aL[:, z, c, tok]), (prH[:], prL[:])).then_inc(s["lg"], 1)

            def queries(G, z, c):
                if c == 0:
                    t.wait_ge(s["af"], 4 * G + 8)
                else:
                    t.wait_ge(s["qs"], 4 * G + c)
                three_pass(t, PJ, (wqH[:, c, :], wqL[:, c, :]), (xH[:, z, :], xL[:, z, :])).then_inc(s["qp"], 1)

            def step(half, z, buckets, attends, finishes):
                G = 2 * half + z
                H = G - 2

                def add(n, G=G, own=True):
                    i, c = n // 4, n % 4
                    if c == 0:
                        t.wait_ge(s["kc"], 4 * G + (i + 1))
                    t.wait_ge(s["pn"], 16 * G + (n + 1))
                    for j in range(HC):
                        last = t.matmul(BK[32 * j:32 * j + 32, S * c:S * c + S], kv[:, i, HC * c + j, :],
                                        pn[:, n % 4, S * j:S * j + S], start=(own and z == 0 and n == 0),
                                        stop=(own and z == 1 and i == GT - 1), skip_group_check=True)
                    last.then_inc(s["bk"], 1)

                def scores(m):
                    if m == 0 and z == 0:
                        t.wait_ge(s["stk"], half)
                    if m >= 2:
                        t.wait_ge(s["mx"], 16 * H + (m - 1))
                    t.matmul(SC(m), qs[:, z, m % 4, P * (m // 4):P * (m // 4) + P],
                             kst[:, m % 4, :, :].rearrange("p j s -> p (j s)"),
                             start=True, stop=True).then_inc(s["sc"], 1)

                def outputs(i, H):
                    if i == 0:
                        t.wait_ge(s["nc"], 4 * H + 4)
                    else:
                        t.wait_ge(s["on"], 4 * H + i)
                    for c in range(NC):
                        last = t.transpose(NV[:, P * c:P * c + P], nT[:, c, P * i:P * i + P], ident[:])
                    last.then_inc(s["ot"], 1)

                def values(c, H):
                    t.wait_ge(s["e2"], 16 * H + (4 * c + 4))
                    if c == 0:
                        t.wait_ge(s["x"], H + 1)
                    else:
                        t.wait_ge(s["nc"], 4 * H + c)
                    for j in range(HC):
                        last = t.matmul(NV[32 * j:32 * j + 32, :], bv[:, HC * c + j, :], e2[:, c % 2, j, :],
                                        start=True, stop=True)
                    last.then_inc(s["pv"], 1)

                for n in range(16):
                    if buckets and n == 0:
                        logits(G, z, 1)
                    if finishes and n == 0:
                        values(NC - 1, H - 1)
                    if finishes and n == 6:
                        t.wait_ge(s["on"], 4 * H)
                        for i in range(GT):
                            last = t.transpose(NV[:, P * i:P * i + P], on[:, i, :], ident[:])
                        last.then_inc(s["ht"], 1)
                    if finishes and n == 7:
                        t.wait_ge(s["oc"], H)
                        for i in range(GT):
                            last = t.matmul(NV[:, P * i:P * i + P], oT[:, P * i:P * i + P], wo[:], start=True, stop=True)
                        last.then_inc(s["y"], 1)
                    if attends and z == 0 and n == 0:
                        t.wait_ge(s["bt"], half)
                        for k in range(NC):
                            last = t.transpose(TPB[:, P * k:P * k + P], bT[:, P * k:P * k + P], ident[:])
                        last.then_inc(s["bvt"], 1)
                    if attends:
                        for m in spread(n, A2[0] + (z == 0), A2[1])[:2]:
                            scores(m)
                    if n < 4 and (attends and (buckets or z == 0) or z == 1 and buckets):
                        queries(G - 1, 1 - z, n)
                    if buckets:
                        if n:
                            logits(G, z, n + 1)
                        if n == 1 and z == 0 and attends:
                            t.wait_ge(s["bv"], half)
                        if 1 <= n <= GT:
                            keys(G, z, n - 1)
                        if n >= LAG:
                            add(n - LAG)
                        elif z == 1:
                            add(16 - LAG + n, G - 1, False)
                        if n == 4:
                            transpose_x(G + 1)
                        if 7 <= n < 11:
                            planes(G + 1, 1 - z, n - 7)
                    if attends:
                        for m in spread(n, A2[0] + (z == 0), A2[1])[2:]:
                            scores(m)
                        for m in spread(n, *A3):
                            k, j = m // 4, m % 4
                            if j == 0:
                                if k == 0:
                                    if buckets:
                                        t.wait_ge(s["kc"], 4 * G + 4)
                                    t.wait_ge(s["nmp"], H + 1)
                                    t.wait_ge(s["mx"], 16 * H + 16)
                                    turn_max(t, k)
                                t.wait_ge(s["qf"], 4 * H + (k + 1))
                                if k < NC - 1:
                                    turn_max(t, k + 1)
                            if m >= 2:
                                t.wait_ge(s["e2"], 16 * H + (m - 1))
                            t.matmul(SC(m), kst[:, k, j, :], qs[:, z, k, :], start=True, stop=True).then_inc(s["ss"], 1)
                            if m % 4 == 1 and m > 4:
                                values(m // 4 - 1, H)
                    if finishes and n in range(OUT, OUT + GT):
                        outputs(n - OUT, H - 1)
                if buckets and z == 1:
                    for n in range(16 - LAG, 16):
                        add(n)

            def turn_max(t, c):
                for i in range(GT):
                    last = t.transpose(TPB[:, P * i:P * i + P],
                                       nmp[:, i, HC * c:HC * c + HC, :].rearrange("p j k -> p (j k)"), ident[:])
                last.then_inc(s["nmt"], 1)

            t.wait_ge(s_x0, 32)
            transpose_x(0)
            t.wait_ge(s_m1, 2)
            t.wait_ge(s_w, 16 * NW)
            t.matmul(LG(0), wk, plane, start=True, stop=True).then_inc(s_m1, 1)
            t.wait_ge(s_wc, WC)
            for c in range(NC):
                planes(0, 0, c)
            logits(0, 0, 0)
            pipeline(t, step)



def ffn(nc, A, mk, ticks, tag, x, ident, W, rwH, rwL, rbias, sel, PS, raw=None, out=None, s_done=None):
    ctx = ExitStack()
    with ctx:
        sb0, sem = mk(ctx)

        def sb(n, shape, d):
            return sb0(tag + n, shape, d)

        identb = sb("identb", [P, P], BF16)
        st, mv = sb("st", [P, GT, 6], F32), sb("mv", [P, GT, 2], F32)
        half_neg, rstd, var_e = (sb(n, [P, GT], F32) for n in ("hn", "rstd", "vare"))
        xn = sb("xn", [P, GT, P], F32)
        xH, xL = sb("xH", [P, 2, GN], F32R), sb("xL", [P, 2, GN], F32R)
        wT = sb("wT", [96, 2, GN], BF16)
        lg, near0, lgs, sil, rec, sc, wgt, w, r1, r2 = (
            sb(n, [P, GT, EXPERTS], F32) for n in "lg near0 lgs sil rec sc wgt w r1 r2".split())
        top8 = sb("top8", [P, GT, NGROUP, 8], F32)
        gsum = sb("gsum", [P, GT, 10], F32)
        g8, e8 = sb("g8", [P, GT, 8], F32), sb("e8", [P, GT, 8], F32)
        gsel = sb("gsel", [P, GT, 10], F32)
        gmask = sb("gmask", [P, GT, NGROUP], F32)
        sfc = sb("sfc", [P, GT, EXPERTS], F32)
        cand = sb("cand", [P, GT, EXPERTS + 4], F32)
        esel = sb("esel", [P, GT, EXPERTS + 4], F32)
        den, rden = sb("den", [P, GT], F32), sb("rden", [P, GT], F32)
        w3 = sb("w3", [P, GT, 96], BF16)
        sg, at = (sb(n, [P, 2, GN], F32) for n in ("sg", "at"))
        bt = sb("bt", [P, 3, GN], F32)
        bH, bL = sb("bH", [P, 3, GN], F32R), sb("bL", [P, 3, GN], F32R)
        yT = sb("yT", [P, GN], F32)
        names = ("stat rstd xn xt xh xl rt lgs sil w3 wt wtc G U WB sg a b bh bl dn yt yo vc init iv").split()
        s = {n: sem(tag + "_" + n) for n in names}
        s.update(ticks)
        NU = UNITS + 1
        TPB, Y = PS[:, 0, :], PS[:, 7, :]
        BANKS = {"G": (2, 3), "U": (4, 5), "WB": (1, 6)}
        block = ctx.enter_context(nc.Block())

        def tokens(g):
            return x[:, ds(g * GT, GT), :]

        def bank(name, u, z):
            return PS[:, BANKS[name][(u + z) % 2], :]

        def buf(u):
            return u % NU % 3

        def reuse(eng, name, k, u):
            if not isinstance(k, int) or k >= 3:
                eng.wait_ge(s[name], k - 2 + (u % NU < 2))

        def run_groups(eng, main):
            main(0, False, True, 0)
            with eng.Fori(0, NG // 2 - 1) as i:
                main(2 * i + 1, True, True, 1)
                main(2 * i + 2, True, True, 0)
            main(NG - 1, True, False, 1)

        if raw is not None:
            selF = sb("selF", [96, UNITS, P], F32)
            s_ld, s_high, s_low, s_lowp = (sem("p_" + n) for n in ("ld", "high", "low", "lowp"))

            @block.sync
            def _(sp):
                sp.dma_start(selF[:], A["sel"]).then_inc(s_ld, 16)

        if out is not None:
            @block.sync
            def _(sp):
                o = out.rearrange("b (p i) d -> p b i d", i=NI)
                per = NI // GT
                for g in range(NG):
                    sp.wait_ge(s["iv"], g + 4)
                    tiles = slice(GT * (g % per), GT * (g % per) + GT)
                    sp.dma_start(o[:, g // per, tiles], x[:, g * GT:(g + 1) * GT, :]).then_inc(s_done, 16)
                sp.wait_ge(s_done, 16 * NG)

        @block.gpsimd
        def _(p):
            p.memset(half_neg[:], -0.5).then_inc(s["init"], 1)
            p.wait_ge(s["init"], 1)

            def prologue(g):
                p.wait_ge(s["stat"], g + 1)
                apart(p, s["tickp"])
                p.tensor_scalar(var_e[:], mv[:, :, 1], LN_EPS, None, ALU.add).then_inc(s["init"], 1)
                p.wait_ge(s["init"], g + 2)
                p.tensor_tensor(rstd[:], var_e[:], half_neg[:], ALU.pow).then_inc(s["rstd"], 1)

            def low(g, u, z):
                k, n = g * NU + u, buf(u)
                p.wait_ge(s["bh"], k + 1)
                reuse(p, "dn", k, u)
                p.tensor_tensor(bL[:, n, :], bt[:, n, :], bH[:, n, :].bitcast(F32),
                                ALU.subtract).then_inc(s["bl"], 1)

            def main(g, before, more, z):
                for u in range(NU):
                    if more and u == 1:
                        prologue(g + 1)
                    low(g, u, z)

            prologue(0)
            if raw is not None:
                for m, n in enumerate("ud"):
                    p.wait_ge(s_high, m + 2)
                    p.tensor_tensor(W[n + "L"][:], raw[n][:], W[n + "H"][:].bitcast(F32), ALU.subtract).then_inc(s_lowp, 1)
            run_groups(p, main)

        @block.scalar
        def _(a):
            def copy_x(g, z):
                a.wait_ge(s["xt"], g + 1)
                a.activation(xH[:, z, :], TPB, ACT.Copy).then_inc(s["xh"], 1)

            def silu_route(g):
                a.wait_ge(s["lgs"], g + 1)
                a.activation(sil[:], lgs[:], ACT.Silu).then_inc(s["sil"], 1)

            def copy_w(g, z):
                a.wait_ge(s["wt"], g + 1)
                a.activation(wT[:, z, :], TPB[0:96, :].bitcast(BF16)[:, 0:GN], ACT.Copy).then_inc(s["wtc"], 1)

            def silu(g, u, z):
                k = g * NU + u
                a.wait_ge(s["G"], k + 1)
                if not isinstance(k, int) or k >= 2:
                    a.wait_ge(s["a"], k - 1)
                a.activation(sg[:, (u + z) % 2, :], bank("G", u, z), ACT.Silu).then_inc(s["sg"], 1)

            def high(g, u, z):
                k, n = g * NU + u, buf(u)
                a.wait_ge(s["b"], k + 1)
                reuse(a, "dn", k, u)
                a.activation(bH[:, n, :], bt[:, n, :], ACT.Copy).then_inc(s["bh"], 1)

            def copy_y(g):
                a.wait_ge(s["dn"], g * NU + NU)
                a.activation(yT[:], Y, ACT.Copy).then_inc(s["yt"], 1)

            def main(g, before, more, z):
                for u in range(1, NU + more):
                    silu(g, u, z)
                    if more and u == NU:
                        copy_w(g + 1, 1 - z)
                    if before and u == LAG:
                        copy_y(g - 1)
                    if before or u >= 2:
                        high(g, u - 2, z)
                    if more and u == X_AT + 1:
                        copy_x(g + 1, 1 - z)
                    if more and u == ROUTE_AT + 1:
                        silu_route(g + 1)
                if not more:
                    for u in range(NU - 2, NU):
                        high(g, u, z)
                    copy_y(g)

            def high_part(n):
                a.activation(W[n + "H"][:], raw[n][:], ACT.Copy).then_inc(s_high, 1)

            if raw is not None:
                high_part("g")
            copy_x(0, 0)
            if raw is not None:
                high_part("u")
                high_part("d")
            silu_route(0)
            if raw is not None:
                a.wait_ge(s_ld, 16)
                a.activation(sel[:], selF[:], ACT.Copy).then_inc(s_high, 1)
            copy_w(0, 0)
            silu(0, 0, 0)
            run_groups(a, main)

        @block.vector
        def _(v):
            c = Chain(v, s["iv"])
            c.step(v.tensor_copy(identb[:], ident[:]))
            c.step(v.memset(gsum[:], LOWEST))
            c.step(v.memset(cand[:], LOWEST))
            PER = 27

            def parts(g, z):
                c = Chain(v, s["vc"], PER, g)
                xg = tokens(g)

                def stats():
                    for i in range(GT):
                        last = v.bn_stats(st[:, i, :], x[:, ds(g * GT + i, 1), :].rearrange("p o f -> p (o f)"))
                    c.step(last)
                    apart(v, s["tick"])
                    for i in range(GT):
                        last = v.bn_aggr(mv[:, i, :], st[:, i, :])
                    last.then_inc(s["stat"], 1)

                def norm():
                    v.wait_ge(s["rstd"], g + 1)
                    for i in range(GT):
                        last = v.tensor_scalar(xn[:, i, :], x[:, ds(g * GT + i, 1), :].rearrange("p o f -> p (o f)"),
                                               mv[:, i, 0:1], rstd[:, i:i + 1], ALU.subtract, ALU.mult)
                    last.then_inc(s["xn"], 1)

                def low_x():
                    v.wait_ge(s["xh"], g + 1)
                    v.tensor_tensor(xL[:, z, :], TPB, xH[:, z, :].bitcast(F32), ALU.subtract).then_inc(s["xl"], 1)

                def logits():
                    v.wait_ge(s["rt"], g + 1)
                    c.step(v.tensor_copy(lg[:], TPB[:, 0:GT * EXPERTS].rearrange("p (i e) -> p i e", i=GT)))
                    c.step(v.tensor_tensor(near0[:], lg[:], lg[:], ALU.mult))
                    c.step(v.tensor_scalar(near0[:], near0[:], 1e-24, 4e-12, ALU.is_lt, ALU.mult))
                    v.tensor_tensor(lgs[:], near0[:], lg[:], ALU.add).then_inc(s["lgs"], 1)

                def recip():
                    v.wait_ge(s["lgs"], g + 1)
                    c.step(v.reciprocal(rec[:], lgs[:]))

                def scores():
                    v.wait_ge(s["sil"], g + 1)
                    c.step(v.tensor_tensor(sc[:], sil[:], rec[:], ALU.mult))
                    c.step(v.tensor_tensor(sfc[:], sc[:], rbias[:].unsqueeze(1).to_broadcast([P, GT, EXPERTS]),
                                           ALU.add))

                def best(tiles):
                    for i in tiles:
                        for q in range(NGROUP):
                            last = v.max(top8[:, i, q, :], sfc[:, i, GE * q:GE * q + GE])
                    return last

                def best_first():
                    best(range(0, GT // 2))

                def best_second():
                    c.step(best(range(GT // 2, GT)))

                def groups():
                    c.step(v.tensor_tensor(gsum[:, :, 0:NGROUP], top8[:, :, :, 0], top8[:, :, :, 1], ALU.add))
                    apart(v, s["tick"])
                    for i in range(GT):
                        last = v.max(g8[:, i, :], gsum[:, i, :])
                    c.step(last)
                    c.step(v.memset(g8[:, :, 2:8], LOWEST))

                def group_mask():
                    apart(v, s["tick"])
                    for i in range(GT):
                        last = v.match_replace(gsel[:, i, :], g8[:, i, :], gsum[:, i, :], -LOWEST)
                    c.step(last)
                    c.step(v.tensor_scalar(gmask[:], gsel[:, :, 0:NGROUP], -LOWEST, None, ALU.is_equal))

                def experts():
                    cv = cand[:, :, 0:EXPERTS].rearrange("p i (q e) -> p i q e", q=NGROUP)
                    for i in range(GT):
                        last = v.tensor_tensor(cv[:, i], sfc[:, i, :].rearrange("p (q e) -> p q e", q=NGROUP),
                                               gmask[:, i, :].unsqueeze(2).to_broadcast([P, NGROUP, GE]), ALU.mult)
                    c.step(last)
                    c.step(v.tensor_scalar(cand[:, :, 0:EXPERTS], cand[:, :, 0:EXPERTS], 0.0, None, ALU.add))

                def best_experts():
                    apart(v, s["tick"])
                    for i in range(GT):
                        last = v.max(e8[:, i, :], cand[:, i, :])
                    c.step(last)
                    c.step(v.memset(e8[:, :, TOPK:8], LOWEST))

                def chosen():
                    apart(v, s["tick"])
                    for i in range(GT):
                        last = v.match_replace(esel[:, i, :], e8[:, i, :], cand[:, i, :], -LOWEST)
                    c.step(last)

                def weights():
                    c.step(v.scalar_tensor_tensor(wgt[:], esel[:, :, 0:EXPERTS], -LOWEST, sc[:], ALU.is_equal,
                                                  ALU.mult))
                    c.step(v.tensor_reduce(den[:], wgt[:], AX.X, ALU.add))
                    c.step(v.tensor_scalar(den[:], den[:], 1e-20, None, ALU.add))
                    c.step(v.reciprocal(rden[:], den[:]))
                    c.step(v.scalar_tensor_tensor(w[:], rden[:].unsqueeze(2).to_broadcast([P, GT, EXPERTS]),
                                                  ROUTE_SCALE, wgt[:], ALU.mult, ALU.mult))

                def thirds():
                    c.step(v.tensor_copy(w3[:, :, 0:32], w[:]))
                    c.step(v.tensor_tensor(r1[:], w[:], w3[:, :, 0:32], ALU.subtract))
                    c.step(v.tensor_copy(w3[:, :, 32:64], r1[:]))
                    c.step(v.tensor_tensor(r2[:], r1[:], w3[:, :, 32:64], ALU.subtract))
                    v.tensor_copy(w3[:, :, 64:96], r2[:]).then_inc(s["w3"], 1)
                    assert c.n == PER, c.n

                return [stats, norm, low_x, logits, recip, scores, best_first, best_second, groups, group_mask, experts,
                        best_experts, chosen, weights, thirds]

            def hidden(g, u, z):
                k, n = g * NU + u, (u + z) % 2
                v.wait_ge(s["U"], k + 1)
                v.wait_ge(s["sg"], k + 1)
                if not isinstance(k, int) or k >= 2:
                    v.wait_ge(s["b"], k - 1)
                shared = u == UNITS
                if shared:
                    reuse(v, "bl", k, u)
                v.tensor_tensor(bt[:, buf(u), :] if shared else at[:, n, :], sg[:, n, :], bank("U", u, z),
                                ALU.mult).then_inc(s["a"], 1)

            def add_y(g):
                v.wait_ge(s["yo"], g + 1)
                xg = tokens(g).rearrange("p i f -> p (i f)")
                v.tensor_tensor(xg, TPB, xg, ALU.add).then_inc(s["iv"], 1)
                v.wait_ge(s["iv"], g + 4)

            def weigh(g, u, z):
                k, n = g * NU + u, (u + z) % 2
                v.wait_ge(s["a"], k + 1)
                if u == UNITS:
                    v.wait_ge(s["b"], k)
                    v.sem_inc(s["b"], 1)
                else:
                    v.wait_ge(s["WB"], g * UNITS + (u + (u < UNITS)))
                    reuse(v, "bl", k, u)
                    v.tensor_tensor(bt[:, buf(u), :], at[:, n, :], bank("WB", u, z), ALU.mult).then_inc(s["b"], 1)

            def main(g, before, more, z):
                after = {}
                if more:
                    for u, part in zip(PART_AT, parts(g + 1, 1 - z)):
                        after.setdefault(u, []).append(part)
                for u in range(1, NU + more):
                    hidden(g, u, z)
                    if u - 1 < UNITS:
                        weigh(g, u - 1, z)
                    if u == UNITS:
                        weigh(g, u, z)
                    if before and u == Y_AT + 2:
                        add_y(g - 1)
                    for part in after.get(u, ()):
                        part()
                if not more:
                    add_y(g)

            for n, part in enumerate(parts(0, 0)):
                part()
                if n == 1 and raw is not None:
                    v.wait_ge(s_high, 1)
                    v.tensor_tensor(W["gL"][:], raw["g"][:], W["gH"][:].bitcast(F32), ALU.subtract).then_inc(s_low, 1)
            hidden(0, 0, 0)
            run_groups(v, main)

        @block.tensor
        def _(t):
            def transpose_x(g):
                t.wait_ge(s["xn"], g + 1)
                for i in range(GT):
                    last = t.transpose(TPB[:, P * i:P * i + P], xn[:, i, :], ident[:])
                last.then_inc(s["xt"], 1)

            def route(g, z):
                t.wait_ge(s["xl"], g + 1)
                for i in range(GT):
                    tok = slice(P * i, P * i + P)
                    last = three_pass(t, TPB[:, EXPERTS * i:EXPERTS * i + EXPERTS], (xH[:, z, tok], xL[:, z, tok]),
                                      (rwH[:], rwL[:]))
                last.then_inc(s["rt"], 1)

            def transpose_w(g):
                t.wait_ge(s["w3"], g + 1)
                apart(t, s["tickt"])
                for i in range(GT):
                    last = t.transpose(TPB[0:96, :].bitcast(BF16)[:, P * i:P * i + P], w3[:, i, :], identb[:])
                last.then_inc(s["wt"], 1)

            def products(g, u, z):
                k, n, zu = g * NU + u, u % NU, (z + u // NU) % 2
                later = not isinstance(k, int) or k >= 2
                xs = (xH[:, zu, :], xL[:, zu, :])
                if later:
                    t.wait_ge(s["sg"], k - 1)
                three_pass(t, bank("G", u, z), (W["gH"][:, n, :], W["gL"][:, n, :]), xs).then_inc(s["G"], 1)
                if later:
                    t.wait_ge(s["a"], k - 1)
                three_pass(t, bank("U", u, z), (W["uH"][:, n, :], W["uL"][:, n, :]), xs).then_inc(s["U"], 1)

            def weight(g, u, z):
                k, n, zu = g * NU + u, u % NU, (z + u // NU) % 2
                if n == UNITS:
                    return
                if n == 0:
                    t.wait_ge(s["wtc"], g + (1 + u // NU))
                if not isinstance(k, int) or k >= 2:
                    t.wait_ge(s["b"], k - 1)
                t.matmul(bank("WB", u, z), sel[:, n, :], wT[:, zu, :], start=True, stop=True).then_inc(s["WB"], 1)

            def main(g, before, more, z):
                def down(u):
                    k, n, w = g * NU + u, buf(u % NU), u % NU
                    t.wait_ge(s["bl"], k + 1)
                    if u == 0 and before:
                        t.wait_ge(s["yt"], g)
                    last = three_pass(t, Y, (W["dH"][:, w, :], W["dL"][:, w, :]), (bH[:, n, :], bL[:, n, :]),
                                      start=(w == 0), stop=(w == UNITS))
                    last.then_inc(s["dn"], 1)

                for u in range(1, NU + more):
                    if more or u + 1 < NU:
                        products(g, u + 1, z)
                    weight(g, u - 1, z)
                    if more and u == NU:
                        transpose_w(g + 1)
                    if before or u >= LAG:
                        down(u - LAG)
                    if more and u == X_AT:
                        transpose_x(g + 1)
                    if more and u == ROUTE_AT:
                        route(g + 1, 1 - z)
                    if before and u == Y_AT:
                        if more:
                            t.wait_ge(s["lgs"], g + 2)
                        transpose_y(g - 1)
                if not more:
                    for u in range(NU - LAG, NU):
                        down(u)
                    transpose_y(g)

            def transpose_y(g):
                t.wait_ge(s["yt"], g + 1)
                for i in range(GT):
                    last = t.transpose(TPB[:, P * i:P * i + P], yT[:, P * i:P * i + P], ident[:])
                last.then_inc(s["yo"], 1)

            transpose_x(0)
            route(0, 0)
            t.wait_ge(s["iv"], 3)
            transpose_w(0)
            if raw is not None:
                t.wait_ge(s_low, 1)
                t.wait_ge(s_lowp, 1)
            for u in range(2):
                products(0, u, 0)
            if raw is not None:
                t.wait_ge(s_high, 4)
                t.wait_ge(s_lowp, 2)
            run_groups(t, main)


LAG = 4
X_AT, ROUTE_AT, Y_AT = 4, 6, 9
PART_AT = (1, 3, 5, 7, 7, 8, 9, 10, 12, 12, 13, 13, 14, 14, 15)



def recon(nc, A, mk, ticks, x, ident, PS):
    ctx = ExitStack()
    with ctx:
        sb0, sem = mk(ctx)

        def sb(n, shape, d=F32):
            return sb0("r_" + n, shape, d)

        NQ = P // RH
        N4 = NI * P // NQ
        QT = N4 // P
        NGB = NI // GT
        tk, tv, tq, tkT, tvT, tqT, dn, dT = (sb(n, [P, P]) for n in "tk tv tq tkT tvT tqT dn dT".split())
        w1T = sb("w1T", [P, RH])
        w2e = sb("w2e", [P, RH + 1])
        w2r = sb("w2r", [P, NQ, RH])
        w2eT = sb("w2eT", [RH + 1, P])
        w2d = sb("w2d", [P, NQ, P])
        b1 = sb("b1", [P, 1])
        own = sb("own", [P, NQ])
        rep = sb("rep", [P, P])
        ones = sb("ones", [RH + 1, P])
        st, mv = sb("st", [P, NI, 6]), sb("mv", [P, NI, 2])
        half_neg, rstd, var_e = (sb(n, [P, NI]) for n in ("hn", "rstd", "vare"))
        xn = sb("xn", [P, NI, P])
        xT = sb("xT", [P, NI * P])
        par = sb("par", [P, 2 * RH])
        cc = sb("cc", [P, 1])
        hh = sb("hh", [P, NQ, RH])
        qpar = sb("qpar", [P, RH])
        v0, v1, vs, rv, cdf, ex, gp, h, dp, h2 = (sb(n, [P, N4]) for n in "v0 v1 vs rv cdf ex gp h dp h2".split())
        db = sb("db", [P, 1])
        hdt = sb("hdt", [P, NI, 96])
        M, Md = sb("M", [P, RH + 1]), sb("Md", [P, RH])
        gram = sb("gram", [RH + 1, RH + 1])
        warm = sb("warm", [P, 1])
        names = ("w wc stat rstd xn xt xT par parc hh pre v1 vs ge ex dh dp ht hc dt dc m mc md mdc up upc u1 u1c tw "
                 "twc w2d q qc pq h2 o x vc g1").split()
        s = {n: sem("r_" + n) for n in names}
        s.update(ticks)
        TPB, PRE, DH, HDT, MM, SM = (PS[:, n, :] for n in range(6))
        OUT = (PS[:, 6, :], PS[:, 7, :])
        C = 2.0 / (NI * P * P)
        SQ = 0.3989422804014327
        block = ctx.enter_context(nc.Block())

        def batches(eng, step):
            with eng.Fori(0, NB - 1) as b:
                step(b, True)
            step(NB - 1, False)

        @block.sync
        def _(sp):
            for dst, n in ((tk, "tk"), (tv, "tv"), (tq, "tq"), (tkT, "tkT"), (tvT, "tvT"), (tqT, "tqT"), (w1T, "w1T"),
                           (own, "own"), (rep, "rep"), (b1, "b1")):
                sp.dma_start(dst[:], A[n]).then_inc(s["w"], 16)
            sp.dma_start(w2e[:, 0:RH], A["w2"]).then_inc(s["w"], 16)
            sp.dma_start(w2e[:, RH:RH + 1], A["b2"].unsqueeze(1)).then_inc(s["w"], 16)
        NW = 12

        @block.gpsimd
        def _(p):
            def norm(b):
                p.wait_ge(s["stat"], b + 1)
                apart(p, s["tickp"])
                p.tensor_scalar(var_e[:], mv[:, :, 1], LN_EPS, None, ALU.add).then_inc(s["g1"], 1)
                p.wait_ge(s["g1"], b + 3)
                p.tensor_tensor(rstd[:], var_e[:], half_neg[:], ALU.pow).then_inc(s["rstd"], 1)

            p.memset(half_neg[:], -0.5)
            p.memset(ones[:], 1.0)
            p.memset(warm[:], 1.0)
            p.memset(hdt[:], 0.0).then_inc(s["g1"], 1)
            p.wait_ge(s["g1"], 1)
            p.memset(hdt[:, :, RH:RH + 1], 1.0).then_inc(s["g1"], 1)
            norm(0)
            with p.Fori(1, NB) as b:
                norm(b)

        @block.scalar
        def _(a):
            def copy_x(b):
                for k in range(NGB):
                    a.wait_ge(s["xt"], b * NGB + (k + 1))
                    a.activation(xT[:, GN * k:GN * k + GN], TPB, ACT.Copy).then_inc(s["xT"], 1)

            def copy_w2():
                a.activation(w2eT[:], TPB[0:RH + 1, 0:P], ACT.Copy).then_inc(s["twc"], 1)

            def tiles(columns, bank):
                return (hdt[:].rearrange("p (j q) c -> p q j c", q=QT)[:, :, :, columns],
                        bank.rearrange("p (q j r) -> p q j r", q=QT, r=RH))

            def step(b, more):
                a.wait_ge(s["par"], b + 1)
                a.activation(par[:], SM[:, 0:2 * RH], ACT.Copy)
                a.activation(cc[:], SM[:, 192:193], ACT.Copy).then_inc(s["parc"], 1)
                a.wait_ge(s["vs"], b + 1)
                a.activation(h[:], vs[:], ACT.Gelu).then_inc(s["ge"], 1)
                a.activation(ex[:], v1[:], ACT.Exp, scale=-0.5).then_inc(s["ex"], 1)
                a.activation(warm[:], warm[:], ACT.Gelu)
                a.wait_ge(s["ht"], b + 1)
                a.activation(*tiles(slice(0, RH), HDT[:, 0:QT * P]), ACT.Copy).then_inc(s["hc"], 1)
                a.wait_ge(s["m"], b + 1)
                a.activation(M[:], MM[:, 0:RH + 1], ACT.Copy)
                a.activation(gram[:], SM[0:RH + 1, 200:200 + RH + 1], ACT.Copy).then_inc(s["mc"], 1)
                a.wait_ge(s["dt"], b + 1)
                a.activation(*tiles(slice(64, 64 + RH), HDT[:, QT * P:2 * QT * P]), ACT.Copy).then_inc(s["dc"], 1)
                a.wait_ge(s["md"], b + 1)
                a.activation(Md[:], MM[:, 64:64 + RH], ACT.Copy).then_inc(s["mdc"], 1)
                a.wait_ge(s["tw"], b + 2)
                copy_w2()
                a.wait_ge(s["q"], b + 1)
                a.activation(qpar[:], SM[:, 240:240 + RH], ACT.Copy).then_inc(s["qc"], 1)
                a.wait_ge(s["pq"], b + 1)
                a.wait_ge(s["u1c"], b + 1)
                a.activation(h2[:], PRE[:, 0:N4], ACT.Gelu, bias=b1[:, 0:1]).then_inc(s["h2"], 1)
                if more:
                    copy_x(b + 1)

            copy_x(0)
            a.wait_ge(s["tw"], 1)
            copy_w2()
            batches(a, step)

        @block.vector
        def _(v):
            PER = 6

            def stats(b):
                for i in range(NI):
                    last = v.bn_stats(st[:, i, :], x[:, ds(b * NI + i, 1), :].rearrange("p o f -> p (o f)"))
                last.then_inc(s["wc"], 1)
                v.wait_ge(s["wc"], b + 2)
                apart(v, s["tick"])
                for i in range(NI):
                    last = v.bn_aggr(mv[:, i, :], st[:, i, :])
                last.then_inc(s["stat"], 1)

            def norm(b):
                v.wait_ge(s["rstd"], b + 1)
                for i in range(NI):
                    last = v.tensor_scalar(xn[:, i, :], x[:, ds(b * NI + i, 1), :].rearrange("p o f -> p (o f)"),
                                           mv[:, i, 0:1], rstd[:, i:i + 1], ALU.subtract, ALU.mult)
                last.then_inc(s["xn"], 1)

            def own_w2():
                v.tensor_tensor(w2d[:], TPB[:, P:2 * P].unsqueeze(1).to_broadcast([P, NQ, P]),
                                own[:].unsqueeze(2).to_broadcast([P, NQ, P]), ALU.mult).then_inc(s["w2d"], 1)

            def step(b, more):
                c = Chain(v, s["vc"], PER, b)
                v.wait_ge(s["parc"], b + 1)
                v.tensor_tensor(hh[:], SM[:, 2 * RH:2 * RH + P].rearrange("p (j r) -> p j r", r=RH),
                                own[:].unsqueeze(2).to_broadcast([P, NQ, RH]), ALU.mult).then_inc(s["hh"], 1)
                v.wait_ge(s["pre"], b + 1)
                c.step(v.tensor_scalar(v0[:], PRE[:, 0:N4], b1[:, 0:1], None, ALU.add))
                v.tensor_tensor(v1[:], v0[:], v0[:], ALU.mult).then_inc(s["v1"], 1)
                v.wait_ge(s["v1"], b + 1)
                c.step(v.tensor_scalar(rv[:], v1[:], 1e-24, 4e-12, ALU.is_lt, ALU.mult))
                v.tensor_tensor(vs[:], v0[:], rv[:], ALU.add).then_inc(s["vs"], 1)
                v.wait_ge(s["vs"], b + 1)
                c.step(v.reciprocal(rv[:], vs[:]))
                v.wait_ge(s["ge"], b + 1)
                c.step(v.tensor_tensor(cdf[:], h[:], rv[:], ALU.mult))
                v.wait_ge(s["ex"], b + 1)
                c.step(v.scalar_tensor_tensor(gp[:], v0[:], SQ, ex[:], ALU.mult, ALU.mult))
                c.step(v.tensor_tensor(gp[:], gp[:], cdf[:], ALU.add))
                v.wait_ge(s["dh"], b + 1)
                v.scalar_tensor_tensor(dp[:], DH[:, 0:N4], cc[:, 0:1], gp[:], ALU.add, ALU.mult).then_inc(s["dp"], 1)
                v.wait_ge(s["dp"], 2 * b + 1)
                v.tensor_reduce(db[:], dp[:], AX.X, ALU.add).then_inc(s["dp"], 1)
                v.wait_ge(s["up"], b + 1)
                v.scalar_tensor_tensor(w2e[:], MM[:, 128:128 + RH + 1], -LR * C, w2e[:], ALU.mult,
                                       ALU.add).then_inc(s["upc"], 1)
                v.wait_ge(s["upc"], 2 * b + 2)
                v.tensor_copy(w2r[:], w2e[:, 0:RH].unsqueeze(1).to_broadcast([P, NQ, RH])).then_inc(s["upc"], 1)
                if more:
                    stats(b + 1)
                v.wait_ge(s["u1"], b + 1)
                v.scalar_tensor_tensor(w1T[:], MM[:, 192:192 + RH], -LR * C, w1T[:], ALU.mult, ALU.add)
                v.scalar_tensor_tensor(b1[:], MM[:, 240:241], -LR * C, b1[:], ALU.mult, ALU.add).then_inc(s["u1c"], 1)
                v.wait_ge(s["twc"], b + 2)
                own_w2()
                if more:
                    norm(b + 1)
                for q in range(QT):
                    v.wait_ge(s["o"], b * QT + (q + 1))
                    xq = x[:, ds(b * NI, NI), :].rearrange("p (j q) f -> p q j f", q=QT)[:, q]
                    v.tensor_tensor(xq, OUT[q].rearrange("p (j f) -> p j f", f=P), xq, ALU.add).then_inc(s["x"], 1)
                c.close()

            v.wait_ge(s["w"], 16 * NW)
            v.tensor_tensor(dn[:], tk[:], tv[:], ALU.subtract)
            v.tensor_copy(w2r[:], w2e[:, 0:RH].unsqueeze(1).to_broadcast([P, NQ, RH])).then_inc(s["upc"], 1)
            v.tensor_tensor(dT[:], tkT[:], tvT[:], ALU.subtract).then_inc(s["wc"], 1)
            stats(0)
            norm(0)
            batches(v, step)

        @block.tensor
        def _(t):
            def transpose_x(b):
                t.wait_ge(s["xn"], b + 1)
                for k in range(NGB):
                    if k:
                        t.wait_ge(s["xT"], b * NGB + k)
                    apart(t, s["tickt"])
                    for i in range(GT):
                        last = t.transpose(TPB[:, P * i:P * i + P], xn[:, GT * k + i, :], ident[:])
                    last.then_inc(s["xt"], 1)

            def turn_w2():
                t.transpose(TPB[0:RH + 1, 0:P], w2e[:], ident[:])
                t.transpose(TPB[:, P:2 * P], w2r[:].rearrange("p j r -> p (j r)"), ident[:]).then_inc(s["tw"], 1)

            def blocks(bank, weights, stop=True):
                for j in range(NQ):
                    last = t.matmul(bank[RH * j:RH * j + RH, 0:N4], weights, xT[:, N4 * j:N4 * j + N4],
                                    start=True, stop=stop, skip_group_check=True)
                return last

            def step(b, more):
                w2 = w2r[:].rearrange("p j r -> p (j r)")
                t.matmul(SM[:, 0:RH], tk[:], w1T[:], start=True, stop=True)
                t.matmul(SM[:, RH:2 * RH], dn[:], w2e[:, 0:RH], start=True, stop=True)
                t.matmul(SM[:, 2 * RH:2 * RH + P], w2, w2, start=True, stop=True)
                t.matmul(SM[:, 192:193], w2, w2e[:, RH:RH + 1], start=True, stop=True).then_inc(s["par"], 1)
                t.wait_ge(s["parc"], b + 1)
                t.wait_ge(s["xT"], b * NGB + NGB)
                blocks(PRE, par[:, 0:RH]).then_inc(s["pre"], 1)
                blocks(DH, par[:, RH:2 * RH], stop=False)
                for q in range(QT):
                    for j in range(NQ):
                        i = QT * j + q
                        t.matmul(OUT[q][:, P * j:P * j + P], xT[:, P * i:P * i + P], tqT[:], start=(j == 0), stop=False,
                                 skip_group_check=True)
                t.wait_ge(s["hh"], b + 1)
                t.wait_ge(s["ge"], b + 1)
                t.matmul(DH[:, 0:N4], hh[:].rearrange("p j r -> p (j r)"), h[:], start=False, stop=True,
                         skip_group_check=True).then_inc(s["dh"], 1)
                for q in range(QT):
                    last = t.transpose(HDT[:, P * q:P * q + P], h[:, P * q:P * q + P], ident[:])
                last.then_inc(s["ht"], 1)
                t.wait_ge(s["hc"], b + 1)
                for i in range(NI):
                    t.matmul(MM[:, 0:RH + 1], xn[:, i, :], hdt[:, i, 0:RH + 1], start=(i == 0), stop=(i == NI - 1))
                for i in range(NI):
                    last = t.matmul(SM[0:RH + 1, 200:200 + RH + 1], hdt[:, i, 0:RH + 1], hdt[:, i, 0:RH + 1],
                                    start=(i == 0), stop=(i == NI - 1))
                last.then_inc(s["m"], 1)
                t.wait_ge(s["mc"], b + 1)
                t.wait_ge(s["twc"], b + 1)
                t.matmul(MM[:, 128:128 + RH + 1], dT[:], M[:], start=True, stop=False)
                t.matmul(MM[:, 128:128 + RH + 1], w2eT[:], gram[:], start=False, stop=True).then_inc(s["up"], 1)
                t.wait_ge(s["dp"], 2 * b + 1)
                apart(t, s["tickt"])
                for q in range(QT):
                    last = t.transpose(HDT[:, P * (QT + q):P * (QT + q) + P], dp[:, P * q:P * q + P], ident[:])
                last.then_inc(s["dt"], 1)
                t.wait_ge(s["upc"], 2 * b + 3)
                t.wait_ge(s["dc"], b + 1)
                for i in range(NI):
                    last = t.matmul(MM[:, 64:64 + RH], xn[:, i, :], hdt[:, i, 64:64 + RH], start=(i == 0),
                                    stop=(i == NI - 1))
                last.then_inc(s["md"], 1)
                t.wait_ge(s["mdc"], b + 1)
                t.wait_ge(s["dp"], 2 * b + 2)
                t.matmul(MM[:, 192:192 + RH], tkT[:], Md[:], start=True, stop=True)
                t.matmul(MM[:, 240:241], rep[:], db[:], start=True, stop=True).then_inc(s["u1"], 1)
                t.wait_ge(s["upc"], 2 * b + 3)
                apart(t, s["tickt"])
                turn_w2()
                t.wait_ge(s["u1c"], b + 1)
                t.matmul(SM[:, 240:240 + RH], tq[:], w1T[:], start=True, stop=True).then_inc(s["q"], 1)
                t.wait_ge(s["twc"], b + 2)
                for q in range(QT):
                    t.matmul(OUT[q], ones[RH:RH + 1, :], w2eT[RH:RH + 1, :].unsqueeze(1).to_broadcast([1, NQ, P]),
                             start=False, stop=False, skip_group_check=True)
                t.wait_ge(s["qc"], b + 1)
                blocks(PRE, qpar[:]).then_inc(s["pq"], 1)
                t.wait_ge(s["w2d"], b + 1)
                t.wait_ge(s["h2"], b + 1)
                for q in range(QT):
                    t.matmul(OUT[q], h2[:, P * q:P * q + P], w2d[:].rearrange("p j f -> p (j f)"), start=False,
                             stop=True, skip_group_check=True).then_inc(s["o"], 1)
                if more:
                    transpose_x(b + 1)
                t.wait_ge(s["x"], b * QT + QT)

            transpose_x(0)
            t.wait_ge(s["xT"], NGB)
            t.wait_ge(s["upc"], 1)
            t.wait_ge(s["g1"], 2)
            turn_w2()
            t.wait_ge(s["twc"], 1)
            batches(t, step)



def kernel(**inputs):
    import numpy as _np
    import concourse.bacc as _bacc
    from concourse import mybir as _mybir
    from concourse.bass_utils import run_bass_kernel_spmd as _run

    nc = _bacc.Bacc("TRN2", target_bir_lowering=False, num_devices=1)
    arrays = lay_out(inputs)
    args = {n: nc.dram_tensor("in_" + n, a.shape, _mybir.dt.from_np(a.dtype), kind="ExternalInput").ap()
            for n, a in arrays.items()}
    out = nc.dram_tensor("out_0", (NB, NI * P, P), _mybir.dt.float32, kind="ExternalOutput").ap()
    build(nc, args, out)
    r = _run(nc, [{"in_" + n: a for n, a in arrays.items()}], core_ids=[0])
    return r.results[0]["out_0"]


def lay_out(inputs):
    a, r, f = "L0_attn_a_", "L0_attn_b_", "L0_ffn_"
    c = np.ascontiguousarray

    def units(w, shared):
        return c(np.concatenate([w.reshape(UNITS, P, P), shared[None]]).transpose(2, 0, 1))

    I = {n: np.asarray(v) for n, v in inputs.items()}
    down = I[f + "down_w"].reshape(UNITS, 2, P, INNER).transpose(1, 3, 0, 2).reshape(P, UNITS, P)
    lo_q, lo_k = np.zeros((2, P), np.float32)
    for j in range(HC):
        lo_q[32 * j + 8:32 * j + 16] = -1
        lo_k[32 * j + 16:32 * j + 24] = -1
    sel = np.zeros((3, EXPERTS, UNITS, 2, INNER), np.float32)
    for e in range(EXPERTS):
        sel[:, e, e // 2, e % 2] = 1
    q, kk, v = (I[a + n].T.reshape(P, HEADS, HD) for n in ("Wq", "Wk", "Wv"))
    planes, protos = np.zeros((HEADS, HD, HEADS, NP), np.float32), np.zeros((HC * TABLES, BITS, HC * TABLES, CORNERS), np.float32)
    for h in range(HEADS):
        planes[h, :, h] = I[a + "planes_T"]
    for n in range(HC * TABLES):
        protos[n, :, n] = I[a + "protos_T"]
    w_a = np.concatenate([np.concatenate([q, q, q, np.zeros_like(q)], 2).reshape(P, 512),
                          np.concatenate([kk, kk, kk, v], 2).reshape(P, 512),
                          planes.reshape(P, 512), protos.reshape(P, 512), I[a + "Wk"]], 1)
    return {
        "x": c(I[a + "x"]),
        "w_a": w_a,
        "woT": c(I[a + "Wo"].T), "bo": c(I[a + "bo"]),
        "protos": c(I[a + "protos_T"]), "temp": c(I[a + "logit_temp"].reshape(1)),
        "rwT": c(I[f + "router_weight"].T), "rbias": c(I[f + "router_bias"]),
        "w_g": units(I[f + "gate_w"], I[f + "shared_gate_w"]),
        "w_u": units(I[f + "up_w"], I[f + "shared_up_w"]),
        "w_d": c(np.concatenate([down, I[f + "shared_down_w"].T[:, None]], axis=1)),
        "tk": c(I[r + "t_k"]), "tv": c(I[r + "t_v"]), "tq": c(I[r + "t_q"]), "tkT": c(I[r + "t_k"].T),
        "tvT": c(I[r + "t_v"].T), "tqT": c(I[r + "t_q"].T), "w1T": c(I[r + "W1"].T), "w2": c(I[r + "W2"]),
        "b1": c(np.tile(I[r + "b1"], P // RH)[:, None]), "b2": c(I[r + "b2"]),
        "ident": np.eye(P, dtype=np.float32), "msk": c(np.stack([lo_q, lo_k], axis=1)),
        "sel": sel.reshape(96, UNITS, P),
        "own": np.repeat(np.eye(P // RH, dtype=np.float32), RH, 0), "rep": np.tile(np.eye(RH, dtype=np.float32), (P // RH, P // RH)),
    }
```
